# Optimizing a Trainium2 kernel written in Bass

```python
import numpy as np
import jax
import jax.numpy as jnp

def _softmax(x, axis=-1):
    return jax.nn.softmax(x, axis=axis)

def _gelu(x):
    return jax.nn.gelu(x, approximate=True)

def _silu(x):
    return jax.nn.silu(x)

def _sigmoid(x):
    return jax.nn.sigmoid(x)

def _layernorm(x, axis=-1, eps=1e-05):
    m = jnp.mean(x, axis=axis, keepdims=True)
    v = jnp.var(x, axis=axis, keepdims=True)
    return (x - m) / jnp.sqrt(v + eps)

def _scatter_add(tgt, idx, src, axis=0):
    return tgt.at[idx].add(src)

def _segment_sum(src, seg, n):
    return jax.ops.segment_sum(src, seg, n)
kernel_name = 'mk_vit_tower_cls_d2_tok_img768_r4_384d76'

def setup_inputs(seed: int=0):
    np.random.seed(seed)
    _w = jnp.asarray

    def _rec_inputs():
        import jax
        import jax.numpy as jnp
        _rk = jax.random.key(seed)
        x = 1.64766e-05 + 1.00005 * jax.random.normal(jax.random.fold_in(_rk, 1), (4, 3, 512, 192), jnp.float32)
        cls_tok = 0.02 * jax.random.normal(jax.random.fold_in(_rk, 5), (1, 1, 192), jnp.float32)
        return (x, cls_tok)
    x, cls_tok = _rec_inputs()

    def _L0_tok_setup():
        import jax, jax.numpy as jnp
        import numpy as np
        NUM_BANDS = 6
        D_MODEL = 192
        B, N = (2, 512)
        IN_FEATURES = 3 * NUM_BANDS * 2 * D_MODEL
        key = jax.random.key(seed)
        k_xyz, k_w = jax.random.split(key)
        xyz = jax.random.normal(k_xyz, (B, 3, N, D_MODEL), dtype=jnp.float32)
        freq_bands = 2.0 ** jnp.linspace(0.0, NUM_BANDS - 1, NUM_BANDS).astype(jnp.float32)
        bound = 1.0 / np.sqrt(IN_FEATURES)
        W = jax.random.uniform(k_w, (D_MODEL, IN_FEATURES), dtype=jnp.float32, minval=-bound, maxval=bound)
        return {'xyz': xyz, 'freq_bands': freq_bands, 'W': W}
    _L0_tok_all = _L0_tok_setup()
    _L0_tok_in = {k: v for k, v in _L0_tok_all.items() if k in ('freq_bands', 'W')}
    del _L0_tok_all

    def _L0_attn_setup():
        import jax, jax.numpy as jnp
        import numpy as np
        D_MODEL = 192
        D_STATE = 8
        EXPAND = 2
        D_HEAD = 64
        D_CONV = 4
        D_INNER = EXPAND * D_MODEL
        N_HEADS = D_INNER // D_HEAD
        PARAM_DIM = 2
        D_PROJ = 2 * D_INNER + N_HEADS * PARAM_DIM
        D_FF = 4 * D_MODEL
        BATCH, SEQ = (2, 512)

        def _rmsnorm(x, w, eps=1e-06):
            return x * jax.lax.rsqrt(jnp.mean(x * x, axis=-1, keepdims=True) + eps) * w

        def _l2norm(x, eps=1e-12):
            return x * jax.lax.rsqrt(jnp.sum(x * x, axis=-1, keepdims=True) + eps)

        def _mixer(x, w_in, conv_w, w_bc, D_skip, w_out):
            Bsz, T, _ = x.shape
            proj = x @ w_in
            gate, vraw, params = jnp.split(proj, [D_INNER, 2 * D_INNER], axis=-1)
            vpad = jnp.pad(vraw, ((0, 0), (D_CONV - 1, 0), (0, 0)))
            kernel = conv_w.T[:, None, :]
            conv = jax.lax.conv_general_dilated(vpad, kernel, window_strides=(1,), padding='VALID', dimension_numbers=('NWC', 'WIO', 'NWC'), feature_group_count=D_INNER)
            v = jax.nn.silu(conv)
            bc = (v @ w_bc).reshape(Bsz, T, N_HEADS, 2, D_STATE)
            Bm = _l2norm(bc[..., 0, :])
            Cm = _l2norm(bc[..., 1, :])
            p = params.reshape(Bsz, T, N_HEADS, PARAM_DIM)
            A = jax.nn.softplus(p[..., 0])
            dt = jax.nn.sigmoid(p[..., 1])
            S = 1.0 / (1.0 + dt * dt * A)
            u = v.reshape(Bsz, T, N_HEADS, D_HEAD)
            tfirst = lambda a: jnp.moveaxis(a, 1, 0)

            def step(carry, inp):
                z, xs = carry
                Bt, Ct, At, dtt, St, ut = inp
                d = dtt[..., None, None]
                a = At[..., None, None]
                s = St[..., None, None]
                bu = Bt[..., :, None] * ut[..., None, :]
                z = s * (z - d * a * xs + d * bu)
                xs = xs + d * z
                y = jnp.einsum('bhn,bhnp->bhp', Ct, xs)
                return ((z, xs), y)
            z0 = jnp.zeros((Bsz, N_HEADS, D_STATE, D_HEAD), x.dtype)
            _, ys = jax.lax.scan(step, (z0, z0), (tfirst(Bm), tfirst(Cm), tfirst(A), tfirst(dt), tfirst(S), tfirst(u)))
            y = jnp.moveaxis(ys, 0, 1)
            gated = (y + D_skip[None, None, :, None] * u) * jax.nn.silu(gate).reshape(Bsz, T, N_HEADS, D_HEAD)
            return gated.reshape(Bsz, T, D_INNER) @ w_out
        key = jax.random.key(seed)
        ks = jax.random.split(key, 8)

        def s(k, shape, scale):
            return jax.random.normal(k, shape, dtype=jnp.float32) * scale
        return {'x': s(ks[0], (BATCH, SEQ, D_MODEL), 1.0), 'norm1_w': jnp.ones((D_MODEL,), jnp.float32), 'w_in': s(ks[1], (D_MODEL, D_PROJ), D_MODEL ** (-0.5)), 'conv_w': s(ks[2], (D_INNER, D_CONV), D_CONV ** (-0.5)), 'w_bc': s(ks[3], (D_INNER, 2 * N_HEADS * D_STATE), D_INNER ** (-0.5)), 'D_skip': s(ks[4], (N_HEADS,), 1.0), 'w_out': s(ks[5], (D_INNER, D_MODEL), D_INNER ** (-0.5)), 'norm2_w': jnp.ones((D_MODEL,), jnp.float32), 'ff_w1': s(ks[6], (D_MODEL, D_FF), D_MODEL ** (-0.5)), 'ff_b1': jnp.zeros((D_FF,), jnp.float32), 'ff_w2': s(ks[7], (D_FF, D_MODEL), D_FF ** (-0.5)), 'ff_b2': jnp.zeros((D_MODEL,), jnp.float32)}
    _L0_attn_all = _L0_attn_setup()
    _L0_attn_in = {k: v for k, v in _L0_attn_all.items() if k in ('norm1_w', 'w_in', 'conv_w', 'w_bc', 'D_skip', 'w_out', 'norm2_w', 'ff_w1', 'ff_b1', 'ff_w2', 'ff_b2')}
    del _L0_attn_all

    def _L0_ffn_setup():
        import jax, jax.numpy as jnp
        import numpy as np
        EPS = 1e-05

        def _ln(x, g, b):
            m = jnp.mean(x, axis=-1, keepdims=True)
            v = jnp.mean((x - m) ** 2, axis=-1, keepdims=True)
            return (x - m) / jnp.sqrt(v + EPS) * g + b
        key = jax.random.key(seed)
        ks = jax.random.split(key, 16)
        B, S, D, H, E, K = (32, 128, 192, 12, 8, 2)
        Dff = 4 * D
        s = 0.02
        return {'x': jax.random.normal(ks[0], (B, S, D), dtype=jnp.float32), 'ln1_g': jnp.ones((D,), jnp.float32), 'ln1_b': jnp.zeros((D,), jnp.float32), 'in_proj_w': jax.random.normal(ks[1], (3 * D, D), jnp.float32) * s, 'in_proj_b': jnp.zeros((3 * D,), jnp.float32), 'out_proj_w': jax.random.normal(ks[2], (D, D), jnp.float32) * s, 'out_proj_b': jnp.zeros((D,), jnp.float32), 'ln2_g': jnp.ones((D,), jnp.float32), 'ln2_b': jnp.zeros((D,), jnp.float32), 'router_w': jax.random.normal(ks[3], (E, D), jnp.float32) * s, 'router_b': jnp.zeros((E,), jnp.float32), 'w1': jax.random.normal(ks[4], (E, D, Dff), jnp.float32) * s, 'b1': jnp.zeros((E, Dff), jnp.float32), 'w2': jax.random.normal(ks[5], (E, Dff, D), jnp.float32) * s, 'b2': jnp.zeros((E, D), jnp.float32)}
    _L0_ffn_all = _L0_ffn_setup()
    _L0_ffn_in = {k: v for k, v in _L0_ffn_all.items() if k in ('ln1_g', 'ln1_b', 'in_proj_w', 'in_proj_b', 'out_proj_w', 'out_proj_b', 'ln2_g', 'ln2_b', 'router_w', 'router_b', 'w1', 'b1', 'w2', 'b2')}
    del _L0_ffn_all

    def _L1_attn_setup():
        import jax, jax.numpy as jnp
        import numpy as np
        TAU = 2.0
        BN_EPS = 1e-05
        SG_ALPHA = 2.0

        @jax.custom_vjp
        def spike(u):
            return (u >= 0).astype(u.dtype)

        def _spike_fwd(u):
            return (spike(u), u)

        def _spike_bwd(u, g):
            sg = SG_ALPHA / 2.0 / (1.0 + (jnp.pi / 2.0 * SG_ALPHA * u) ** 2)
            return (g * sg,)
        spike.defvjp(_spike_fwd, _spike_bwd)

        def lif(x, v_th):
            return spike(x / TAU - v_th)

        def bn_eval(x, gamma, beta, mean, var):
            inv = gamma / jnp.sqrt(var + BN_EPS)
            return x * inv + (beta - mean * inv)
        key = jax.random.key(seed)
        ks = jax.random.split(key, 7)
        B, N, D = (2, 512, 192)
        x = jax.random.normal(ks[0], (B, N, D), dtype=jnp.float32)
        W = jax.random.normal(ks[1], (4, D, D), dtype=jnp.float32) * 0.02
        b = jnp.zeros((4, D), dtype=jnp.float32)
        bn_gamma = jax.random.uniform(ks[2], (4, D), dtype=jnp.float32, minval=0.5, maxval=1.5)
        bn_beta = jax.random.normal(ks[3], (4, D), dtype=jnp.float32) * 0.1
        bn_mean = jax.random.normal(ks[4], (4, D), dtype=jnp.float32) * 0.1
        bn_var = jax.random.uniform(ks[5], (4, D), dtype=jnp.float32, minval=0.5, maxval=1.5)
        return {'x': x, 'W': W, 'b': b, 'bn_gamma': bn_gamma, 'bn_beta': bn_beta, 'bn_mean': bn_mean, 'bn_var': bn_var}
    _L1_attn_all = _L1_attn_setup()
    _L1_attn_in = {k: v for k, v in _L1_attn_all.items() if k in ('W', 'b', 'bn_gamma', 'bn_beta', 'bn_mean', 'bn_var')}
    del _L1_attn_all

    def _L1_ffn_setup():
        import jax, jax.numpy as jnp
        import numpy as np
        H = 12
        ALPHA = (1, 2, 3)
        DEPTH = 5
        BLOCK_DEPTH = 3
        TOTAL_DEPTH_M1 = 14 - 1
        SMALL_ACTIVE = BLOCK_DEPTH <= DEPTH <= TOTAL_DEPTH_M1 - BLOCK_DEPTH

        def _ln(x, g, b, eps=1e-05):
            m = jnp.mean(x, axis=-1, keepdims=True)
            v = jnp.mean((x - m) ** 2, axis=-1, keepdims=True)
            return (x - m) * jax.lax.rsqrt(v + eps) * g + b

        def _attn_branch(xp, w_qkv, w_proj, b_proj, keep_heads, keep_ch):
            B2, N, C = xp.shape
            hd = C // H
            scale = hd ** (-0.5)
            qkv = (xp @ w_qkv).reshape(B2, N, 3, H, hd).transpose(2, 0, 3, 1, 4)
            hmask = (jnp.arange(H) < keep_heads).astype(xp.dtype)[None, :, None, None]
            q, k, v = (qkv[0] * hmask, qkv[1] * hmask, qkv[2] * hmask)
            a = jax.nn.softmax(jnp.einsum('bhnd,bhmd->bhnm', q, k) * scale, axis=-1)
            o = jnp.einsum('bhnm,bhmd->bhnd', a, v).transpose(0, 2, 1, 3).reshape(B2, N, C)
            o = o @ w_proj + b_proj
            cmask = (jnp.arange(C) < keep_ch).astype(xp.dtype)
            return o * cmask

        def _mlp_branch(xp, w1, b1, w2, b2, keep_ch):
            C = xp.shape[-1]
            cmask = (jnp.arange(C) < keep_ch).astype(xp.dtype)
            h = jax.nn.gelu(xp * cmask @ w1 + b1, approximate=False)
            return (h @ w2 + b2) * cmask
        key = jax.random.key(seed)
        ks = jax.random.split(key, 8)
        B, N, C = (64, 257, 192)
        HID = 4 * C

        def w(k, shape):
            return jax.random.normal(k, shape, jnp.float32) * 0.02
        return {'x': jax.random.normal(ks[0], (B, N, C), jnp.float32), 'gumbel_weights': jax.random.uniform(ks[1], (3,), jnp.float32), 'n1l_g': jnp.ones((C,), jnp.float32), 'n1l_b': jnp.zeros((C,), jnp.float32), 'n1s_g': jnp.ones((C,), jnp.float32), 'n1s_b': jnp.zeros((C,), jnp.float32), 'w_qkv': w(ks[2], (C, 3 * C)), 'w_proj': w(ks[3], (C, C)), 'b_proj': jnp.zeros((C,), jnp.float32), 'n2l_g': jnp.ones((C,), jnp.float32), 'n2l_b': jnp.zeros((C,), jnp.float32), 'n2s_g': jnp.ones((C,), jnp.float32), 'n2s_b': jnp.zeros((C,), jnp.float32), 'w_fc1': w(ks[4], (C, HID)), 'b_fc1': jnp.zeros((HID,), jnp.float32), 'w_fc2': w(ks[5], (HID, C)), 'b_fc2': jnp.zeros((C,), jnp.float32)}
    _L1_ffn_all = _L1_ffn_setup()
    _L1_ffn_in = {k: v for k, v in _L1_ffn_all.items() if k in ('gumbel_weights', 'n1l_g', 'n1l_b', 'n1s_g', 'n1s_b', 'w_qkv', 'w_proj', 'b_proj', 'n2l_g', 'n2l_b', 'n2s_g', 'n2s_b', 'w_fc1', 'b_fc1', 'w_fc2', 'b_fc2')}
    del _L1_ffn_all
    return {'x': x, 'cls_tok': cls_tok, 'L0_tok_freq_bands': _L0_tok_in['freq_bands'], 'L0_tok_W': _L0_tok_in['W'], 'L0_attn_norm1_w': _L0_attn_in['norm1_w'], 'L0_attn_w_in': _L0_attn_in['w_in'], 'L0_attn_conv_w': _L0_attn_in['conv_w'], 'L0_attn_w_bc': _L0_attn_in['w_bc'], 'L0_attn_D_skip': _L0_attn_in['D_skip'], 'L0_attn_w_out': _L0_attn_in['w_out'], 'L0_attn_norm2_w': _L0_attn_in['norm2_w'], 'L0_attn_ff_w1': _L0_attn_in['ff_w1'], 'L0_attn_ff_b1': _L0_attn_in['ff_b1'], 'L0_attn_ff_w2': _L0_attn_in['ff_w2'], 'L0_attn_ff_b2': _L0_attn_in['ff_b2'], 'L0_ffn_ln1_g': _L0_ffn_in['ln1_g'], 'L0_ffn_ln1_b': _L0_ffn_in['ln1_b'], 'L0_ffn_in_proj_w': _L0_ffn_in['in_proj_w'], 'L0_ffn_in_proj_b': _L0_ffn_in['in_proj_b'], 'L0_ffn_out_proj_w': _L0_ffn_in['out_proj_w'], 'L0_ffn_out_proj_b': _L0_ffn_in['out_proj_b'], 'L0_ffn_ln2_g': _L0_ffn_in['ln2_g'], 'L0_ffn_ln2_b': _L0_ffn_in['ln2_b'], 'L0_ffn_router_w': _L0_ffn_in['router_w'], 'L0_ffn_router_b': _L0_ffn_in['router_b'], 'L0_ffn_w1': _L0_ffn_in['w1'], 'L0_ffn_b1': _L0_ffn_in['b1'], 'L0_ffn_w2': _L0_ffn_in['w2'], 'L0_ffn_b2': _L0_ffn_in['b2'], 'L1_attn_W': _L1_attn_in['W'], 'L1_attn_b': _L1_attn_in['b'], 'L1_attn_bn_gamma': _L1_attn_in['bn_gamma'], 'L1_attn_bn_beta': _L1_attn_in['bn_beta'], 'L1_attn_bn_mean': _L1_attn_in['bn_mean'], 'L1_attn_bn_var': _L1_attn_in['bn_var'], 'L1_ffn_gumbel_weights': _L1_ffn_in['gumbel_weights'], 'L1_ffn_n1l_g': _L1_ffn_in['n1l_g'], 'L1_ffn_n1l_b': _L1_ffn_in['n1l_b'], 'L1_ffn_n1s_g': _L1_ffn_in['n1s_g'], 'L1_ffn_n1s_b': _L1_ffn_in['n1s_b'], 'L1_ffn_w_qkv': _L1_ffn_in['w_qkv'], 'L1_ffn_w_proj': _L1_ffn_in['w_proj'], 'L1_ffn_b_proj': _L1_ffn_in['b_proj'], 'L1_ffn_n2l_g': _L1_ffn_in['n2l_g'], 'L1_ffn_n2l_b': _L1_ffn_in['n2l_b'], 'L1_ffn_n2s_g': _L1_ffn_in['n2s_g'], 'L1_ffn_n2s_b': _L1_ffn_in['n2s_b'], 'L1_ffn_w_fc1': _L1_ffn_in['w_fc1'], 'L1_ffn_b_fc1': _L1_ffn_in['b_fc1'], 'L1_ffn_w_fc2': _L1_ffn_in['w_fc2'], 'L1_ffn_b_fc2': _L1_ffn_in['b_fc2']}

def reference(x, cls_tok, L0_tok_freq_bands, L0_tok_W, L0_attn_norm1_w, L0_attn_w_in, L0_attn_conv_w, L0_attn_w_bc, L0_attn_D_skip, L0_attn_w_out, L0_attn_norm2_w, L0_attn_ff_w1, L0_attn_ff_b1, L0_attn_ff_w2, L0_attn_ff_b2, L0_ffn_ln1_g, L0_ffn_ln1_b, L0_ffn_in_proj_w, L0_ffn_in_proj_b, L0_ffn_out_proj_w, L0_ffn_out_proj_b, L0_ffn_ln2_g, L0_ffn_ln2_b, L0_ffn_router_w, L0_ffn_router_b, L0_ffn_w1, L0_ffn_b1, L0_ffn_w2, L0_ffn_b2, L1_attn_W, L1_attn_b, L1_attn_bn_gamma, L1_attn_bn_beta, L1_attn_bn_mean, L1_attn_bn_var, L1_ffn_gumbel_weights, L1_ffn_n1l_g, L1_ffn_n1l_b, L1_ffn_n1s_g, L1_ffn_n1s_b, L1_ffn_w_qkv, L1_ffn_w_proj, L1_ffn_b_proj, L1_ffn_n2l_g, L1_ffn_n2l_b, L1_ffn_n2s_g, L1_ffn_n2s_b, L1_ffn_w_fc1, L1_ffn_b_fc1, L1_ffn_w_fc2, L1_ffn_b_fc2):
    import jax
    import jax.numpy as jnp

    def _L0_tok_ref(xyz, freq_bands, W):
        import jax, jax.numpy as jnp
        import numpy as np
        NUM_BANDS = 6
        D_MODEL = 192
        B, N = (2, 512)
        IN_FEATURES = 3 * NUM_BANDS * 2 * D_MODEL
        b, c, n, d = xyz.shape
        xb = 2.0 * jnp.pi * xyz[..., None] * freq_bands
        feat = jnp.concatenate([jnp.sin(xb), jnp.cos(xb)], axis=-1)
        feat = feat.reshape(b, n, -1)
        return jnp.einsum('bnf,of->bno', feat, W)

    def _L0_attn_ref(x, norm1_w, w_in, conv_w, w_bc, D_skip, w_out, norm2_w, ff_w1, ff_b1, ff_w2, ff_b2):
        import jax, jax.numpy as jnp
        import numpy as np
        D_MODEL = 192
        D_STATE = 8
        EXPAND = 2
        D_HEAD = 64
        D_CONV = 4
        D_INNER = EXPAND * D_MODEL
        N_HEADS = D_INNER // D_HEAD
        PARAM_DIM = 2
        D_PROJ = 2 * D_INNER + N_HEADS * PARAM_DIM
        D_FF = 4 * D_MODEL
        BATCH, SEQ = (2, 512)

        def _rmsnorm(x, w, eps=1e-06):
            return x * jax.lax.rsqrt(jnp.mean(x * x, axis=-1, keepdims=True) + eps) * w

        def _l2norm(x, eps=1e-12):
            return x * jax.lax.rsqrt(jnp.sum(x * x, axis=-1, keepdims=True) + eps)

        def _mixer(x, w_in, conv_w, w_bc, D_skip, w_out):
            Bsz, T, _ = x.shape
            proj = x @ w_in
            gate, vraw, params = jnp.split(proj, [D_INNER, 2 * D_INNER], axis=-1)
            vpad = jnp.pad(vraw, ((0, 0), (D_CONV - 1, 0), (0, 0)))
            kernel = conv_w.T[:, None, :]
            conv = jax.lax.conv_general_dilated(vpad, kernel, window_strides=(1,), padding='VALID', dimension_numbers=('NWC', 'WIO', 'NWC'), feature_group_count=D_INNER)
            v = jax.nn.silu(conv)
            bc = (v @ w_bc).reshape(Bsz, T, N_HEADS, 2, D_STATE)
            Bm = _l2norm(bc[..., 0, :])
            Cm = _l2norm(bc[..., 1, :])
            p = params.reshape(Bsz, T, N_HEADS, PARAM_DIM)
            A = jax.nn.softplus(p[..., 0])
            dt = jax.nn.sigmoid(p[..., 1])
            S = 1.0 / (1.0 + dt * dt * A)
            u = v.reshape(Bsz, T, N_HEADS, D_HEAD)
            tfirst = lambda a: jnp.moveaxis(a, 1, 0)

            def step(carry, inp):
                z, xs = carry
                Bt, Ct, At, dtt, St, ut = inp
                d = dtt[..., None, None]
                a = At[..., None, None]
                s = St[..., None, None]
                bu = Bt[..., :, None] * ut[..., None, :]
                z = s * (z - d * a * xs + d * bu)
                xs = xs + d * z
                y = jnp.einsum('bhn,bhnp->bhp', Ct, xs)
                return ((z, xs), y)
            z0 = jnp.zeros((Bsz, N_HEADS, D_STATE, D_HEAD), x.dtype)
            _, ys = jax.lax.scan(step, (z0, z0), (tfirst(Bm), tfirst(Cm), tfirst(A), tfirst(dt), tfirst(S), tfirst(u)))
            y = jnp.moveaxis(ys, 0, 1)
            gated = (y + D_skip[None, None, :, None] * u) * jax.nn.silu(gate).reshape(Bsz, T, N_HEADS, D_HEAD)
            return gated.reshape(Bsz, T, D_INNER) @ w_out
        x = x + _mixer(_rmsnorm(x, norm1_w), w_in, conv_w, w_bc, D_skip, w_out)
        h = _rmsnorm(x, norm2_w)
        return x + (jax.nn.gelu(h @ ff_w1 + ff_b1) @ ff_w2 + ff_b2)

    def _L0_ffn_ref(x, ln1_g, ln1_b, in_proj_w, in_proj_b, out_proj_w, out_proj_b, ln2_g, ln2_b, router_w, router_b, w1, b1, w2, b2):
        import jax, jax.numpy as jnp
        import numpy as np
        EPS = 1e-05

        def _ln(x, g, b):
            m = jnp.mean(x, axis=-1, keepdims=True)
            v = jnp.mean((x - m) ** 2, axis=-1, keepdims=True)
            return (x - m) / jnp.sqrt(v + EPS) * g + b
        B, S, D = x.shape
        H = 12
        Dh = D // H
        E = router_w.shape[0]
        K = 2
        x2 = _ln(x, ln1_g, ln1_b)
        qkv = x2 @ in_proj_w.T + in_proj_b
        q, k, v = jnp.split(qkv, 3, axis=-1)
        q = q.reshape(B, S, H, Dh)
        k = k.reshape(B, S, H, Dh)
        v = v.reshape(B, S, H, Dh)
        scores = jnp.einsum('bqhd,bkhd->bhqk', q, k) / jnp.sqrt(jnp.float32(Dh))
        attn = jax.nn.softmax(scores, axis=-1)
        ao = jnp.einsum('bhqk,bkhd->bqhd', attn, v).reshape(B, S, D)
        ao = ao @ out_proj_w.T + out_proj_b
        x = x + ao
        xm = _ln(x, ln2_g, ln2_b).reshape(B * S, D)
        T = B * S
        logits = xm @ router_w.T + router_b
        probs = jax.nn.softmax(logits, axis=-1)
        topw, topi = jax.lax.top_k(probs, K)
        topw = topw / jnp.sum(topw, axis=-1, keepdims=True)
        combine = jnp.zeros((T, E), xm.dtype).at[jnp.arange(T)[:, None], topi].add(topw)
        out = jnp.zeros_like(xm)
        for e in range(E):
            h = jax.nn.gelu(xm @ w1[e] + b1[e], approximate=False)
            y = h @ w2[e] + b2[e]
            out = out + combine[:, e:e + 1] * y
        x = x + out.reshape(B, S, D)
        return x

    def _L1_attn_ref(x, W, b, bn_gamma, bn_beta, bn_mean, bn_var):
        import jax, jax.numpy as jnp
        import numpy as np
        TAU = 2.0
        BN_EPS = 1e-05
        SG_ALPHA = 2.0

        @jax.custom_vjp
        def spike(u):
            return (u >= 0).astype(u.dtype)

        def _spike_fwd(u):
            return (spike(u), u)

        def _spike_bwd(u, g):
            sg = SG_ALPHA / 2.0 / (1.0 + (jnp.pi / 2.0 * SG_ALPHA * u) ** 2)
            return (g * sg,)
        spike.defvjp(_spike_fwd, _spike_bwd)

        def lif(x, v_th):
            return spike(x / TAU - v_th)

        def bn_eval(x, gamma, beta, mean, var):
            inv = gamma / jnp.sqrt(var + BN_EPS)
            return x * inv + (beta - mean * inv)
        B, N, D = x.shape
        H = 12
        Hd = D // H
        scale = Hd ** (-0.125)

        def branch(inp, i, v_th=1.0):
            y = jnp.einsum('bnd,od->bno', inp, W[i]) + b[i]
            y = bn_eval(y, bn_gamma[i], bn_beta[i], bn_mean[i], bn_var[i])
            return lif(y, v_th)
        q = branch(x, 0)
        k = branch(x, 1)
        v = branch(x, 2)
        q = q.reshape(B, N, H, Hd).transpose(0, 2, 1, 3)
        k = k.reshape(B, N, H, Hd).transpose(0, 2, 1, 3)
        v = v.reshape(B, N, H, Hd).transpose(0, 2, 1, 3)
        attn = jnp.einsum('bhnd,bhmd->bhnm', q, k) * scale
        xa = jnp.einsum('bhnm,bhmd->bhnd', attn, v)
        xa = xa.transpose(0, 2, 1, 3).reshape(B, N, D)
        xa = lif(xa, 0.5)
        xa = branch(xa, 3)
        return xa

    def _L1_ffn_ref(x, gumbel_weights, n1l_g, n1l_b, n1s_g, n1s_b, w_qkv, w_proj, b_proj, n2l_g, n2l_b, n2s_g, n2s_b, w_fc1, b_fc1, w_fc2, b_fc2):
        import jax, jax.numpy as jnp
        import numpy as np
        H = 12
        ALPHA = (1, 2, 3)
        DEPTH = 5
        BLOCK_DEPTH = 3
        TOTAL_DEPTH_M1 = 14 - 1
        SMALL_ACTIVE = BLOCK_DEPTH <= DEPTH <= TOTAL_DEPTH_M1 - BLOCK_DEPTH

        def _ln(x, g, b, eps=1e-05):
            m = jnp.mean(x, axis=-1, keepdims=True)
            v = jnp.mean((x - m) ** 2, axis=-1, keepdims=True)
            return (x - m) * jax.lax.rsqrt(v + eps) * g + b

        def _attn_branch(xp, w_qkv, w_proj, b_proj, keep_heads, keep_ch):
            B2, N, C = xp.shape
            hd = C // H
            scale = hd ** (-0.5)
            qkv = (xp @ w_qkv).reshape(B2, N, 3, H, hd).transpose(2, 0, 3, 1, 4)
            hmask = (jnp.arange(H) < keep_heads).astype(xp.dtype)[None, :, None, None]
            q, k, v = (qkv[0] * hmask, qkv[1] * hmask, qkv[2] * hmask)
            a = jax.nn.softmax(jnp.einsum('bhnd,bhmd->bhnm', q, k) * scale, axis=-1)
            o = jnp.einsum('bhnm,bhmd->bhnd', a, v).transpose(0, 2, 1, 3).reshape(B2, N, C)
            o = o @ w_proj + b_proj
            cmask = (jnp.arange(C) < keep_ch).astype(xp.dtype)
            return o * cmask

        def _mlp_branch(xp, w1, b1, w2, b2, keep_ch):
            C = xp.shape[-1]
            cmask = (jnp.arange(C) < keep_ch).astype(xp.dtype)
            h = jax.nn.gelu(xp * cmask @ w1 + b1, approximate=False)
            return (h @ w2 + b2) * cmask
        B, N, C = x.shape
        B2 = B // 2
        nl = _ln(x[:B2], n1l_g, n1l_b)
        ns = _ln(x[B2:], n1s_g, n1s_b)
        a_large = _attn_branch(nl, w_qkv, w_proj, b_proj, H, C)
        if SMALL_ACTIVE:
            a_small = sum((gumbel_weights[i] * _attn_branch(ns, w_qkv, w_proj, b_proj, H // ALPHA[i], C // ALPHA[i]) for i in range(3)))
            attn_out = jnp.concatenate([a_large, a_small], axis=0)
        else:
            attn_out = jnp.concatenate([a_large, a_large], axis=0)
        x = x + attn_out
        nl2 = _ln(x[:B2], n2l_g, n2l_b)
        ns2 = _ln(x[B2:], n2s_g, n2s_b)
        m_large = _mlp_branch(nl2, w_fc1, b_fc1, w_fc2, b_fc2, C)
        if SMALL_ACTIVE:
            m_small = sum((gumbel_weights[i] * _mlp_branch(ns2, w_fc1, b_fc1, w_fc2, b_fc2, C // ALPHA[i]) for i in range(3)))
            mlp_out = jnp.concatenate([m_large, m_small], axis=0)
        else:
            mlp_out = jnp.concatenate([m_large, m_large], axis=0)
        return x + mlp_out
    h = _L0_tok_ref(x, L0_tok_freq_bands, L0_tok_W)
    h = jnp.concatenate([jnp.broadcast_to(cls_tok, (h.shape[0], 1, h.shape[2])), h], axis=1)
    h = h + _L0_attn_ref(_layernorm(h, axis=-1), L0_attn_norm1_w, L0_attn_w_in, L0_attn_conv_w, L0_attn_w_bc, L0_attn_D_skip, L0_attn_w_out, L0_attn_norm2_w, L0_attn_ff_w1, L0_attn_ff_b1, L0_attn_ff_w2, L0_attn_ff_b2)
    h = h + _L0_ffn_ref(_layernorm(h, axis=-1), L0_ffn_ln1_g, L0_ffn_ln1_b, L0_ffn_in_proj_w, L0_ffn_in_proj_b, L0_ffn_out_proj_w, L0_ffn_out_proj_b, L0_ffn_ln2_g, L0_ffn_ln2_b, L0_ffn_router_w, L0_ffn_router_b, L0_ffn_w1, L0_ffn_b1, L0_ffn_w2, L0_ffn_b2)
    h = h + _L1_attn_ref(_layernorm(h, axis=-1), L1_attn_W, L1_attn_b, L1_attn_bn_gamma, L1_attn_bn_beta, L1_attn_bn_mean, L1_attn_bn_var)
    h = h + _L1_ffn_ref(_layernorm(h, axis=-1), L1_ffn_gumbel_weights, L1_ffn_n1l_g, L1_ffn_n1l_b, L1_ffn_n1s_g, L1_ffn_n1s_b, L1_ffn_w_qkv, L1_ffn_w_proj, L1_ffn_b_proj, L1_ffn_n2l_g, L1_ffn_n2l_b, L1_ffn_n2s_g, L1_ffn_n2s_b, L1_ffn_w_fc1, L1_ffn_b_fc1, L1_ffn_w_fc2, L1_ffn_b_fc2)
    return h

_drawn_inputs = setup_inputs


def setup_inputs(seed=0):
    import zlib

    import numpy as np

    out = dict(_drawn_inputs(seed))
    spreads = {'L0_attn_norm1_w': (1.0, 0.2),
     'L0_attn_norm2_w': (1.0, 0.2),
     'L0_attn_ff_b1': (0.0, 0.1),
     'L0_attn_ff_b2': (0.0, 0.1),
     'L0_ffn_ln1_g': (1.0, 0.6),
     'L0_ffn_ln1_b': (0.0, 0.8),
     'L0_ffn_in_proj_b': (0.0, 0.646),
     'L0_ffn_out_proj_b': (0.0, 0.1),
     'L0_ffn_ln2_g': (1.0, 0.6),
     'L0_ffn_ln2_b': (0.0, 0.8),
     'L0_ffn_router_b': (0.0, 0.446),
     'L0_ffn_b1': (0.0, 0.8),
     'L0_ffn_b2': (0.0, 0.293),
     'L1_attn_b': (0.0, 0.1),
     'L1_ffn_n1l_g': (1.0, 0.6),
     'L1_ffn_n1l_b': (0.0, 0.8),
     'L1_ffn_n1s_g': (1.0, 0.6),
     'L1_ffn_n1s_b': (0.0, 0.8),
     'L1_ffn_b_proj': (0.0, 0.346),
     'L1_ffn_n2l_g': (1.0, 0.6),
     'L1_ffn_n2l_b': (0.0, 0.8),
     'L1_ffn_n2s_g': (1.0, 0.6),
     'L1_ffn_n2s_b': (0.0, 0.8),
     'L1_ffn_b_fc1': (0.0, 0.8),
     'L1_ffn_b_fc2': (0.0, 0.395)}
    factors = {'L0_ffn_in_proj_w': 6.427,
     'L0_ffn_out_proj_w': 3.772,
     'L1_ffn_gumbel_weights': 8.0,
     'L1_ffn_w_qkv': 8.0,
     'L1_ffn_w_proj': 8.0,
     'L1_ffn_w_fc1': 3.275,
     'L1_ffn_w_fc2': 3.031}
    for name, (base, spread) in spreads.items():
        noise = np.random.default_rng([zlib.crc32(name.encode()), seed]).standard_normal(out[name].shape)
        drawn = base * np.exp(spread * noise) if base else spread * noise
        out[name] = jnp.asarray(drawn.astype(out[name].dtype))
    for name, factor in factors.items():
        out[name] = (out[name] * factor).astype(out[name].dtype)
    return out
```

```python
from contextlib import ExitStack

import numpy as np

import concourse.bass as bass
from concourse import mybir

ALU = mybir.AluOpType
ACT = mybir.ActivationFunctionType
F32 = mybir.dt.float32
F16 = mybir.dt.float16
X = mybir.AxisListType.X

BATCH, SEQ, D = 4, 512, 192
T = SEQ + 1
NT = BATCH * T
TT = 114
NTILE = NT // TT
CW = 3 * TT
NCH = NT // CW
DH = D // 2
NW = SEQ * 3 * D * BATCH // (BATCH * SEQ)
NB2 = 12
HEADS, HD = 12, 16
FF = 4 * D
NF = FF // 128
EXPERTS = 8
DIN, SH, ST, SP = 384, 6, 8, 64
L = 57
NC1 = T // L
NBC = NT // L
LANES = NBC * SH // 2
KT = [(k * TT, min(TT, T - k * TT)) for k in range((T + TT - 1) // TT)]
MAGIC = 12582912.0
TWO_PI = 6.283185
HALF_PI = 1.5707963

CONST = {}


def _constants():
    p = np.arange(128)
    parts = [("ident", np.eye(128))]
    row_h, row_z, row_n = p // 16, (p // 8) % 2, p % 8
    parts.append(("bd", (row_h[:, None] == (np.arange(DIN) // SP)[None]) & (p < 96)[:, None]))
    q = np.arange(96)
    swap = np.zeros((128, 96))
    swap[q, (q // 16) * 16 + (1 - (q // 8) % 2) * 8 + q % 8] = 1
    parts.append(("swap", swap))
    parts.append(("h48", (p // 8)[:, None] == np.arange(SH)[None]))
    for z in range(2):
        parts.append((f"sel{z}", ((p % SH)[:, None] == (q // 16)[None]) & (((q // 8) % 2) == z)[None]))
    parts.append(("bc", (p // SH)[:, None] == np.arange(NBC // 2)[None]))
    parts.append(("kv", (p // HD)[:, None] == (q // HD)[None]))
    parts.append(("rank", np.broadcast_to(EXPERTS - np.arange(EXPERTS), (128, EXPERTS))))
    at, cols = 0, []
    for name, a in parts:
        CONST[name] = (at, a.shape[1])
        at += a.shape[1]
        cols.append(np.asarray(a, np.float32))
    return np.ascontiguousarray(np.concatenate(cols, 1))


CONSTANTS = _constants()


class Own:

    def __init__(self, eng, sem):
        self.eng, self.sem, self.n = eng, sem, 0

    def did(self, ins):
        self.n += 1
        ins.then_inc(self.sem, 1)
        return ins

    def wait(self, but=0):
        if self.n > but:
            self.eng.wait_ge(self.sem, self.n - but)


class Core:

    def __init__(self, nc, ins):
        self.nc, self.ins, self.sems = nc, ins, []
        self.stored = nc.alloc_semaphore("out_stored")
        self.pair = [nc.alloc_psum_tensor(f"banks{2 * i}{2 * i + 1}", [128, 1024], F32) for i in range(4)]
        self.bank = [self.pair[i // 2][:, i % 2 * 512:(i % 2 + 1) * 512] for i in range(8)]

    def sem(self, name):
        self.sems.append(self.nc.alloc_semaphore(name))
        return self.sems[-1]

    def layer_end(self):
        self.nc.all_engine_barrier()
        self.nc.clear_and_free_semaphores(self.sems)
        self.nc.all_engine_barrier()
        self.sems = []

    def sb(self, ctx, name, shape, dt=F32):
        return ctx.enter_context(self.nc.sbuf_tensor(name, shape, dt))

    def const(self, name, rows=128):
        at, n = CONST[name]
        return self.consts[0:rows, at:at + n]


def bc(ap, shape):
    return ap.broadcast_to(shape)


def load_shared(c, out_ctx):
    nc = c.nc
    c.consts = c.sb(out_ctx, "consts", [128, CONSTANTS.shape[1]])
    c.ones = c.sb(out_ctx, "ones", [128, 512])
    c.hN = c.sb(out_ctx, "hN", [128, NTILE, D])
    loaded, ones_set = c.sem("consts_loaded"), c.sem("ones_set")
    with nc.Block() as block:
        @block.sync
        def _(sp):
            sp.dma_start(c.consts[:, :], c.ins["consts"]).then_inc(loaded, 16)
            sp.wait_ge(loaded, 16)

        @block.vector
        def _(dve):
            dve.memset(c.ones[:, :], 1.0).then_inc(ones_set, 1)
            dve.wait_ge(ones_set, 1)


def layer_buffers(c, ctx):
    c.xN = c.sb(ctx, "xN", [128, NTILE, D])
    c.xT = c.sb(ctx, "xT", [DH, 2, NT])


def tok_features(c):
    nc = c.nc
    NCC = 5
    CC = [(k * 128, min(128, NW - k * 128)) for k in range(NCC)]
    HALF = NT // 2
    with ExitStack() as ctx:
        wT = c.sb(ctx, "tok_wT", [128, NCC, NB2, D])
        rT = c.sb(ctx, "raw_T", [128, NCC, NT])
        freq = c.sb(ctx, "freq", [128, 6])
        with ExitStack() as early:
            w = c.sb(early, "tok_w", [DH, 2, NW * NB2])
            raw = c.sb(early, "raw", [128, 4, 4, NW])
            w_in, raw_in, f_in = c.sem("tok_w_in"), c.sem("raw_in"), c.sem("freq_in")
            tp, ev = c.sem("tok_transposed"), [c.sem("tok_copied_v"), c.sem("tok_copied_s")]
            zero_set = c.sem("cls_columns_zeroed")
            jobs = []
            for i in range(BATCH):
                for k, (c0, n) in enumerate(CC):
                    jobs.append(("raw", i, k, n))
            for k, (c0, n) in enumerate(CC):
                for f in range(0, NB2, 2):
                    jobs.append(("w", k, f, n))
            with nc.Block() as block:
                @block.sync
                def _(sp):
                    for b in range(BATCH):
                        sp.dma_start(raw[:, b, :, :], c.ins["x"][b].rearrange("c n d -> (c n d)").rearrange(
                            "(i p w) -> p i w", p=128, w=NW)).then_inc(raw_in, 16)
                    for o in range(2):
                        sp.dma_start(w[:, o, :], c.ins["L0_tok_W"][o * DH:(o + 1) * DH, :]).then_inc(w_in, 16)
                    sp.dma_start(freq[:, :], c.ins["L0_tok_freq_bands"].rearrange(
                        "(a n) -> a n", a=1).broadcast_to((128, 6))).then_inc(f_in, 16)
                    sp.wait_ge(f_in, 16)

                @block.tensor
                def _(pe):
                    pe.wait_ge(raw_in, 16 * BATCH)
                    for n, (kind, a, k, m) in enumerate(jobs):
                        if n >= 8:
                            pe.wait_ge(ev[n % 2], (n - 8) // 2 + 1)
                        if kind == "raw":
                            for i in range(4):
                                c0 = CC[k][0]
                                ins = pe.transpose(c.bank[n % 8][0:m, i * 128:(i + 1) * 128],
                                                   raw[:, a, i, c0:c0 + m], c.const("ident"))
                        else:
                            if n == BATCH * NCC:
                                pe.wait_ge(w_in, 32)
                            c0 = CC[a][0]
                            for f in range(2):
                                for o in range(2):
                                    s = c0 * NB2 + k + f
                                    ins = pe.transpose(
                                        c.bank[n % 8][0:m, (f * 2 + o) * DH:(f * 2 + o + 1) * DH],
                                        w[:, o, s:s + (m - 1) * NB2 + 1:NB2], c.const("ident", DH)[:, 0:DH])
                        ins.then_inc(tp, 1)

                def copy_out(eng, copy, par):
                    for n, (kind, a, k, m) in enumerate(jobs):
                        if n % 2 != par:
                            continue
                        eng.wait_ge(tp, n + 1)
                        if kind == "raw":
                            dst = rT[0:m, k, a * T + 1:(a + 1) * T]
                            src = c.bank[n % 8][0:m, :]
                        else:
                            dst = wT[0:m, a, k:k + 2, :].rearrange("p f d -> p (f d)")
                            src = c.bank[n % 8][0:m, 0:2 * D]
                        copy(dst, src).then_inc(ev[par], 1)

                @block.vector
                def _(dve):
                    for b in range(BATCH):
                        dve.memset(rT[:, :, b * T:b * T + 1], 0.0).then_inc(zero_set, 1)
                    copy_out(dve, dve.tensor_copy, 0)

                @block.scalar
                def _(act):
                    copy_out(act, act.copy, 1)

        fy = c.sb(ctx, "angle", [128, HALF])
        fm = c.sb(ctx, "angle_rounded", [128, HALF])
        fr = c.sb(ctx, "angle_rest", [128, 2, HALF])
        fa = c.sb(ctx, "angle_abs", [128, 2, HALF])
        feat = c.sb(ctx, "features", [128, 2, 2, HALF])
        halfpi = c.sb(ctx, "half_pi", [128, 1])
        vown = c.sem("tok_v_own")
        rest, used = c.sem("angle_ready"), c.sem("angle_used")
        fready, fused = c.sem("features_ready"), c.sem("features_used")
        accd, out_v, cls_in = c.sem("tok_accumulated"), c.sem("tok_h_written"), c.sem("cls_in")
        steps = [(hf, k, f) for hf in range(2) for k in range(NCC) for f in range(6)]
        per = NCC * 6
        with nc.Block() as block:
            @block.vector
            def _(dve):
                own = Own(dve, vown)
                own.did(dve.memset(halfpi[:, :], HALF_PI))

                def write_h(hf):
                    dve.wait_ge(accd, hf + 1)
                    for t in range(9):
                        dve.tensor_copy(c.hN[0:TT, hf * 9 + t, :],
                                        c.bank[t // 2][0:TT, (t % 2) * D:(t % 2 + 1) * D]).then_inc(out_v, 1)

                for n, (hf, k, f) in enumerate(steps):
                    m, s = CC[k][1], n % 2
                    src = rT[0:m, k, hf * HALF:(hf + 1) * HALF]
                    own.did(dve.tensor_scalar(fy[0:m, :], src, freq[0:m, f:f + 1], None, ALU.mult))
                    own.wait()
                    own.did(dve.tensor_scalar(fm[0:m, :], fy[0:m, :], MAGIC, MAGIC, ALU.add, ALU.subtract))
                    own.wait()
                    if n >= 2:
                        dve.wait_ge(used, 2 * (n - 1))
                    own.did(dve.tensor_tensor(fr[0:m, s, :], fy[0:m, :], fm[0:m, :], ALU.subtract))
                    own.wait()
                    dve.scalar_tensor_tensor(fa[0:m, s, :], fr[0:m, s, :], -1.0, fr[0:m, s, :], ALU.mult, ALU.max).then_inc(rest, 1)
                    if n == per:
                        write_h(0)
                write_h(1)

            @block.scalar
            def _(act):
                for n, (hf, k, f) in enumerate(steps):
                    m, s = CC[k][1], n % 2
                    act.wait_ge(rest, n + 1)
                    if n >= 2:
                        act.wait_ge(fused, n - 1)
                    act.activation(feat[0:m, s, 0, :], fr[0:m, s, :], ACT.Sin, scale=TWO_PI).then_inc(used, 1)
                    act.activation(feat[0:m, s, 1, :], fa[0:m, s, :], ACT.Sin, bias=halfpi[0:m, :],
                                   scale=-TWO_PI).then_inc(used, 1)

            @block.tensor
            def _(pe):
                for n, (hf, k, f) in enumerate(steps):
                    m, s = CC[k][1], n % 2
                    pe.wait_ge(used, 2 * n + 2)
                    if n == per:
                        pe.wait_ge(out_v, 9)
                    for q in range(2):
                        for t in range(9):
                            ins = pe.matmul(c.bank[t // 2][0:TT, (t % 2) * D:(t % 2 + 1) * D],
                                            feat[0:m, s, q, t * TT:(t + 1) * TT], wT[0:m, k, 6 * q + f, :],
                                            start=(n % per == 0 and q == 0 and t % 2 == 0),
                                            stop=(n % per == per - 1 and q == 1), skip_group_check=True)
                    ins.then_inc(fused, 1)
                    if n % per == per - 1:
                        pe.matmul(c.bank[7][0:1, 0:1], c.ones[0:1, 0:1], c.ones[0:1, 0:1],
                                  start=True, stop=True).then_inc(accd, 1)

            @block.sync
            def _(sp):
                sp.wait_ge(out_v, 18)
                for b in range(BATCH):
                    t, r = divmod(b * T, TT)
                    sp.dma_start(c.hN[r:r + 1, t, :], c.ins["cls_tok"][0]).then_inc(cls_in, 16)
                sp.wait_ge(cls_in, 16 * BATCH)


def stats(dve, own, c, src, st, mv):
    for i in range(NTILE):
        own.did(dve.bn_stats(st[0:TT, i, :], src[0:TT, i, :]))
    own.wait()
    for i in range(NTILE):
        own.did(dve.bn_aggr(mv[0:TT, i, :], st[0:TT, i, :]))
    own.wait()


def norm(c, name, outer, kind, gains, biases=None, residual=False):
    nc = c.nc
    with ExitStack() as ctx:
        st = c.sb(ctx, name + "_st", [128, NTILE, 6])
        mv = c.sb(ctx, name + "_mv", [128, NTILE, 2])
        ve = c.sb(ctx, name + "_ve", [128, NTILE])
        sd = c.sb(ctx, name + "_sd", [128, NTILE])
        rs = c.sb(ctx, name + "_rs", [128, NTILE])
        yN = c.sb(ctx, name + "_yN", [128, NTILE, D])
        gb = c.sb(ctx, name + "_gb", [DH, 4, 2])
        own_s, gb_in = c.sem(name + "_v_own"), c.sem(name + "_gains_in")
        var_ready, sd_ready, y_ready = c.sem(name + "_var"), c.sem(name + "_sqrt"), c.sem(name + "_normed")
        tp, ev = c.sem(name + "_transposed"), [c.sem(name + "_cp_v"), c.sem(name + "_cp_s")]
        n_dma = len(gains or []) + len(biases or [])
        halves = len(gains) if gains else 1
        src = yN if kind else c.xN
        passes = int(outer) + (kind is not None)
        with nc.Block() as block:
            @block.sync
            def _(sp):
                for i, g in enumerate((gains or []) + (biases or [])):
                    at = i if i < halves else 2 + i - halves
                    sp.dma_start(gb[:, at, :], c.ins[g].rearrange("(o p) -> p o", p=DH),
                                 allow_slow_non_contiguous=True).then_inc(gb_in, 16)
                if n_dma:
                    sp.wait_ge(gb_in, 16 * n_dma)

            def copy_out(eng, par):
                if n_dma:
                    eng.wait_ge(gb_in, 16 * n_dma)
                for n in range(2 * NCH):
                    if n % 2 != par:
                        continue
                    ch, o = divmod(n, 2)
                    half = 1 if halves == 2 and ch >= NCH // 2 else 0
                    eng.wait_ge(tp, n + 1)
                    dst, ps = c.xT[:, o, ch * CW:(ch + 1) * CW], c.bank[n % 8][0:DH, 0:CW]
                    g, b = gb[:, half, o:o + 1], gb[:, 2 + half, o:o + 1]
                    if par == 0:
                        if not gains:
                            ins = eng.tensor_copy(dst, ps)
                        elif biases:
                            ins = eng.tensor_scalar(dst, ps, g, b, ALU.mult, ALU.add)
                        else:
                            ins = eng.tensor_scalar(dst, ps, g, None, ALU.mult)
                    else:
                        if not gains:
                            ins = eng.activation(dst, ps, ACT.Copy)
                        elif biases:
                            ins = eng.activation(dst, ps, ACT.Identity, bias=b, scale=g)
                        else:
                            ins = eng.activation(dst, ps, ACT.Copy, scale=g)
                    ins.then_inc(ev[par], 1)

            @block.vector
            def _(dve):
                own = Own(dve, own_s)
                done = 0

                def rstd(e):
                    nonlocal done
                    dve.tensor_scalar(ve[0:TT, :], var, e, None, ALU.add).then_inc(var_ready, 1)
                    done += 1
                    dve.wait_ge(sd_ready, done)
                    own.did(dve.reciprocal(rs[0:TT, :], sd[0:TT, :]))
                    own.wait()

                if residual:
                    own.did(dve.tensor_tensor(c.hN[0:TT, :, :], c.hN[0:TT, :, :], c.xN[0:TT, :, :], ALU.add))
                    own.wait()
                if outer:
                    stats(dve, own, c, c.hN, st, mv)
                    var = mv[0:TT, :, 1]
                    rstd(1e-5)
                    for i in range(NTILE):
                        ins = dve.tensor_scalar(c.xN[0:TT, i, :], c.hN[0:TT, i, :], mv[0:TT, i, 0:1],
                                                rs[0:TT, i:i + 1], ALU.subtract, ALU.mult)
                        if kind is None:
                            ins.then_inc(y_ready, 1)
                        else:
                            own.did(ins)
                    own.wait()
                if kind:
                    stats(dve, own, c, c.xN, st, mv)
                    var = mv[0:TT, :, 1]
                    if kind == "rms":
                        own.did(dve.tensor_tensor(ve[0:TT, :], mv[0:TT, :, 0], mv[0:TT, :, 0], ALU.mult))
                        own.wait()
                        own.did(dve.tensor_tensor(mv[0:TT, :, 1], ve[0:TT, :], mv[0:TT, :, 1], ALU.add))
                        own.wait()
                    rstd(1e-6 if kind == "rms" else 1e-5)
                    for i in range(NTILE):
                        if kind == "rms":
                            ins = dve.tensor_scalar(yN[0:TT, i, :], c.xN[0:TT, i, :], rs[0:TT, i:i + 1], None,
                                                    ALU.mult)
                        else:
                            ins = dve.tensor_scalar(yN[0:TT, i, :], c.xN[0:TT, i, :], mv[0:TT, i, 0:1],
                                                    rs[0:TT, i:i + 1], ALU.subtract, ALU.mult)
                        ins.then_inc(y_ready, 1)
                copy_out(dve, 0)

            @block.scalar
            def _(act):
                for i in range(passes):
                    act.wait_ge(var_ready, i + 1)
                    act.activation(sd[0:TT, :], ve[0:TT, :], ACT.Sqrt).then_inc(sd_ready, 1)
                copy_out(act, 1)

            @block.tensor
            def _(pe):
                for n in range(2 * NCH):
                    ch, o = divmod(n, 2)
                    if n >= 8:
                        pe.wait_ge(ev[n % 2], (n - 8) // 2 + 1)
                    pe.wait_ge(y_ready, 3 * ch + 3)
                    for i in range(3):
                        ins = pe.transpose(c.bank[n % 8][0:DH, i * TT:(i + 1) * TT],
                                           src[0:TT, 3 * ch + i, o * DH:(o + 1) * DH],
                                           c.const("ident", TT)[:, 0:TT])
                    ins.then_inc(tp, 1)


def mixer(c):
    with ExitStack() as ctx:
        sg = c.sb(ctx, "gate_silu", [128, 3, NT])
        vT = c.sb(ctx, "u_T", [128, 3, NT])
        coef = c.sb(ctx, "coef", [128, 3, 2, L])
        mixer_project(c, sg, vT, coef)
        gs = c.sb(ctx, "G_s", [128, L, 2 * LANES])
        acT = c.sb(ctx, "C_start_T", [96, NT])
        bw = c.sb(ctx, "B_end", [128, NBC * SH, 2, ST])
        ab = c.sb(ctx, "start_resp", [128, 2, 2 * LANES])
        zx = c.sb(ctx, "end_resp", [128, 2 * LANES])
        de = c.sb(ctx, "end_trans", [96, 2, NBC])
        with ExitStack() as inner:
            mixer_responses(c, inner, coef, gs, ab, zx, de)
        with ExitStack() as inner:
            mixer_bc(c, inner, vT, gs, ab, zx, acT, bw)
        with ExitStack() as inner:
            mixer_chain(c, inner, sg, vT, gs, acT, bw, de)
        with ExitStack() as inner:
            w = c.sb(inner, "mix_wout", [128, 3, D])
            to_tokens(c, "mixout", [(w[:, :, :], c.ins["L0_attn_w_out"].rearrange("(k p) n -> p k n", p=128))],
                      lambda i: [(sg[:, k, :], w[:, k, :]) for k in range(3)], None)


def to_tokens(c, name, loads, terms, row, into=None, spike=None):
    nc = c.nc
    into = c.xN if into is None else into
    w_in, done, added = c.sem(name + "_w_in"), c.sem(name + "_done"), c.sem(name + "_added")
    with nc.Block() as block:
        @block.sync
        def _(sp):
            for dst, src in loads:
                sp.dma_start(dst, src).then_inc(w_in, 16)

        @block.tensor
        def _(pe):
            if loads:
                pe.wait_ge(w_in, 16 * len(loads))
            for i in range(NTILE):
                if i >= 8:
                    pe.wait_ge(added, i - 7)
                ps = c.bank[i % 8][0:TT, 0:D]
                if row is not None:
                    pe.matmul(ps, c.ones[0:1, 0:TT], row(i), start=True, stop=False)
                for k, (a, w) in enumerate(terms(i)):
                    ins = pe.matmul(ps, a[:, i * TT:(i + 1) * TT], w, start=(row is None and k == 0),
                                    stop=(k == len(terms(i)) - 1))
                ins.then_inc(done, 1)

        @block.vector
        def _(dve):
            for i in range(NTILE):
                dve.wait_ge(done, i + 1)
                ps, x = c.bank[i % 8][0:TT, 0:D], into[0:TT, i, :]
                if spike is None:
                    ins = dve.tensor_tensor(x, ps, x, ALU.add)
                else:
                    ins = dve.scalar_tensor_tensor(x, ps, spike, x, ALU.is_ge, ALU.add)
                ins.then_inc(added, 1)


def mixer_project(c, sg, vT, coef):
    nc = c.nc
    PROJ = 2 * DIN + 2 * SH
    S3 = T // 3
    with ExitStack() as ctx:
        vpad = c.sb(ctx, "v_padded", [128, 3, BATCH, T + 3])
        w = c.sb(ctx, "mix_win", [DH, 2, PROJ])
        cw = c.sb(ctx, "conv_w", [128, 3, 4])
        par = c.sb(ctx, "params", [128, NBC * SH, 2])
        q3 = c.sb(ctx, "lane_values", [128, 3, NBC * SH])
        tmp = c.sb(ctx, "param_tmp", [128, 4, NBC * SH])
        w_in, cw_in = c.sem("mix_w_in"), c.sem("conv_w_in")
        proj, ev = c.sem("mix_projected"), [c.sem("mix_v_copied"), c.sem("mix_gate_done")]
        pad0, own_s, conv = c.sem("v_pad_zeroed"), c.sem("mixp_v_own"), c.sem("convolved")
        pdone, pcopy, a1, a2 = c.sem("params_done"), c.sem("params_copied"), c.sem("params_act"), c.sem("params_max")
        qs, qt, silu = c.sem("lane_ready"), c.sem("lane_transposed"), c.sem("u_done")
        jobs = [(g, m, b, s) for b in range(BATCH) for s in range(3) for m in range(3) for g in (1, 0)]
        with nc.Block() as block:
            @block.sync
            def _(sp):
                sp.dma_start(w[:, :, :], c.ins["L0_attn_w_in"].rearrange("(o p) n -> p o n", p=DH)).then_inc(w_in, 16)
                sp.dma_start(cw[:, :, :], c.ins["L0_attn_conv_w"].rearrange("(k p) t -> p k t", p=128)
                             ).then_inc(cw_in, 16)

            @block.tensor
            def _(pe):
                pe.wait_ge(w_in, 16)
                for i in range(NBC):
                    for o in range(2):
                        ins = pe.matmul(c.bank[7][0:L, i * 2 * SH:(i + 1) * 2 * SH],
                                        c.xT[:, o, i * L:(i + 1) * L], w[:, o, 2 * DIN:PROJ],
                                        start=(o == 0), stop=(o == 1))
                ins.then_inc(pdone, 1)
                for n, (g, m, b, s) in enumerate(jobs):
                    if n >= 6:
                        pe.wait_ge(ev[n % 2], (n - 6) // 2 + 1)
                    for o in range(2):
                        ins = pe.matmul(c.bank[n % 6][:, 0:S3], w[:, o, g * DIN + m * 128:g * DIN + (m + 1) * 128],
                                        c.xT[:, o, b * T + s * S3:b * T + (s + 1) * S3],
                                        start=(o == 0), stop=(o == 1))
                    ins.then_inc(proj, 1)
                    if n == len(jobs) // 2:
                        pe.wait_ge(qs, 1)
                        for q in range(3):
                            for g2 in range(2):
                                at = (q * 2 + g2) * L
                                ins = pe.transpose(c.bank[6][0:LANES, at:at + L],
                                                   q3[0:L, q, g2 * LANES:(g2 + 1) * LANES],
                                                   c.const("ident", L)[:, 0:L])
                        ins.then_inc(qt, 1)

            @block.scalar
            def _(act):
                act.wait_ge(a2, 1)
                act.activation(tmp[0:L, 1, :], tmp[0:L, 0, :], ACT.Exp).then_inc(a1, 1)
                act.wait_ge(a1, 1)
                act.activation(tmp[0:L, 2, :], tmp[0:L, 1, :], ACT.Ln, bias=1.0).then_inc(a1, 1)
                act.activation(q3[0:L, 0, :], par[0:L, :, 1], ACT.Sigmoid).then_inc(a1, 1)
                for n, (g, m, b, s) in enumerate(jobs):
                    if g == 0:
                        act.wait_ge(proj, n + 1)
                        act.activation(sg[:, m, b * T + s * S3:b * T + (s + 1) * S3], c.bank[n % 6][:, 0:S3],
                                       ACT.Silu).then_inc(ev[1], 1)
                for k in range(3):
                    act.wait_ge(conv, k + 1)
                    act.activation(vT[:, k, :], vT[:, k, :], ACT.Silu).then_inc(silu, 1)

            @block.vector
            def _(dve):
                own = Own(dve, own_s)
                dve.memset(vpad[:, :, :, 0:3], 0.0).then_inc(pad0, 1)
                dve.wait_ge(pdone, 1)
                own.did(dve.tensor_copy(par[0:L, :, :].rearrange("p a b -> p (a b)"), c.bank[7][0:L, 0:2 * SH * NBC]))
                own.wait()
                a, nega, lg = par[0:L, :, 0], tmp[0:L, 0, :], tmp[0:L, 2, :]
                dve.scalar_tensor_tensor(nega, a, -1.0, a, ALU.mult, ALU.min).then_inc(a2, 1)
                own.did(dve.tensor_scalar(tmp[0:L, 3, :], a, 0.0, None, ALU.max))
                for n, (g, m, b, s) in enumerate(jobs):
                    if g == 1:
                        dve.wait_ge(proj, n + 1)
                        dve.tensor_copy(vpad[:, m, b, 3 + s * S3:3 + (s + 1) * S3],
                                        c.bank[n % 6][:, 0:S3]).then_inc(ev[0], 1)
                    if n == 5:
                        dve.wait_ge(a1, 3)
                        own.wait()
                        A, dt, S = tmp[0:L, 3, :], q3[0:L, 0, :], q3[0:L, 1, :]
                        own.did(dve.tensor_tensor(A, A, lg, ALU.add))
                        own.did(dve.tensor_tensor(tmp[0:L, 1, :], dt, dt, ALU.mult))
                        own.wait()
                        own.did(dve.tensor_tensor(tmp[0:L, 1, :], tmp[0:L, 1, :], A, ALU.mult))
                        own.wait()
                        own.did(dve.tensor_scalar(tmp[0:L, 1, :], tmp[0:L, 1, :], 1.0, None, ALU.add))
                        own.wait()
                        own.did(dve.reciprocal(S, tmp[0:L, 1, :]))
                        own.wait()
                        own.did(dve.tensor_tensor(tmp[0:L, 1, :], S, dt, ALU.mult))
                        own.wait()
                        dve.scalar_tensor_tensor(q3[0:L, 2, :], tmp[0:L, 1, :], -1.0, A, ALU.mult,
                                                 ALU.mult).then_inc(qs, 1)
                dve.wait_ge(qt, 1)
                dve.tensor_copy(coef[0:LANES, :, :, :].rearrange("p a b c -> p (a b c)"),
                                c.bank[6][0:LANES, 0:6 * L]).then_inc(pcopy, 1)
                dve.wait_ge(cw_in, 16)
                dve.wait_ge(pad0, 1)
                dve.wait_ge(ev[0], len(jobs) // 2)
                for k in range(3):
                    o = vT[:, k, :].rearrange("p (b t) -> p b t", b=BATCH)
                    own.did(dve.tensor_scalar(o, vpad[:, k, :, 0:T], cw[:, k, 0:1], None, ALU.mult))
                    for t in range(1, 4):
                        own.wait()
                        ins = dve.scalar_tensor_tensor(o, vpad[:, k, :, t:t + T], cw[:, k, t:t + 1], o,
                                                       ALU.mult, ALU.add)
                        if t < 3:
                            own.did(ins)
                        else:
                            ins.then_inc(conv, 1)


def mixer_responses(c, ctx, coef, gs, ab, zx, de):
    nc = c.nc
    W = L + 2
    g = c.sb(ctx, "G", [128, 2, L, W])
    zb = c.sb(ctx, "z_state", [128, 2, W])
    zt = c.sb(ctx, "z_tmp", [128, 2, W])
    x0 = c.sb(ctx, "x_start", [128, W])
    sd = c.sb(ctx, "S_dt", [128, 2, L])
    r = c.sb(ctx, "lane_masked", [128, 2, 4, NBC // 2])
    own_s, masked = c.sem("scan_steps"), c.sem("lane_masked_ready")

    def scan_count(t):
        return 8 + 6 * (t + 1)

    tp, ev, rest_ev = c.sem("G_transposed"), [c.sem("G_copied_v"), c.sem("G_copied_s")], c.sem("resp_copied")
    P = LANES
    jobs = [(q, t0) for t0 in range(0, L, 4) for q in range(2)]
    with nc.Block() as block:
        def copy_out(eng, copy, par):
            for n, (q, t0) in enumerate(jobs):
                if par is not None and n % 2 != par:
                    continue
                k = min(4, L - t0)
                eng.wait_ge(tp, n + 1)
                copy(gs[0:L, t0:t0 + k, q * P:(q + 1) * P],
                     c.bank[n % 6][0:L, 0:k * P].rearrange("p (a b) -> p a b", a=k)).then_inc(ev[0 if par is None else par], 1)

        @block.vector
        def _(dve):
            own = Own(dve, own_s)
            own.did(dve.memset(g[0:P].rearrange("p a b c -> p (a b c)"), 0.0))
            own.did(dve.memset(zb[0:P, :, :], 0.0))
            own.did(dve.memset(x0[0:P, :], 0.0))
            own.did(dve.tensor_tensor(sd[0:P, :, :], coef[0:P, 0, :, :], coef[0:P, 1, :, :], ALU.mult))
            own.wait()
            own.did(dve.memset(zb[0:P, :, L:L + 1], 1.0))
            own.did(dve.memset(x0[0:P, L + 1:L + 2], 1.0))
            for q in range(2):
                flat = g[0:P, q, :, :].rearrange("p t s -> p (t s)")
                own.did(dve.tensor_copy(flat[:, 0:(L - 1) * (W + 1) + 1:W + 1], sd[0:P, q, :]))
            own.wait()

            def prev(q, t):
                return g[0:P, q, t - 1, :] if t else x0[0:P, :]

            for t in range(L):
                for q in range(2):
                    own.wait(1)
                    own.did(dve.scalar_tensor_tensor(zt[0:P, q, :], prev(q, t), coef[0:P, 2, q, t:t + 1],
                                                     g[0:P, q, t, :], ALU.mult, ALU.add))
                for q in range(2):
                    own.wait(1)
                    own.did(dve.scalar_tensor_tensor(zb[0:P, q, :], zb[0:P, q, :], coef[0:P, 1, q, t:t + 1],
                                                     zt[0:P, q, :], ALU.mult, ALU.add))
                for q in range(2):
                    own.wait(1)
                    own.did(dve.scalar_tensor_tensor(g[0:P, q, t, :], zb[0:P, q, :], coef[0:P, 0, q, t:t + 1],
                                                     prev(q, t), ALU.mult, ALU.add))
                assert own.n == scan_count(t)
            own.wait()
            for q in range(2):
                vals = [zb[0:P, q, L:L + 1], g[0:P, q, L - 1, L + 1:L + 2],
                        g[0:P, q, L - 1, L:L + 1], zb[0:P, q, L + 1:L + 2]]
                for j, v in enumerate(vals):
                    dve.tensor_scalar(r[0:P, q, j, :], c.const("bc", P), v, None, ALU.mult).then_inc(masked, 1)
            copy_out(dve, dve.tensor_copy, 0)
            dve.wait_ge(tp, len(jobs) + 1)
            dve.tensor_copy(ab[0:L, :, :].rearrange("p a b -> p (a b)"), c.bank[6][0:L, 0:4 * P]).then_inc(rest_ev, 1)
            dve.wait_ge(tp, len(jobs) + 3)
            dve.tensor_copy(zx[0:L, :], c.bank[7][0:L, 0:2 * P]).then_inc(rest_ev, 1)
            dve.tensor_copy(de[:, :, :].rearrange("p a b -> p (a b)"),
                            c.bank[7][0:96, 256:256 + 2 * NBC]).then_inc(rest_ev, 1)

        @block.scalar
        def _(act):
            copy_out(act, act.copy, 1)

        @block.tensor
        def _(pe):
            idn = c.const("ident", P)[:, 0:P]
            for n, (q, t0) in enumerate(jobs):
                k = min(4, L - t0)
                if n >= 6:
                    pe.wait_ge(ev[n % 2], (n - 6) // 2 + 1)
                pe.wait_ge(own_s, scan_count(t0 + k - 1))
                for t in range(t0, t0 + k):
                    ins = pe.transpose(c.bank[n % 6][0:L, (t - t0) * P:(t - t0 + 1) * P], g[0:P, q, t, 0:L], idn)
                ins.then_inc(tp, 1)
            for z in range(2):
                for q in range(2):
                    at = (z * 2 + q) * P
                    ins = pe.transpose(c.bank[6][0:L, at:at + P], g[0:P, q, :, L + z], idn)
            ins.then_inc(tp, 1)
            pe.wait_ge(masked, 8)
            for q in range(2):
                ins = pe.transpose(c.bank[7][0:L, q * P:(q + 1) * P], zb[0:P, q, 0:L], idn)
            ins.then_inc(tp, 1)
            for j in range(2):
                for q in range(2):
                    at = 256 + j * NBC + q * (NBC // 2)
                    for z in range(2):
                        ins = pe.matmul(c.bank[7][0:96, at:at + NBC // 2], c.const(f"sel{z}", P), r[0:P, q, 2 * j + z, :],
                                        start=(z == 0), stop=(z == 1))
            ins.then_inc(tp, 1)


def mixer_bc(c, ctx, vT, gs, ab, zx, acT, bw):
    nc = c.nc
    NG = NBC * SH
    w = c.sb(ctx, "w_bc", [128, 3, 96])
    bcn = c.sb(ctx, "bc_normed", [128, 2, NG, ST])
    ac = c.sb(ctx, "C_start", [128, NG, 2, ST])
    ss = c.sb(ctx, "bc_sumsq", [128, 2 * NG])
    sr = c.sb(ctx, "bc_norm", [128, 2 * NG])
    w_in, done, sq, own_s = c.sem("w_bc_in"), c.sem("bc_done"), c.sem("bc_squared"), c.sem("bc_own")
    sm, rt, nd = c.sem("bc_sums"), c.sem("bc_roots"), c.sem("bc_normed_ready")
    tp, ev = c.sem("bc_transposed"), [c.sem("bc_copied_v"), c.sem("bc_copied_s")]
    per = [min(5, NBC - 5 * i) for i in range(8)]
    jobs = [(kind, i) for kind in range(3) for i in range(0, NBC, 8)]
    with nc.Block() as block:
        @block.sync
        def _(sp):
            sp.dma_start(w[:, :, :], c.ins["L0_attn_w_bc"].rearrange("(k p) n -> p k n", p=128)).then_inc(w_in, 16)

        @block.tensor
        def _(pe):
            pe.wait_ge(w_in, 16)
            for i in range(NBC):
                for k in range(3):
                    ins = pe.matmul(c.bank[i // 5][0:L, (i % 5) * 96:(i % 5 + 1) * 96],
                                    vT[:, k, i * L:(i + 1) * L], w[:, k, :], start=(k == 0), stop=(k == 2))
                if i % 5 == 4 or i == NBC - 1:
                    ins.then_inc(done, 1)
            pe.wait_ge(nd, 10)
            for n, (kind, i) in enumerate(jobs):
                k = min(8, NBC - i)
                if n >= 8:
                    pe.wait_ge(ev[n % 2], (n - 8) // 2 + 1)
                rows = 48 if kind < 2 else 96
                for j in range(i, i + k):
                    src = (bcn[0:L, kind, j * SH:(j + 1) * SH, :].rearrange("p a b -> p (a b)") if kind < 2 else
                           ac[0:L, j * SH:(j + 1) * SH, :, :].rearrange("p a b c -> p (a b c)"))
                    ins = pe.transpose(c.bank[n % 8][0:rows, (j - i) * L:(j - i + 1) * L], src,
                                       c.const("ident", L)[:, 0:L])
                ins.then_inc(tp, 1)

        def copy_out(eng, copy, par):
            for n, (kind, i) in enumerate(jobs):
                if n % 2 != par:
                    continue
                k = min(8, NBC - i)
                rows = 48 if kind < 2 else 96
                eng.wait_ge(tp, n + 1)
                dst = c.xT[0:48, kind, i * L:(i + k) * L] if kind < 2 else acT[:, i * L:(i + k) * L]
                copy(dst, c.bank[n % 8][0:rows, 0:k * L]).then_inc(ev[par], 1)

        @block.scalar
        def _(act):
            for i in range(8):
                act.wait_ge(done, i + 1)
                n = per[i] * 96
                act.activation(ac[0:L].rearrange("p a b c -> p (a b c)")[:, i * 480:i * 480 + n],
                               c.bank[i][0:L, 0:n], ACT.Square).then_inc(sq, 1)
            act.wait_ge(sm, 1)
            act.activation(sr[0:L, :], ss[0:L, :], ACT.Sqrt).then_inc(rt, 1)
            copy_out(act, act.copy, 1)

        @block.vector
        def _(dve):
            own = Own(dve, own_s)
            dve.wait_ge(sq, 8)
            own.did(dve.tensor_reduce(ss[0:L, :], ac[0:L].rearrange("p a b c -> p (a b) c"), X, ALU.add))
            own.wait()
            dve.tensor_scalar(ss[0:L, :], ss[0:L, :], 1e-12, None, ALU.add).then_inc(sm, 1)
            dve.wait_ge(rt, 1)
            own.did(dve.reciprocal(ss[0:L, :], sr[0:L, :]))
            own.wait()
            for i in range(8):
                k = per[i] * SH
                dve.tensor_tensor(bcn[0:L, :, i * 30:i * 30 + k, :].rearrange("p z g n -> p g z n"),
                                  c.bank[i][0:L, 0:k * 2 * ST].rearrange("p (g z n) -> p g z n", z=2, n=ST),
                                  ss[0:L, i * 60:i * 60 + 2 * k].rearrange("p (g z) -> p g z", z=2).unsqueeze(3)
                                  .broadcast_to((L, k, 2, ST)), ALU.mult).then_inc(nd, 1)
            dve.wait_ge(nd, 8)
            for z in range(2):
                dve.tensor_tensor(ac[0:L, :, z, :], bcn[0:L, 1, :, :],
                                  ab[0:L, z, :].unsqueeze(2).broadcast_to((L, NG, ST)), ALU.mult).then_inc(nd, 1)
                end = zx[0:L, :] if z == 0 else gs[0:L, L - 1, :]
                own.did(dve.tensor_tensor(bw[0:L, :, z, :], bcn[0:L, 0, :, :],
                                          end.unsqueeze(2).broadcast_to((L, NG, ST)), ALU.mult))
            copy_out(dve, dve.tensor_copy, 0)


def mixer_chain(c, ctx, sg, vT, gs, acT, bw, de):
    nc = c.nc
    cbd = c.sb(ctx, "C_by_head", [48, 2, SH, L])
    u = c.sb(ctx, "u_tokens", [128, 2, DIN])
    wt = c.sb(ctx, "mix_matrix", [128, 2, SH, L])
    tm = c.sb(ctx, "transition", [96, 2, 96])
    state = c.sb(ctx, "state", [96, BATCH, 2, DIN])
    yd = c.sb(ctx, "y_plus_Du", [128, 2, 3, L])
    dsk = c.sb(ctx, "D_skip", [128, 3])
    names = ["cbd_ready", "u_transposed", "u_copied", "cb_done", "wt_ready", "y_done", "y_used", "tm_ready",
             "state_done", "state_ready"]
    cbd_ready, u_t, u_ready, cb_done, wt_ready, y_done, y_used, tm_ready, s_done, s_ready = map(c.sem, names)
    d_in, own_s = c.sem("D_skip_in"), c.sem("chain_own")
    N = NBC
    steps = [(ch, b, b * NC1 + ch) for ch in range(NC1) for b in range(BATCH)]
    last = N - BATCH
    with nc.Block() as block:
        @block.sync
        def _(sp):
            for e in range(2):
                for k in range(3):
                    h = 2 * k + e
                    sp.dma_start(dsk[64 * e:64 * e + 64, k:k + 1], c.ins["L0_attn_D_skip"][h:h + 1].rearrange(
                        "(a n) -> a n", a=1).broadcast_to((64, 1))).then_inc(d_in, 16)

        @block.gpsimd
        def _(pool):
            for n, (ch, b, bc_) in enumerate(steps):
                if n >= 2:
                    pool.wait_ge(cb_done, n - 1)
                pool.tensor_tensor(cbd[:, n % 2, :, :],
                                   c.xT[0:48, 1, bc_ * L:(bc_ + 1) * L].unsqueeze(1).broadcast_to((48, SH, L)),
                                   c.const("h48", 48).unsqueeze(2).broadcast_to((48, SH, L)),
                                   ALU.mult).then_inc(cbd_ready, 1)

        @block.scalar
        def _(act):
            for n in range(N):
                act.wait_ge(u_t, n + 1)
                if n >= 2:
                    act.wait_ge(y_done, n - 1)
                    act.wait_ge(s_done, min(n - 1, last))
                act.copy(u[0:L, n % 2, :], c.bank[n % 2][0:L, 0:DIN]).then_inc(u_ready, 1)

        @block.tensor
        def _(pe):
            def prepare(n):
                ch, b, bc_ = steps[n]
                if n >= 2:
                    pe.wait_ge(u_ready, n - 1)
                for k in range(3):
                    ins = pe.transpose(c.bank[n % 2][0:L, k * 128:(k + 1) * 128], vT[:, k, bc_ * L:(bc_ + 1) * L],
                                       c.const("ident"))
                ins.then_inc(u_t, 1)
                pe.wait_ge(cbd_ready, n + 1)
                if n >= 2:
                    pe.wait_ge(wt_ready, n - 1)
                pe.matmul(c.bank[2 + n % 2][0:L, 0:SH * L], c.xT[0:48, 0, bc_ * L:(bc_ + 1) * L],
                          cbd[:, n % 2, :, :].rearrange("p a b -> p (a b)"), start=True, stop=True).then_inc(cb_done, 1)

            prepare(0)
            for n, (ch, b, bc_) in enumerate(steps):
                if n + 1 < N:
                    prepare(n + 1)
                ybank, sbank = c.bank[4 + n % 2], c.bank[6 + n % 2]
                if n >= 2:
                    pe.wait_ge(y_used, 3 * (n - 1))
                if ch:
                    pe.wait_ge(s_ready, n - BATCH + 1)
                pe.wait_ge(u_ready, n + 1)
                if n < last:
                    pe.wait_ge(tm_ready, n + 1)
                    if ch:
                        pe.matmul(sbank[0:96, 0:DIN], tm[:, n % 2, :], state[:, b, (ch - 1) % 2, :],
                                  start=True, stop=False)
                    pe.matmul(sbank[0:96, 0:DIN],
                              bw[0:L, bc_ * SH:(bc_ + 1) * SH, :, :].rearrange("p a b c -> p (a b c)"),
                              u[0:L, n % 2, :], start=(ch == 0), stop=True).then_inc(s_done, 1)
                pe.wait_ge(wt_ready, n + 1)
                for k in range(3):
                    if ch:
                        pe.matmul(ybank[:, k * L:(k + 1) * L], state[:, b, (ch - 1) % 2, k * 128:(k + 1) * 128],
                                  acT[:, bc_ * L:(bc_ + 1) * L], start=True, stop=False, skip_group_check=True)
                    for e in range(2):
                        h = 2 * k + e
                        ins = pe.matmul(ybank[64 * e:64 * e + 64, k * L:(k + 1) * L],
                                        u[0:L, n % 2, h * SP:(h + 1) * SP], wt[0:L, n % 2, h, :],
                                        start=(ch == 0), stop=True, skip_group_check=True)
                ins.then_inc(y_done, 1)

        @block.vector
        def _(dve):
            own = Own(dve, own_s)

            def prepare(n):
                ch, b, bc_ = steps[n]
                if n < last:
                    if n >= 2:
                        dve.wait_ge(s_done, n - 1)
                    own.did(dve.tensor_scalar(tm[:, n % 2, :], c.const("ident", 96)[:, 0:96],
                                              de[:, 0, bc_:bc_ + 1], None, ALU.mult))
                    own.wait()
                    dve.scalar_tensor_tensor(tm[:, n % 2, :], c.const("swap", 96), de[:, 1, bc_:bc_ + 1],
                                             tm[:, n % 2, :], ALU.mult, ALU.add).then_inc(tm_ready, 1)
                dve.wait_ge(cb_done, n + 1)
                if n >= 2:
                    dve.wait_ge(y_done, n - 1)
                dve.tensor_tensor(wt[0:L, n % 2, :, :],
                                  c.bank[2 + n % 2][0:L, 0:SH * L].rearrange("p (a b) -> p a b", a=SH),
                                  gs[0:L, :, bc_ * SH:(bc_ + 1) * SH].rearrange("p t h -> p h t"),
                                  ALU.mult).then_inc(wt_ready, 1)

            dve.wait_ge(d_in, 96)
            prepare(0)
            for n, (ch, b, bc_) in enumerate(steps):
                if n + 1 < N:
                    prepare(n + 1)
                if n < last:
                    dve.wait_ge(s_done, n + 1)
                    if ch >= 2:
                        dve.wait_ge(y_done, n - BATCH + 1)
                    dve.tensor_tensor(state[:, b, ch % 2, :], c.bank[6 + n % 2][0:96, 0:DIN], c.const("bd", 96),
                                      ALU.mult).then_inc(s_ready, 1)
                dve.wait_ge(y_done, n + 1)
                for k in range(3):
                    dve.scalar_tensor_tensor(yd[:, n % 2, k, :], vT[:, k, bc_ * L:(bc_ + 1) * L], dsk[:, k:k + 1],
                                             c.bank[4 + n % 2][:, k * L:(k + 1) * L], ALU.mult, ALU.add
                                             ).then_inc(y_used, 1)
                dve.wait_ge(y_used, 3 * (n + 1))
                o = sg[:, :, bc_ * L:(bc_ + 1) * L]
                own.did(dve.tensor_tensor(o, yd[:, n % 2, :, :], o, ALU.mult))


def mlps(c, name, variants, func):
    nc = c.nc
    with ExitStack() as ctx:
        w1 = c.sb(ctx, name + "_w1", [DH, 2, 2, FF])
        w2 = c.sb(ctx, name + "_w2", [128, 2, NF, D])
        b1 = c.sb(ctx, name + "_b1", [128, 2, NF])
        b2 = c.sb(ctx, name + "_b2", [1, 2, D])
        hid = c.sb(ctx, name + "_hidden", [128, 2, NF, CW])
        w_in = [c.sem(name + "_w_in0"), c.sem(name + "_w_in1")]
        up, act_done, down, added = (c.sem(name + x) for x in ("_up", "_act", "_down", "_added"))
        jobs = [(v, ch) for v, va in enumerate(variants) for ch in va["chunks"]]
        first, final, before, seen = {}, {}, {}, {}
        for n, (v, ch) in enumerate(jobs):
            first.setdefault(v, n)
            final[v] = n
            before[n] = seen.get(ch)
            seen[ch] = n
        with nc.Block() as block:
            @block.sync
            def _(sp):
                for v, va in enumerate(variants):
                    s = v % 2
                    if v >= 2:
                        sp.wait_ge(down, 3 * (final[v - 2] + 1))
                        sp.wait_ge(act_done, NF * (final[v - 2] + 1))
                    sp.dma_start(w1[:, s, :, :], va["w1"].rearrange("(o p) n -> p o n", p=DH)).then_inc(w_in[s], 16)
                    sp.dma_start(w2[:, s, :, :], va["w2"].rearrange("(f p) n -> p f n", p=128)).then_inc(w_in[s], 16)
                    sp.dma_start(b1[:, s, :], va["b1"].rearrange("(f p) -> p f", p=128),
                                 allow_slow_non_contiguous=True).then_inc(w_in[s], 16)
                    sp.dma_start(b2[:, s, :], va["b2"].rearrange("(a n) -> a n", a=1)).then_inc(w_in[s], 16)

            @block.tensor
            def _(pe):
                def up_proj(n):
                    v, ch = jobs[n]
                    s = v % 2
                    if n == first[v]:
                        pe.wait_ge(w_in[s], 64 * (v // 2 + 1))
                    for f in range(NF):
                        m = n * NF + f
                        if m >= 4:
                            pe.wait_ge(act_done, m - 3)
                        parts = variants[v]["parts"]
                        for k, (o, rows) in enumerate(parts):
                            ins = pe.matmul(c.bank[m % 4][:, 0:CW], w1[0:rows, s, o, f * 128:(f + 1) * 128],
                                            c.xT[0:rows, o, ch * CW:(ch + 1) * CW],
                                            start=(k == 0), stop=(k == len(parts) - 1))
                        ins.then_inc(up, 1)

                up_proj(0)
                for n, (v, ch) in enumerate(jobs):
                    if n + 1 < len(jobs):
                        up_proj(n + 1)
                    s, cols = v % 2, variants[v]["n"]
                    pe.wait_ge(act_done, NF * (n + 1))
                    for i in range(3):
                        m = 3 * n + i
                        if m >= 4:
                            pe.wait_ge(added, m - 3)
                        ps = c.bank[4 + m % 4][0:TT, 0:cols]
                        pe.matmul(ps, c.ones[0:1, 0:TT], b2[:, s, 0:cols], start=True, stop=False)
                        for f in range(NF):
                            ins = pe.matmul(ps, hid[:, n % 2, f, i * TT:(i + 1) * TT], w2[:, s, f, 0:cols],
                                            start=False, stop=(f == NF - 1))
                        ins.then_inc(down, 1)

            @block.scalar
            def _(act):
                for n, (v, ch) in enumerate(jobs):
                    if n >= 2:
                        act.wait_ge(down, 3 * (n - 1))
                    for f in range(NF):
                        m = n * NF + f
                        act.wait_ge(up, m + 1)
                        act.activation(hid[:, n % 2, f, :], c.bank[m % 4][:, 0:CW], func,
                                       bias=b1[:, v % 2, f:f + 1]).then_inc(act_done, 1)

            @block.vector
            def _(dve):
                for n, (v, ch) in enumerate(jobs):
                    cols, gain = variants[v]["n"], variants[v]["gain"]
                    for i in range(3):
                        m, t = 3 * n + i, 3 * ch + i
                        dve.wait_ge(down, m + 1)
                        if before[n] is not None:
                            dve.wait_ge(added, 3 * before[n] + i + 1)
                        ps, x = c.bank[4 + m % 4][0:TT, 0:cols], c.xN[0:TT, t, 0:cols]
                        if gain is None:
                            ins = dve.tensor_tensor(x, ps, x, ALU.add)
                        else:
                            ins = dve.scalar_tensor_tensor(x, ps, gain(t), x, ALU.mult, ALU.add)
                        ins.then_inc(added, 1)


def qkv(c, name, sources, bias, qT, kT, v):
    nc = c.nc
    with ExitStack() as ctx:
        wqk = c.sb(ctx, name + "_wqk", [DH, 2, 2, 3 * 128])
        wv = c.sb(ctx, name + "_wv", [DH, 2, D])
        bqk = c.sb(ctx, name + "_bqk", [128, 2, 3])
        bv = c.sb(ctx, name + "_bv", [1, D])
        wrow = c.sb(ctx, name + "_rows", [DH, 6, D])
        w_in, pads, wr = c.sem(name + "_w_in"), c.sem(name + "_pads"), c.sem(name + "_w_placed")
        tp, ev = c.sem(name + "_done"), [c.sem(name + "_cp_v"), c.sem(name + "_cp_s")]
        qjobs = [(z, m, ch) for z in range(2) for m in range(3) for ch in range(NCH)]
        vjobs = [(b, k) for b in range(BATCH) for k in range(len(KT))]
        jobs = [("q", j) for j in qjobs] + [("v", j) for j in vjobs]
        ndma = 2 if not bias is None else 1
        with nc.Block() as block:
            @block.sync
            def _(sp):
                if bias is None:
                    for o in range(2):
                        sp.dma_start(wrow[:, 3 * o:3 * o + 3, :], sources[o * DH:(o + 1) * DH, :].rearrange(
                            "p (a n) -> p a n", a=3)).then_inc(w_in, 16)
                else:
                    sp.dma_start(wrow[:, :, :], sources.rearrange("(a p) n -> p a n", p=DH)).then_inc(w_in, 16)
                    sp.dma_start(bv[:, :], bias[2 * D:3 * D].rearrange("(a n) -> a n", a=1)).then_inc(w_in, 16)
                    sp.wait_ge(pads, 1)
                    for z in range(2):
                        for h in range(HEADS):
                            r, at = 32 * (h % 4), z * D + h * HD
                            sp.dma_start(bqk[r:r + HD, z, h // 4:h // 4 + 1],
                                         bias[at:at + HD].rearrange("(p a) -> p a", a=1),
                                         allow_slow_non_contiguous=True).then_inc(w_in, 16)

            @block.gpsimd
            def _(pool):
                pool.memset(bqk[:, :, :], 0.0).then_inc(pads, 1)
                pool.memset(wqk[:, :, :, :], 0.0).then_inc(pads, 1)
                pool.memset(v[:, :, :, :, HD:HD + 1], 1.0).then_inc(pads, 1)

            def head_view(o, z):
                return wqk[:, o, z, :].rearrange("p (h e) -> p h e", e=32)[:, :, 0:HD]

            n_w = 32 if bias is None else 32 + 16 * 2 * HEADS

            @block.tensor
            def _(pe):
                if bias is not None:
                    pe.wait_ge(w_in, n_w)
                    for a in range(6):
                        for o in range(2):
                            ins = pe.transpose(c.bank[a][0:DH, o * DH:(o + 1) * DH],
                                               wrow[:, a, o * DH:(o + 1) * DH], c.const("ident", DH)[:, 0:DH])
                        ins.then_inc(tp, 1)
                base = 0 if bias is None else 6
                pe.wait_ge(wr, 6)
                for n, (kind, j) in enumerate(jobs):
                    if n >= 8:
                        pe.wait_ge(ev[n % 2], (n - 8) // 2 + 1)
                    if kind == "q":
                        z, m, ch = j
                        for o in range(2):
                            ins = pe.matmul(c.bank[n % 8][:, 0:CW], wqk[:, o, z, m * 128:(m + 1) * 128],
                                            c.xT[:, o, ch * CW:(ch + 1) * CW], start=(o == 0), stop=(o == 1))
                    else:
                        b, k = j
                        k0, kn = KT[k]
                        ps = c.bank[n % 8][0:kn, 0:D]
                        if bias is not None:
                            pe.matmul(ps, c.ones[0:1, 0:kn], bv[:, :], start=True, stop=False)
                        for o in range(2):
                            ins = pe.matmul(ps, c.xT[:, o, b * T + k0:b * T + k0 + kn], wv[:, o, :],
                                            start=(bias is None and o == 0), stop=(o == 1))
                    ins.then_inc(tp, 1)

            def copy_out(eng, copy, par):
                base = 0 if bias is None else 6
                if bias is not None:
                    eng.wait_ge(w_in, n_w)
                eng.wait_ge(pads, 3)
                for n, (kind, j) in enumerate(jobs):
                    if n % 2 != par:
                        continue
                    eng.wait_ge(tp, base + n + 1)
                    if kind == "q":
                        z, m, ch = j
                        dst, ps = (qT, kT)[z][:, m, ch * CW:(ch + 1) * CW], c.bank[n % 8][:, 0:CW]
                        if bias is None:
                            ins = copy(dst, ps)
                        elif par:
                            ins = eng.activation(dst, ps, ACT.Identity, bias=bqk[:, z, m:m + 1])
                        else:
                            ins = eng.tensor_scalar(dst, ps, bqk[:, z, m:m + 1], None, ALU.add)
                    else:
                        b, k = j
                        kn = KT[k][1]
                        ins = copy(v[0:kn, b, k, :, 0:HD], c.bank[n % 8][0:kn, 0:D].rearrange("p (h e) -> p h e", e=HD))
                    ins.then_inc(ev[par], 1)

            @block.vector
            def _(dve):
                dve.wait_ge(pads, 2)
                if bias is None:
                    dve.wait_ge(w_in, n_w)
                    for o in range(2):
                        for z in range(2):
                            dve.tensor_copy(head_view(o, z), wrow[:, 3 * o + z, :].rearrange("p (h e) -> p h e", e=HD)
                                            ).then_inc(wr, 1)
                        dve.tensor_copy(wv[:, o, :], wrow[:, 3 * o + 2, :]).then_inc(wr, 1)
                else:
                    for a in range(6):
                        dve.wait_ge(tp, a + 1)
                        src = c.bank[a][0:DH, 0:D].rearrange("p (o n) -> p o n", o=2)
                        z, half = divmod(a, 2)
                        if z == 2:
                            ins = dve.tensor_copy(wv[:, :, half * DH:(half + 1) * DH], src)
                        else:
                            dst = wqk[:, :, z, half * 192:(half + 1) * 192].rearrange("p o (h e) -> p o h e", e=32)
                            ins = dve.tensor_copy(dst[:, :, :, 0:HD], src.rearrange("p o (h e) -> p o h e", e=HD))
                        ins.then_inc(wr, 1)
                copy_out(dve, dve.tensor_copy, 0)

            @block.scalar
            def _(act):
                copy_out(act, act.copy, 1)


def attention(c, name, qT, kT, v):
    nc = c.nc
    NK = len(KT)
    scale = HD ** -0.5
    with ExitStack() as ctx:
        p = c.sb(ctx, name + "_p", [128, 2, T])
        pT = c.sb(ctx, name + "_pT", [128, 2, NK, TT])
        mx = c.sb(ctx, name + "_max", [128, 2, 1])
        nm = c.sb(ctx, name + "_negmax", [128, 2, 1])
        rc = c.sb(ctx, name + "_recip", [128, HEADS])
        ao = c.sb(ctx, name + "_out", [128, 2, D])
        names = ["_scores", "_max_own", "_negmax_ready", "_exp", "_p_turned", "_pT_main", "_pT_last", "_pv",
                 "_normed", "_out_turned", "_out_copied", "_rc_own"]
        scored, maxed, neg, expd, turned, pt_v, pt_s, pv, normed, ot, oc, rown = (c.sem(name + x) for x in names)
        groups = [(b, k) for b in range(BATCH) for k in range(NK)]
        jobs = [(g, b, k, h) for g, (b, k) in enumerate(groups) for h in range(HEADS)]
        LASTC = 600
        with nc.Block() as block:
            @block.tensor
            def _(pe):
                def scores(n):
                    g, b, k, h = jobs[n]
                    q0, qn = KT[k]
                    r = 32 * (h % 4)
                    if n >= 2:
                        pe.wait_ge(pt_s, n - 1)
                    q = qT[r:r + HD, h // 4, b * T + q0:b * T + q0 + qn]
                    pe.matmul(c.pair[n % 2][0:qn, 0:512], q, kT[r:r + HD, h // 4, b * T:b * T + 512],
                              start=True, stop=True)
                    pe.matmul(c.pair[n % 2][0:qn, 512:T], q, kT[r:r + HD, h // 4, b * T + 512:(b + 1) * T],
                              start=True, stop=True).then_inc(scored, 1)

                def turn(n):
                    g, b, k, h = jobs[n]
                    qn = KT[k][1]
                    pe.wait_ge(expd, n + 1)
                    if n >= 2:
                        pe.wait_ge(pt_v, n - 1)
                    for j, (k0, kn) in enumerate(KT):
                        out = (c.bank[4 + n % 2][0:kn, j * TT:j * TT + qn] if j < NK - 1 else
                               c.pair[n % 2][0:kn, LASTC:LASTC + qn])
                        ins = pe.transpose(out, p[0:qn, n % 2, k0:k0 + kn], c.const("ident", qn)[:, 0:qn])
                    ins.then_inc(turned, 1)

                def values(n):
                    g, b, k, h = jobs[n]
                    qn = KT[k][1]
                    pe.wait_ge(pt_v, n + 1)
                    pe.wait_ge(pt_s, n + 1)
                    if h == 0 and g:
                        pe.wait_ge(normed, g)
                    for j, (k0, kn) in enumerate(KT):
                        ins = pe.matmul(c.bank[6][0:qn, h * (HD + 1):(h + 1) * (HD + 1)],
                                        pT[0:kn, n % 2, j, 0:qn], v[0:kn, b, j, h, :],
                                        start=(j == 0), stop=(j == NK - 1))
                    ins.then_inc(pv, 1)

                def turn_out(g):
                    qn = KT[groups[g][1]][1]
                    pe.wait_ge(normed, g + 1)
                    if g:
                        pe.wait_ge(oc, g)
                    for o in range(2):
                        ins = pe.transpose(c.bank[7][0:DH, o * TT:o * TT + qn], ao[0:qn, g % 2, o * DH:(o + 1) * DH],
                                           c.const("ident", qn)[:, 0:qn])
                    ins.then_inc(ot, 1)

                scores(0)
                for n in range(len(jobs) + 1):
                    if n + 1 < len(jobs):
                        scores(n + 1)
                    if n < len(jobs):
                        turn(n)
                    if n:
                        values(n - 1)
                    if n >= HEADS + 2 and (n - 2) % HEADS == 0:
                        turn_out((n - 2) // HEADS - 1)
                turn_out(len(groups) - 1)

            @block.vector
            def _(dve):
                def finish(g):
                    qn = KT[groups[g][1]][1]
                    dve.wait_ge(pv, HEADS * (g + 1))
                    if g >= 2:
                        dve.wait_ge(ot, g - 1)
                    o = c.bank[6][0:qn, 0:HEADS * (HD + 1)].rearrange("p (h e) -> p h e", e=HD + 1)
                    dve.reciprocal(rc[0:qn, :], o[:, :, HD]).then_inc(rown, 1)
                    dve.wait_ge(rown, g + 1)
                    dve.tensor_tensor(ao[0:qn, g % 2, :].rearrange("p (h e) -> p h e", e=HD), o[:, :, 0:HD],
                                      rc[0:qn, :].unsqueeze(2).broadcast_to((qn, HEADS, HD)), ALU.mult
                                      ).then_inc(normed, 1)

                def copy_turned(n):
                    g, b, k, h = jobs[n]
                    qn = KT[k][1]
                    dve.wait_ge(turned, n + 1)
                    if n >= 2:
                        dve.wait_ge(pv, n - 1)
                    src = c.bank[4 + n % 2][0:TT, 0:(NK - 1) * TT].rearrange("p (a b) -> p a b", b=TT)
                    dve.tensor_copy(pT[0:TT, n % 2, 0:NK - 1, 0:qn], src[:, :, 0:qn]).then_inc(pt_v, 1)

                for n, (g, b, k, h) in enumerate(jobs):
                    qn = KT[k][1]
                    dve.wait_ge(scored, n + 1)
                    dve.reduce_max(mx[0:qn, n % 2, :], c.pair[n % 2][0:qn, 0:T], X).then_inc(maxed, 1)
                    dve.wait_ge(maxed, n + 1)
                    if n >= 2:
                        dve.wait_ge(expd, n - 1)
                    dve.tensor_scalar(nm[0:qn, n % 2, :], mx[0:qn, n % 2, :], -scale, None, ALU.mult).then_inc(neg, 1)
                    if n:
                        copy_turned(n - 1)
                    if n >= HEADS + 1 and (n - 1) % HEADS == 0:
                        finish((n - 1) // HEADS - 1)
                copy_turned(len(jobs) - 1)
                finish(len(groups) - 1)

            @block.scalar
            def _(act):
                def last_turned(n):
                    g, b, k, h = jobs[n]
                    qn, kn = KT[k][1], KT[NK - 1][1]
                    act.wait_ge(turned, n + 1)
                    if n >= 2:
                        act.wait_ge(pv, n - 1)
                    act.copy(pT[0:kn, n % 2, NK - 1, 0:qn], c.pair[n % 2][0:kn, LASTC:LASTC + qn]).then_inc(pt_s, 1)

                def out_copy(g):
                    b, k = groups[g]
                    q0, qn = KT[k]
                    act.wait_ge(ot, g + 1)
                    act.copy(c.xT[:, :, b * T + q0:b * T + q0 + qn],
                             c.bank[7][0:DH, 0:2 * TT].rearrange("p (o n) -> p o n", o=2)[:, :, 0:qn]).then_inc(oc, 1)

                for n, (g, b, k, h) in enumerate(jobs):
                    qn = KT[k][1]
                    act.wait_ge(neg, n + 1)
                    act.activation(p[0:qn, n % 2, :], c.pair[n % 2][0:qn, 0:T], ACT.Exp, bias=nm[0:qn, n % 2, :],
                                   scale=scale).then_inc(expd, 1)
                    if n:
                        last_turned(n - 1)
                    if n >= HEADS + 3 and (n - 3) % HEADS == 0:
                        out_copy((n - 3) // HEADS - 1)
                last_turned(len(jobs) - 1)
                out_copy(len(groups) - 1)


def ff0(c):
    i = c.ins
    mlps(c, "ff0", [dict(w1=i["L0_attn_ff_w1"], b1=i["L0_attn_ff_b1"], w2=i["L0_attn_ff_w2"], b2=i["L0_attn_ff_b2"],
                         parts=[(0, DH), (1, DH)], n=D, gain=None, chunks=range(NCH))],
         ACT.Gelu_apprx_tanh)


def attention_layer(c, name, w, bias):
    with ExitStack() as ctx:
        qT = c.sb(ctx, name + "_qT", [128, 3, NT])
        kT = c.sb(ctx, name + "_kT", [128, 3, NT])
        v = c.sb(ctx, name + "_v", [128, BATCH, len(KT), HEADS, HD + 1])
        qkv(c, name + "_qkv", w, bias, qT, kT, v)
        attention(c, name, qT, kT, v)


def out_proj0(c):
    nc = c.nc
    with ExitStack() as ctx:
        row = c.sb(ctx, "outp_rows", [DH, 2, D])
        w = c.sb(ctx, "outp_w", [DH, 2, D])
        w_in, tp, placed = c.sem("outp_in"), c.sem("outp_turned"), c.sem("outp_placed")
        with nc.Block() as block:
            @block.sync
            def _(sp):
                sp.dma_start(row[:, :, :], c.ins["L0_ffn_out_proj_w"].rearrange("(a p) n -> p a n", p=DH)
                             ).then_inc(w_in, 16)

            turn_weights(c, block, w_in, 16, tp, placed, row, w, None)
        bias = c.sb(ctx, "outp_b", [1, D])
        to_tokens(c, "outp", [(bias[:, :], c.ins["L0_ffn_out_proj_b"].rearrange("(a n) -> a n", a=1))],
                  lambda i: [(c.xT[:, o, :], w[:, o, :]) for o in range(2)], lambda i: bias[:, :])


def turn_weights(c, block, w_in, w_count, tp, placed, row, w, bank0):
    b = bank0 or 0

    @block.tensor
    def _(pe):
        pe.wait_ge(w_in, w_count)
        for a in range(2):
            for o in range(2):
                ins = pe.transpose(c.bank[b + o][0:DH, a * DH:(a + 1) * DH], row[:, a, o * DH:(o + 1) * DH],
                                   c.const("ident", DH)[:, 0:DH])
        ins.then_inc(tp, 1)

    @block.vector
    def _(dve):
        dve.wait_ge(tp, 1)
        for o in range(2):
            dve.tensor_copy(w[:, o, :], c.bank[b + o][0:DH, 0:D]).then_inc(placed, 1)


def route(c, comb):
    nc = c.nc
    E = EXPERTS
    with ExitStack() as ctx:
        row = c.sb(ctx, "router_rows", [E, D])
        w = c.sb(ctx, "router_w", [DH, 2, E])
        rb = c.sb(ctx, "router_b", [1, E])
        lg = c.sb(ctx, "router_logits", [128, NTILE, E])
        pr = c.sb(ctx, "router_probs", [128, NTILE, E])
        top = c.sb(ctx, "top_one", [128, NTILE, E])
        tie = c.sb(ctx, "top_rank", [128, NTILE, E])
        m = c.sb(ctx, "router_max", [128, 4, NTILE])
        w_in, tp, placed, done = c.sem("router_in"), c.sem("router_turned"), c.sem("router_placed"), c.sem("logits")
        own_s, shifted, exped = c.sem("route_own"), c.sem("logits_shifted"), c.sem("router_exp")
        with nc.Block() as block:
            @block.sync
            def _(sp):
                sp.dma_start(row[:, :], c.ins["L0_ffn_router_w"]).then_inc(w_in, 16)
                sp.dma_start(rb[:, :], c.ins["L0_ffn_router_b"].rearrange("(a n) -> a n", a=1)).then_inc(w_in, 16)

            @block.tensor
            def _(pe):
                pe.wait_ge(w_in, 32)
                for o in range(2):
                    ins = pe.transpose(c.bank[1][0:DH, o * E:(o + 1) * E], row[:, o * DH:(o + 1) * DH],
                                       c.const("ident", E)[:, 0:E])
                ins.then_inc(tp, 1)
                pe.wait_ge(placed, 1)
                for i in range(NTILE):
                    ps = c.bank[0][0:TT, i * E:(i + 1) * E]
                    pe.matmul(ps, c.ones[0:1, 0:TT], rb[:, :], start=True, stop=False)
                    for o in range(2):
                        ins = pe.matmul(ps, c.xT[:, o, i * TT:(i + 1) * TT], w[:, o, :], start=False, stop=(o == 1))
                ins.then_inc(done, 1)

            @block.scalar
            def _(act):
                act.wait_ge(shifted, 1)
                act.activation(pr[0:TT, :, :], lg[0:TT, :, :], ACT.Exp).then_inc(exped, 1)

            @block.vector
            def _(dve):
                own = Own(dve, own_s)

                def wide(ap):
                    return ap.unsqueeze(2).broadcast_to((TT, NTILE, E))

                def tt(out, a, b, op):
                    own.did(dve.tensor_tensor(out, a, b, op))
                    own.wait()

                def largest(out, a):
                    own.did(dve.tensor_reduce(out, a, X, ALU.max))
                    own.wait()

                P, L_, R, TOP = pr[0:TT], lg[0:TT], tie[0:TT], top[0:TT]
                m1, m2, mr, sm = (m[0:TT, k, :] for k in range(4))
                rank = c.const("rank", TT).unsqueeze(1).broadcast_to((TT, NTILE, E))
                dve.wait_ge(tp, 1)
                dve.tensor_copy(w[:, :, :].rearrange("p o e -> p (o e)"), c.bank[1][0:DH, 0:2 * E]).then_inc(placed, 1)
                dve.wait_ge(done, 1)
                own.did(dve.tensor_copy(L_.rearrange("p a b -> p (a b)"), c.bank[0][0:TT, 0:NTILE * E]))
                own.wait()
                largest(m1, L_)
                dve.tensor_tensor(L_, L_, wide(m1), ALU.subtract).then_inc(shifted, 1)
                dve.wait_ge(exped, 1)
                own.did(dve.tensor_reduce(sm, P, X, ALU.add))
                own.wait()
                own.did(dve.reciprocal(sm, sm))
                own.wait()
                tt(P, P, wide(sm), ALU.mult)

                def pick(values, best, one):
                    largest(best, values)
                    tt(R, values, wide(best), ALU.is_equal)
                    tt(R, R, rank, ALU.mult)
                    largest(mr, R)
                    tt(one, R, wide(mr), ALU.is_equal)

                pick(P, m1, TOP)
                own.did(dve.scalar_tensor_tensor(L_, TOP, -2.0, P, ALU.mult, ALU.add))
                own.wait()
                C = comb[0:TT]
                pick(L_, m2, C)
                tt(C, C, TOP, ALU.add)
                tt(C, C, P, ALU.mult)
                tt(sm, m1, m2, ALU.add)
                own.did(dve.reciprocal(sm, sm))
                own.wait()
                tt(C, C, wide(sm), ALU.mult)


def moe(c):
    i = c.ins
    with ExitStack() as ctx:
        comb = c.sb(ctx, "combine", [128, NTILE, EXPERTS])
        route(c, comb)
        mlps(c, "moe", [dict(w1=i["L0_ffn_w1"][e], b1=i["L0_ffn_b1"][e], w2=i["L0_ffn_w2"][e], b2=i["L0_ffn_b2"][e],
                             parts=[(0, DH), (1, DH)], n=D, gain=lambda t, e=e: comb[0:TT, t, e:e + 1],
                             chunks=range(NCH)) for e in range(EXPERTS)], ACT.Gelu)


def spiking(c):
    nc = c.nc
    NK, S3 = len(KT), T // 3
    with ExitStack() as ctx:
        wT = c.sb(ctx, "sp_wT", [DH, 4, 2, D])
        crow = c.sb(ctx, "sp_crow", [1, 4 * D])
        qs = c.sb(ctx, "q_spikes", [DH, 2, NT], F16)
        ks = c.sb(ctx, "k_spikes", [128, BATCH, NK, D], F16)
        vs = c.sb(ctx, "v_spikes", [128, BATCH, NK, D], F16)
        kv = c.sb(ctx, "kv_counts", [DH, BATCH, 2, DH], F16)
        x3 = c.sb(ctx, "xa_spikes", [DH, 2, NT])
        with ExitStack() as early:
            wr = c.sb(early, "sp_rows", [DH, 4, 2, D])
            pc = c.sb(early, "sp_cols", [DH, 4, 4, 2])
            pr = c.sb(early, "sp_prow", [1, 7, 4 * D])
            w_in, var_r, sq_r, own_s = c.sem("sp_in"), c.sem("sp_var"), c.sem("sp_sqrt"), c.sem("sp_own")
            scaled, tp, placed = c.sem("sp_scaled"), c.sem("sp_turned"), c.sem("sp_placed")
            with nc.Block() as block:
                @block.sync
                def _(sp):
                    for w in range(4):
                        sp.dma_start(wr[:, w, :, :], c.ins["L1_attn_W"][w].rearrange("(a p) n -> p a n", p=DH)
                                     ).then_inc(w_in, 16)
                        for k, n in enumerate(("bn_gamma", "bn_var")):
                            sp.dma_start(pc[:, k, w, :], c.ins["L1_attn_" + n][w].rearrange("(a p) -> p a", p=DH),
                                         allow_slow_non_contiguous=True).then_inc(w_in, 16)
                    for k, n in enumerate(("b", "bn_gamma", "bn_beta", "bn_mean", "bn_var")):
                        sp.dma_start(pr[:, k, :], c.ins["L1_attn_" + n].rearrange("w n -> (w n)").rearrange(
                            "(a n) -> a n", a=1)).then_inc(w_in, 16)

                @block.scalar
                def _(act):
                    act.wait_ge(var_r, 2)
                    act.activation(pc[:, 2, :, :], pc[:, 1, :, :], ACT.Sqrt).then_inc(sq_r, 1)
                    act.activation(pr[:, 5, :], pr[:, 4, :], ACT.Sqrt).then_inc(sq_r, 1)

                @block.vector
                def _(dve):
                    own = Own(dve, own_s)
                    dve.wait_ge(w_in, 16 * 17)
                    dve.tensor_scalar(pc[:, 1, :, :], pc[:, 1, :, :], 1e-5, None, ALU.add).then_inc(var_r, 1)
                    dve.tensor_scalar(pr[:, 4, :], pr[:, 4, :], 1e-5, None, ALU.add).then_inc(var_r, 1)
                    dve.wait_ge(sq_r, 2)
                    own.did(dve.reciprocal(pc[:, 3, :, :], pc[:, 2, :, :]))
                    own.did(dve.reciprocal(pr[:, 6, :], pr[:, 5, :]))
                    own.wait()
                    own.did(dve.tensor_tensor(pc[:, 3, :, :], pc[:, 3, :, :], pc[:, 0, :, :], ALU.mult))
                    own.did(dve.tensor_tensor(pr[:, 6, :], pr[:, 6, :], pr[:, 1, :], ALU.mult))
                    own.did(dve.tensor_tensor(pr[:, 0, :], pr[:, 0, :], pr[:, 3, :], ALU.subtract))
                    own.wait()
                    own.did(dve.tensor_tensor(pr[:, 0, :], pr[:, 0, :], pr[:, 6, :], ALU.mult))
                    own.wait()
                    own.did(dve.tensor_tensor(crow[:, :], pr[:, 0, :], pr[:, 2, :], ALU.add))
                    for w in range(4):
                        for a in range(2):
                            dve.tensor_scalar(wr[:, w, a, :], wr[:, w, a, :], pc[:, 3, w, a:a + 1], None, ALU.mult
                                              ).then_inc(scaled, 1)
                    for n in range(8):
                        w, o = divmod(n, 2)
                        dve.wait_ge(tp, n + 1)
                        dve.tensor_copy(wT[:, w, o, :], c.bank[n][0:DH, 0:D]).then_inc(placed, 1)

                @block.tensor
                def _(pe):
                    pe.wait_ge(scaled, 8)
                    for n in range(8):
                        w, o = divmod(n, 2)
                        for a in range(2):
                            ins = pe.transpose(c.bank[n][0:DH, a * DH:(a + 1) * DH], wr[:, w, a, o * DH:(o + 1) * DH],
                                               c.const("ident", DH)[:, 0:DH])
                        ins.then_inc(tp, 1)
        kjobs = [("kv", w, b, k) for w in (1, 2) for b in range(BATCH) for k in range(NK)]
        qjobs = [("q", m, ch, 0) for m in range(2) for ch in range(NCH)]
        cjobs = [("count", b, m, 0) for b in range(BATCH) for m in range(2)]
        xjobs = [("x", b, m, s) for b in range(BATCH) for m in range(2) for s in range(3)]
        jobs = kjobs + qjobs + cjobs + xjobs
        done, spiked = c.sem("sp_done"), c.sem("sp_spiked")
        with nc.Block() as block:
            @block.tensor
            def _(pe):
                for n, (kind, a, b, k) in enumerate(jobs):
                    if n >= 8:
                        pe.wait_ge(spiked, n - 7)
                    bank = c.bank[n % 8]
                    if kind == "kv":
                        k0, kn = KT[k]
                        ps = bank[0:kn, 0:D]
                        pe.matmul(ps, c.ones[0:1, 0:kn], crow[:, a * D:(a + 1) * D], start=True, stop=False)
                        for o in range(2):
                            ins = pe.matmul(ps, c.xT[:, o, b * T + k0:b * T + k0 + kn], wT[:, a, o, :],
                                            start=False, stop=(o == 1))
                    elif kind == "q":
                        ps = bank[0:DH, 0:CW]
                        pe.matmul(ps, crow[:, a * DH:(a + 1) * DH], c.ones[0:1, 0:CW], start=True, stop=False)
                        for o in range(2):
                            ins = pe.matmul(ps, wT[:, 0, o, a * DH:(a + 1) * DH], c.xT[:, o, b * CW:(b + 1) * CW],
                                            start=False, stop=(o == 1))
                    elif kind == "count":
                        if n == len(kjobs) + len(qjobs):
                            pe.wait_ge(spiked, n)
                        for j, (k0, kn) in enumerate(KT):
                            ins = pe.matmul(bank[0:DH, 0:DH], ks[0:kn, a, j, b * DH:(b + 1) * DH],
                                            vs[0:kn, a, j, b * DH:(b + 1) * DH], start=(j == 0), stop=(j == NK - 1))
                    else:
                        if n == len(jobs) - len(xjobs):
                            pe.wait_ge(spiked, n)
                        at = a * T + k * S3
                        ins = pe.matmul(bank[0:DH, 0:S3], kv[:, a, b, :], qs[:, b, at:at + S3], start=True, stop=True)
                    ins.then_inc(done, 1)

            @block.vector
            def _(dve):
                for n, (kind, a, b, k) in enumerate(jobs):
                    dve.wait_ge(done, n + 1)
                    bank = c.bank[n % 8]
                    if kind == "kv":
                        kn = KT[k][1]
                        ins = dve.tensor_scalar((ks, vs)[a - 1][0:kn, b, k, :], bank[0:kn, 0:D], 2.0, None, ALU.is_ge)
                    elif kind == "q":
                        ins = dve.tensor_scalar(qs[:, a, b * CW:(b + 1) * CW], bank[0:DH, 0:CW], 2.0, None, ALU.is_ge)
                    elif kind == "count":
                        ins = dve.tensor_tensor(kv[:, a, b, :], bank[0:DH, 0:DH], c.const("kv", DH), ALU.mult)
                    else:
                        at = a * T + k * S3
                        ins = dve.tensor_scalar(x3[:, b, at:at + S3], bank[0:DH, 0:S3], HD ** -0.125, 1.0,
                                                ALU.mult, ALU.is_ge)
                    ins.then_inc(spiked, 1)
        to_tokens(c, "sp_out", [], lambda i: [(x3[:, o, :], wT[:, 3, o, :]) for o in range(2)],
                  lambda i: crow[:, 3 * D:4 * D], into=c.hN, spike=2.0)


WIDTHS = (D, D // 2, D // 3)


def small_proj(c, g):
    nc = c.nc
    with ExitStack() as ctx:
        w = c.sb(ctx, "proj_w", [DH, 2, 2, D])
        b = c.sb(ctx, "proj_b", [1, 2, D])
        w_in, own_s = c.sem("proj_in"), c.sem("proj_own")
        with nc.Block() as block:
            @block.sync
            def _(sp):
                sp.dma_start(w[:, 0, :, :], c.ins["L1_ffn_w_proj"].rearrange("(o p) n -> p o n", p=DH)).then_inc(w_in, 16)
                sp.dma_start(b[:, 0, :], c.ins["L1_ffn_b_proj"].rearrange("(a n) -> a n", a=1)).then_inc(w_in, 16)

            @block.vector
            def _(dve):
                own = Own(dve, own_s)
                dve.wait_ge(w_in, 32)
                own.did(dve.tensor_scalar(w[:, 1, :, :], w[:, 0, :, :], g[0:DH, 0:1], None, ALU.mult))
                own.did(dve.tensor_scalar(b[:, 1, :], b[:, 0, :], g[0:1, 0:1], None, ALU.mult))
                for i in (1, 2):
                    n = WIDTHS[i]
                    own.wait()
                    own.did(dve.scalar_tensor_tensor(w[0:n, 1, 0, 0:n], w[0:n, 0, 0, 0:n], g[0:n, i:i + 1],
                                                     w[0:n, 1, 0, 0:n], ALU.mult, ALU.add))
                    own.did(dve.scalar_tensor_tensor(b[:, 1, 0:n], b[:, 0, 0:n], g[0:1, i:i + 1],
                                                     b[:, 1, 0:n], ALU.mult, ALU.add))
        half = NTILE // 2
        to_tokens(c, "proj", [], lambda i: [(c.xT[:, o, :], w[:, i // half, o, :]) for o in range(2)],
                  lambda i: b[:, i // half, :])


def last_mlps(c, g):
    i = c.ins
    w = dict(w1=i["L1_ffn_w_fc1"], b1=i["L1_ffn_b_fc1"], w2=i["L1_ffn_w_fc2"], b2=i["L1_ffn_b_fc2"])
    parts = [[(0, DH), (1, DH)], [(0, WIDTHS[1])], [(0, WIDTHS[2])]]
    variants = [dict(w, parts=parts[0], n=D, gain=None, chunks=range(NCH // 2))]
    for k in range(3):
        variants.append(dict(w, parts=parts[k], n=WIDTHS[k], gain=lambda t, k=k: g[0:TT, k:k + 1],
                             chunks=range(NCH // 2, NCH)))
    mlps(c, "last", variants, ACT.Gelu)


def write_out(c, out):
    nc = c.nc
    summed, stored = c.sem("out_summed"), c.stored
    with nc.Block() as block:
        @block.vector
        def _(dve):
            for k in range(3):
                s = slice(6 * k, 6 * k + 6)
                dve.tensor_tensor(c.hN[0:TT, s, :], c.hN[0:TT, s, :], c.xN[0:TT, s, :], ALU.add).then_inc(summed, 1)

        @block.sync
        def _(sp):
            view = out.rearrange("b t d -> (b t) d").rearrange("(i p) d -> p i d", p=TT)
            for k in range(3):
                s = slice(6 * k, 6 * k + 6)
                sp.wait_ge(summed, k + 1)
                sp.dma_start(view[:, s, :], c.hN[0:TT, s, :]).then_inc(stored, 16)
            sp.wait_ge(stored, 48)


def last_ffn(c, ctx):
    nc = c.nc
    g = c.sb(ctx, "gumbel", [128, 3])
    g_in = c.sem("gumbel_in")
    with nc.Block() as block:
        @block.sync
        def _(sp):
            sp.dma_start(g[:, :], c.ins["L1_ffn_gumbel_weights"].rearrange("(a n) -> a n", a=1).broadcast_to((128, 3))
                         ).then_inc(g_in, 16)
            sp.wait_ge(g_in, 16)
    norm(c, "n1", True, "ln", ["L1_ffn_n1l_g", "L1_ffn_n1s_g"], ["L1_ffn_n1l_b", "L1_ffn_n1s_b"])
    attention_layer(c, "att1", c.ins["L1_ffn_w_qkv"], None)
    small_proj(c, g)
    norm(c, "n2", False, "ln", ["L1_ffn_n2l_g", "L1_ffn_n2s_g"], ["L1_ffn_n2l_b", "L1_ffn_n2s_b"])
    last_mlps(c, g)


def tower(nc, ins, out):
    with ExitStack() as ctx:
        c = Core(nc, ins)
        load_shared(c, ctx)
        tok_features(c)
        layer_buffers(c, ctx)
        norm(c, "mixn", True, "rms", ["L0_attn_norm1_w"])
        mixer(c)
        c.layer_end()
        norm(c, "ff0n", False, "rms", ["L0_attn_norm2_w"])
        ff0(c)
        norm(c, "att0n", True, "ln", ["L0_ffn_ln1_g"], ["L0_ffn_ln1_b"], residual=True)
        attention_layer(c, "att0", ins["L0_ffn_in_proj_w"], ins["L0_ffn_in_proj_b"])
        out_proj0(c)
        c.layer_end()
        norm(c, "moen", False, "ln", ["L0_ffn_ln2_g"], ["L0_ffn_ln2_b"])
        moe(c)
        c.layer_end()
        norm(c, "spn", True, None, None, residual=True)
        spiking(c)
        c.layer_end()
        last_ffn(c, ctx)
        write_out(c, out)


_INS = ['x', 'cls_tok', 'L0_tok_freq_bands', 'L0_tok_W', 'L0_attn_norm1_w', 'L0_attn_w_in', 'L0_attn_conv_w',
        'L0_attn_w_bc', 'L0_attn_D_skip', 'L0_attn_w_out', 'L0_attn_norm2_w', 'L0_attn_ff_w1', 'L0_attn_ff_b1',
        'L0_attn_ff_w2', 'L0_attn_ff_b2', 'L0_ffn_ln1_g', 'L0_ffn_ln1_b', 'L0_ffn_in_proj_w', 'L0_ffn_in_proj_b',
        'L0_ffn_out_proj_w', 'L0_ffn_out_proj_b', 'L0_ffn_ln2_g', 'L0_ffn_ln2_b', 'L0_ffn_router_w',
        'L0_ffn_router_b', 'L0_ffn_w1', 'L0_ffn_b1', 'L0_ffn_w2', 'L0_ffn_b2', 'L1_attn_W', 'L1_attn_b',
        'L1_attn_bn_gamma', 'L1_attn_bn_beta', 'L1_attn_bn_mean', 'L1_attn_bn_var', 'L1_ffn_gumbel_weights',
        'L1_ffn_n1l_g', 'L1_ffn_n1l_b', 'L1_ffn_n1s_g', 'L1_ffn_n1s_b', 'L1_ffn_w_qkv', 'L1_ffn_w_proj',
        'L1_ffn_b_proj', 'L1_ffn_n2l_g', 'L1_ffn_n2l_b', 'L1_ffn_n2s_g', 'L1_ffn_n2s_b', 'L1_ffn_w_fc1',
        'L1_ffn_b_fc1', 'L1_ffn_w_fc2', 'L1_ffn_b_fc2']


def kernel(**inputs):
    import numpy as _np
    import concourse.bacc as _bacc
    from concourse import mybir as _mybir
    from concourse.bass_utils import run_bass_kernel_spmd as _run

    nc = _bacc.Bacc("TRN2", target_bir_lowering=False, num_devices=1)
    arrays, ins = {}, {}
    for name in _INS + ["consts"]:
        a = CONSTANTS if name == "consts" else _np.ascontiguousarray(inputs[name])
        arrays[f"in_{name}_dram"] = a
        ins[name] = nc.dram_tensor(f"in_{name}_dram", a.shape, _mybir.dt.from_np(a.dtype), kind="ExternalInput").ap()
    out = nc.dram_tensor("out_0_dram", (BATCH, T, D), F32, kind="ExternalOutput").ap()
    tower(nc, ins, out)
    r = _run(nc, [arrays], core_ids=[0])
    return r.results[0]["out_0_dram"]
```

```python
from contextlib import ExitStack

import numpy as np

import concourse.bass as bass
from concourse import mybir

ALU = mybir.AluOpType
ACT = mybir.ActivationFunctionType
F32 = mybir.dt.float32
F16 = mybir.dt.float16
X = mybir.AxisListType.X

BATCH, SEQ, D = 4, 512, 192
T = SEQ + 1
NT = BATCH * T
TT = 114
NTILE = NT // TT
CW = 3 * TT
NCH = NT // CW
DH = D // 2
NW = SEQ * 3 * D * BATCH // (BATCH * SEQ)
NB2 = 12
HEADS, HD = 12, 16
FF = 4 * D
NF = FF // 128
EXPERTS = 8
DIN, SH, ST, SP = 384, 6, 8, 64
L = 57
NC1 = T // L
NBC = NT // L
LANES = NBC * SH // 2
KT = [(k * TT, min(TT, T - k * TT)) for k in range((T + TT - 1) // TT)]
MAGIC = 12582912.0
TWO_PI = 6.283185
HALF_PI = 1.5707963

CONST = {}


def _constants():
    p = np.arange(128)
    parts = [("ident", np.eye(128))]
    row_h, row_z, row_n = p // 16, (p // 8) % 2, p % 8
    parts.append(("bd", (row_h[:, None] == (np.arange(DIN) // SP)[None]) & (p < 96)[:, None]))
    q = np.arange(96)
    swap = np.zeros((128, 96))
    swap[q, (q // 16) * 16 + (1 - (q // 8) % 2) * 8 + q % 8] = 1
    parts.append(("swap", swap))
    parts.append(("h48", (p // 8)[:, None] == np.arange(SH)[None]))
    for z in range(2):
        parts.append((f"sel{z}", ((p % SH)[:, None] == (q // 16)[None]) & (((q // 8) % 2) == z)[None]))
    parts.append(("bc", (p // SH)[:, None] == np.arange(NBC // 2)[None]))
    parts.append(("kv", (p // HD)[:, None] == (q // HD)[None]))
    parts.append(("rank", np.broadcast_to(EXPERTS - np.arange(EXPERTS), (128, EXPERTS))))
    at, cols = 0, []
    for name, a in parts:
        CONST[name] = (at, a.shape[1])
        at += a.shape[1]
        cols.append(np.asarray(a, np.float32))
    return np.ascontiguousarray(np.concatenate(cols, 1))


CONSTANTS = _constants()


class Own:

    def __init__(self, eng, sem):
        self.eng, self.sem, self.n = eng, sem, 0

    def did(self, ins):
        self.n += 1
        ins.then_inc(self.sem, 1)
        return ins

    def wait(self, but=0):
        if self.n > but:
            self.eng.wait_ge(self.sem, self.n - but)


class Core:

    def __init__(self, nc, ins):
        self.nc, self.ins, self.sems = nc, ins, []
        self.stored = nc.alloc_semaphore("out_stored")
        self.pair = [nc.alloc_psum_tensor(f"banks{2 * i}{2 * i + 1}", [128, 1024], F32) for i in range(4)]
        self.bank = [self.pair[i // 2][:, i % 2 * 512:(i % 2 + 1) * 512] for i in range(8)]

    def sem(self, name):
        self.sems.append(self.nc.alloc_semaphore(name))
        return self.sems[-1]

    def layer_end(self):
        self.nc.all_engine_barrier()
        self.nc.clear_and_free_semaphores(self.sems)
        self.nc.all_engine_barrier()
        self.sems = []

    def sb(self, ctx, name, shape, dt=F32):
        return ctx.enter_context(self.nc.sbuf_tensor(name, shape, dt))

    def const(self, name, rows=128):
        at, n = CONST[name]
        return self.consts[0:rows, at:at + n]


def bc(ap, shape):
    return ap.broadcast_to(shape)


def load_shared(c, out_ctx):
    nc = c.nc
    c.consts = c.sb(out_ctx, "consts", [128, CONSTANTS.shape[1]])
    c.ones = c.sb(out_ctx, "ones", [128, 512])
    c.hN = c.sb(out_ctx, "hN", [128, NTILE, D])
    loaded, ones_set = c.sem("consts_loaded"), c.sem("ones_set")
    with nc.Block() as block:
        @block.sync
        def _(sp):
            sp.dma_start(c.consts[:, :], c.ins["consts"]).then_inc(loaded, 16)
            sp.wait_ge(loaded, 16)

        @block.vector
        def _(dve):
            dve.memset(c.ones[:, :], 1.0).then_inc(ones_set, 1)
            dve.wait_ge(ones_set, 1)


def layer_buffers(c, ctx):
    c.xN = c.sb(ctx, "xN", [128, NTILE, D])
    c.xT = c.sb(ctx, "xT", [DH + 1, 2, NT])
    ones_row = c.sem("ones_row")
    with c.nc.Block() as block:
        @block.vector
        def _(dve):
            dve.memset(c.xT[DH:DH + 1, :, :], 1.0).then_inc(ones_row, 1)


def tok_features(c):
    nc = c.nc
    NCC = 5
    CC = [(k * 128, min(128, NW - k * 128)) for k in range(NCC)]
    HALF = NT // 2
    with ExitStack() as ctx:
        wT = c.sb(ctx, "tok_wT", [128, NCC, NB2, D])
        rT = c.sb(ctx, "raw_T", [128, NCC, NT])
        freq = c.sb(ctx, "freq", [128, 6])
        with ExitStack() as early:
            w = c.sb(early, "tok_w", [DH, 2, NW * NB2])
            raw = c.sb(early, "raw", [128, 4, 4, NW])
            w_in, raw_in, f_in = c.sem("tok_w_in"), c.sem("raw_in"), c.sem("freq_in")
            tp, ev = c.sem("tok_transposed"), [c.sem("tok_copied_v"), c.sem("tok_copied_s")]
            zero_set = c.sem("cls_columns_zeroed")
            jobs = []
            for i in range(BATCH):
                for k, (c0, n) in enumerate(CC):
                    jobs.append(("raw", i, k, n))
            for k, (c0, n) in enumerate(CC):
                for f in range(0, NB2, 2):
                    jobs.append(("w", k, f, n))
            with nc.Block() as block:
                @block.sync
                def _(sp):
                    for b in range(BATCH):
                        sp.dma_start(raw[:, b, :, :], c.ins["x"][b].rearrange("c n d -> (c n d)").rearrange(
                            "(i p w) -> p i w", p=128, w=NW)).then_inc(raw_in, 16)
                    for o in range(2):
                        sp.dma_start(w[:, o, :], c.ins["L0_tok_W"][o * DH:(o + 1) * DH, :]).then_inc(w_in, 16)
                    sp.dma_start(freq[:, :], c.ins["L0_tok_freq_bands"].rearrange(
                        "(a n) -> a n", a=1).broadcast_to((128, 6))).then_inc(f_in, 16)
                    sp.wait_ge(f_in, 16)

                @block.tensor
                def _(pe):
                    pe.wait_ge(raw_in, 16 * BATCH)
                    for n, (kind, a, k, m) in enumerate(jobs):
                        if n >= 8:
                            pe.wait_ge(ev[n % 2], (n - 8) // 2 + 1)
                        if kind == "raw":
                            for i in range(4):
                                c0 = CC[k][0]
                                ins = pe.transpose(c.bank[n % 8][0:m, i * 128:(i + 1) * 128],
                                                   raw[:, a, i, c0:c0 + m], c.const("ident"))
                        else:
                            if n == BATCH * NCC:
                                pe.wait_ge(w_in, 32)
                            c0 = CC[a][0]
                            for f in range(2):
                                for o in range(2):
                                    s = c0 * NB2 + k + f
                                    ins = pe.transpose(
                                        c.bank[n % 8][0:m, (f * 2 + o) * DH:(f * 2 + o + 1) * DH],
                                        w[:, o, s:s + (m - 1) * NB2 + 1:NB2], c.const("ident", DH)[:, 0:DH])
                        ins.then_inc(tp, 1)

                def copy_out(eng, copy, par):
                    for n, (kind, a, k, m) in enumerate(jobs):
                        if n % 2 != par:
                            continue
                        eng.wait_ge(tp, n + 1)
                        if kind == "raw":
                            dst = rT[0:m, k, a * T + 1:(a + 1) * T]
                            src = c.bank[n % 8][0:m, :]
                        else:
                            dst = wT[0:m, a, k:k + 2, :].rearrange("p f d -> p (f d)")
                            src = c.bank[n % 8][0:m, 0:2 * D]
                        copy(dst, src).then_inc(ev[par], 1)

                @block.vector
                def _(dve):
                    for b in range(BATCH):
                        dve.memset(rT[:, :, b * T:b * T + 1], 0.0).then_inc(zero_set, 1)
                    copy_out(dve, dve.tensor_copy, 0)

                @block.scalar
                def _(act):
                    copy_out(act, act.copy, 1)

        fy = c.sb(ctx, "angle", [128, HALF])
        fm = c.sb(ctx, "angle_rounded", [128, HALF])
        fr = c.sb(ctx, "angle_rest", [128, 2, HALF])
        fa = c.sb(ctx, "angle_abs", [128, 2, HALF])
        feat = c.sb(ctx, "features", [128, 2, 2, HALF])
        halfpi = c.sb(ctx, "half_pi", [128, 1])
        vown = c.sem("tok_v_own")
        rest, used = c.sem("angle_ready"), c.sem("angle_used")
        fready, fused = c.sem("features_ready"), c.sem("features_used")
        accd, out_v, cls_in = c.sem("tok_accumulated"), c.sem("tok_h_written"), c.sem("cls_in")
        steps = [(hf, k, f) for hf in range(2) for k in range(NCC) for f in range(6)]
        per = NCC * 6
        with nc.Block() as block:
            @block.vector
            def _(dve):
                own = Own(dve, vown)
                own.did(dve.memset(halfpi[:, :], HALF_PI))

                def write_h(hf):
                    dve.wait_ge(accd, hf + 1)
                    for t in range(9):
                        dve.tensor_copy(c.hN[0:TT, hf * 9 + t, :],
                                        c.bank[t // 2][0:TT, (t % 2) * D:(t % 2 + 1) * D]).then_inc(out_v, 1)

                for n, (hf, k, f) in enumerate(steps):
                    m, s = CC[k][1], n % 2
                    src = rT[0:m, k, hf * HALF:(hf + 1) * HALF]
                    own.did(dve.tensor_scalar(fy[0:m, :], src, freq[0:m, f:f + 1], None, ALU.mult))
                    own.wait()
                    own.did(dve.tensor_scalar(fm[0:m, :], fy[0:m, :], MAGIC, MAGIC, ALU.add, ALU.subtract))
                    own.wait()
                    if n >= 2:
                        dve.wait_ge(used, 2 * (n - 1))
                    own.did(dve.tensor_tensor(fr[0:m, s, :], fy[0:m, :], fm[0:m, :], ALU.subtract))
                    own.wait()
                    dve.scalar_tensor_tensor(fa[0:m, s, :], fr[0:m, s, :], -1.0, fr[0:m, s, :], ALU.mult, ALU.max).then_inc(rest, 1)
                    if n == per:
                        write_h(0)
                write_h(1)

            @block.scalar
            def _(act):
                for n, (hf, k, f) in enumerate(steps):
                    m, s = CC[k][1], n % 2
                    act.wait_ge(rest, n + 1)
                    if n >= 2:
                        act.wait_ge(fused, n - 1)
                    act.activation(feat[0:m, s, 0, :], fr[0:m, s, :], ACT.Sin, scale=TWO_PI).then_inc(used, 1)
                    act.activation(feat[0:m, s, 1, :], fa[0:m, s, :], ACT.Sin, bias=halfpi[0:m, :],
                                   scale=-TWO_PI).then_inc(used, 1)

            @block.tensor
            def _(pe):
                for n, (hf, k, f) in enumerate(steps):
                    m, s = CC[k][1], n % 2
                    pe.wait_ge(used, 2 * n + 2)
                    if n == per:
                        pe.wait_ge(out_v, 9)
                    for q in range(2):
                        for t in range(9):
                            ins = pe.matmul(c.bank[t // 2][0:TT, (t % 2) * D:(t % 2 + 1) * D],
                                            feat[0:m, s, q, t * TT:(t + 1) * TT], wT[0:m, k, 6 * q + f, :],
                                            start=(n % per == 0 and q == 0 and t % 2 == 0),
                                            stop=(n % per == per - 1 and q == 1), skip_group_check=True)
                    ins.then_inc(fused, 1)
                    if n % per == per - 1:
                        pe.matmul(c.bank[7][0:1, 0:1], c.ones[0:1, 0:1], c.ones[0:1, 0:1],
                                  start=True, stop=True).then_inc(accd, 1)

            @block.sync
            def _(sp):
                sp.wait_ge(out_v, 18)
                for b in range(BATCH):
                    t, r = divmod(b * T, TT)
                    sp.dma_start(c.hN[r:r + 1, t, :], c.ins["cls_tok"][0]).then_inc(cls_in, 16)
                sp.wait_ge(cls_in, 16 * BATCH)


def stats(dve, own, c, src, st, mv):
    for i in range(NTILE):
        own.did(dve.bn_stats(st[0:TT, i, :], src[0:TT, i, :]))
    own.wait()
    for i in range(NTILE):
        own.did(dve.bn_aggr(mv[0:TT, i, :], st[0:TT, i, :]))
    own.wait()


def norm(c, name, outer, kind, gains, biases=None, residual=False):
    nc = c.nc
    with ExitStack() as ctx:
        st = c.sb(ctx, name + "_st", [128, NTILE, 6])
        mv = c.sb(ctx, name + "_mv", [128, NTILE, 2])
        ve = c.sb(ctx, name + "_ve", [128, NTILE])
        sd = c.sb(ctx, name + "_sd", [128, NTILE])
        rs = c.sb(ctx, name + "_rs", [128, NTILE])
        yN = c.sb(ctx, name + "_yN", [128, NTILE, D])
        gb = c.sb(ctx, name + "_gb", [DH, 4, 2])
        own_s, gb_in = c.sem(name + "_v_own"), c.sem(name + "_gains_in")
        var_ready, sd_ready, y_ready = c.sem(name + "_var"), c.sem(name + "_sqrt"), c.sem(name + "_normed")
        tp, ev = c.sem(name + "_transposed"), [c.sem(name + "_cp_v"), c.sem(name + "_cp_s")]
        n_dma = len(gains or []) + len(biases or [])
        halves = len(gains) if gains else 1
        src = yN if kind else c.xN
        passes = int(outer) + (kind is not None)
        with nc.Block() as block:
            @block.sync
            def _(sp):
                for i, g in enumerate((gains or []) + (biases or [])):
                    at = i if i < halves else 2 + i - halves
                    sp.dma_start(gb[:, at, :], c.ins[g].rearrange("(o p) -> p o", p=DH),
                                 allow_slow_non_contiguous=True).then_inc(gb_in, 16)
                if n_dma:
                    sp.wait_ge(gb_in, 16 * n_dma)

            def copy_out(eng, par):
                if n_dma:
                    eng.wait_ge(gb_in, 16 * n_dma)
                for n in range(2 * NCH):
                    if n % 2 != par:
                        continue
                    ch, o = divmod(n, 2)
                    half = 1 if halves == 2 and ch >= NCH // 2 else 0
                    eng.wait_ge(tp, n + 1)
                    dst, ps = c.xT[0:DH, o, ch * CW:(ch + 1) * CW], c.bank[n % 8][0:DH, 0:CW]
                    g, b = gb[:, half, o:o + 1], gb[:, 2 + half, o:o + 1]
                    if par == 0:
                        if not gains:
                            ins = eng.tensor_copy(dst, ps)
                        elif biases:
                            ins = eng.tensor_scalar(dst, ps, g, b, ALU.mult, ALU.add)
                        else:
                            ins = eng.tensor_scalar(dst, ps, g, None, ALU.mult)
                    else:
                        if not gains:
                            ins = eng.activation(dst, ps, ACT.Copy)
                        elif biases:
                            ins = eng.activation(dst, ps, ACT.Identity, bias=b, scale=g)
                        else:
                            ins = eng.activation(dst, ps, ACT.Copy, scale=g)
                    ins.then_inc(ev[par], 1)

            @block.vector
            def _(dve):
                own = Own(dve, own_s)
                done = 0

                def rstd(e):
                    nonlocal done
                    dve.tensor_scalar(ve[0:TT, :], var, e, None, ALU.add).then_inc(var_ready, 1)
                    done += 1
                    dve.wait_ge(sd_ready, done)
                    own.did(dve.reciprocal(rs[0:TT, :], sd[0:TT, :]))
                    own.wait()

                if residual:
                    own.did(dve.tensor_tensor(c.hN[0:TT, :, :], c.hN[0:TT, :, :], c.xN[0:TT, :, :], ALU.add))
                    own.wait()
                if outer:
                    stats(dve, own, c, c.hN, st, mv)
                    var = mv[0:TT, :, 1]
                    rstd(1e-5)
                    for i in range(NTILE):
                        ins = dve.tensor_scalar(c.xN[0:TT, i, :], c.hN[0:TT, i, :], mv[0:TT, i, 0:1],
                                                rs[0:TT, i:i + 1], ALU.subtract, ALU.mult)
                        if kind is None:
                            ins.then_inc(y_ready, 1)
                        else:
                            own.did(ins)
                    own.wait()
                if kind:
                    stats(dve, own, c, c.xN, st, mv)
                    var = mv[0:TT, :, 1]
                    if kind == "rms":
                        own.did(dve.tensor_tensor(ve[0:TT, :], mv[0:TT, :, 0], mv[0:TT, :, 0], ALU.mult))
                        own.wait()
                        own.did(dve.tensor_tensor(mv[0:TT, :, 1], ve[0:TT, :], mv[0:TT, :, 1], ALU.add))
                        own.wait()
                    rstd(1e-6 if kind == "rms" else 1e-5)
                    for i in range(NTILE):
                        if kind == "rms":
                            ins = dve.tensor_scalar(yN[0:TT, i, :], c.xN[0:TT, i, :], rs[0:TT, i:i + 1], None,
                                                    ALU.mult)
                        else:
                            ins = dve.tensor_scalar(yN[0:TT, i, :], c.xN[0:TT, i, :], mv[0:TT, i, 0:1],
                                                    rs[0:TT, i:i + 1], ALU.subtract, ALU.mult)
                        ins.then_inc(y_ready, 1)
                copy_out(dve, 0)

            @block.scalar
            def _(act):
                for i in range(passes):
                    act.wait_ge(var_ready, i + 1)
                    act.activation(sd[0:TT, :], ve[0:TT, :], ACT.Sqrt).then_inc(sd_ready, 1)
                copy_out(act, 1)

            @block.tensor
            def _(pe):
                for n in range(2 * NCH):
                    ch, o = divmod(n, 2)
                    if n >= 8:
                        pe.wait_ge(ev[n % 2], (n - 8) // 2 + 1)
                    pe.wait_ge(y_ready, 3 * ch + 3)
                    for i in range(3):
                        ins = pe.transpose(c.bank[n % 8][0:DH, i * TT:(i + 1) * TT],
                                           src[0:TT, 3 * ch + i, o * DH:(o + 1) * DH],
                                           c.const("ident", TT)[:, 0:TT])
                    ins.then_inc(tp, 1)


def mixer(c):
    with ExitStack() as ctx:
        sg = c.sb(ctx, "gate_silu", [128, 3, NT])
        vT = c.sb(ctx, "u_T", [128, 3, NT])
        coef = c.sb(ctx, "coef", [128, 3, 2, L])
        mixer_project(c, sg, vT, coef)
        gs = c.sb(ctx, "G_s", [128, L, 2 * LANES])
        acT = c.sb(ctx, "C_start_T", [96, NT])
        bw = c.sb(ctx, "B_end", [128, NBC * SH, 2, ST])
        ab = c.sb(ctx, "start_resp", [128, 2, 2 * LANES])
        zx = c.sb(ctx, "end_resp", [128, 2 * LANES])
        de = c.sb(ctx, "end_trans", [96, 2, NBC])
        with ExitStack() as inner:
            mixer_responses(c, inner, coef, gs, ab, zx, de)
        with ExitStack() as inner:
            mixer_bc(c, inner, vT, gs, ab, zx, acT, bw)
        with ExitStack() as inner:
            mixer_chain(c, inner, sg, vT, gs, acT, bw, de)
        with ExitStack() as inner:
            w = c.sb(inner, "mix_wout", [128, 3, D])
            to_tokens(c, "mixout", [(w[:, :, :], c.ins["L0_attn_w_out"].rearrange("(k p) n -> p k n", p=128))],
                      lambda i: [(sg[:, k, :], w[:, k, :]) for k in range(3)], None)


def to_tokens(c, name, loads, terms, row, into=None, spike=None):
    nc = c.nc
    into = c.xN if into is None else into
    w_in, done, added = c.sem(name + "_w_in"), c.sem(name + "_done"), c.sem(name + "_added")
    biased = c.sem(name + "_biased")
    with nc.Block() as block:
        @block.sync
        def _(sp):
            for dst, src in loads:
                sp.dma_start(dst, src).then_inc(w_in, 16)

        @block.gpsimd
        def _(pool):
            if row is not None:
                for i in range(NTILE):
                    pool.tensor_tensor(into[0:TT, i, :], into[0:TT, i, :], row(i), ALU.add).then_inc(biased, 1)

        @block.tensor
        def _(pe):
            if loads:
                pe.wait_ge(w_in, 16 * len(loads))
            for i in range(NTILE):
                if i >= 8:
                    pe.wait_ge(added, i - 7)
                ps = c.bank[i % 8][0:TT, 0:D]
                for k, (a, w) in enumerate(terms(i)):
                    ins = pe.matmul(ps, a[:, i * TT:(i + 1) * TT], w, start=(k == 0), stop=(k == len(terms(i)) - 1))
                ins.then_inc(done, 1)

        @block.vector
        def _(dve):
            for i in range(NTILE):
                dve.wait_ge(done, i + 1)
                if row is not None:
                    dve.wait_ge(biased, i + 1)
                ps, x = c.bank[i % 8][0:TT, 0:D], into[0:TT, i, :]
                if spike is None:
                    ins = dve.tensor_tensor(x, ps, x, ALU.add)
                else:
                    ins = dve.scalar_tensor_tensor(x, ps, spike, x, ALU.is_ge, ALU.add)
                ins.then_inc(added, 1)


def mixer_project(c, sg, vT, coef):
    nc = c.nc
    PROJ = 2 * DIN + 2 * SH
    S3 = T // 3
    with ExitStack() as ctx:
        vpad = c.sb(ctx, "v_padded", [128, 3, BATCH, T + 3])
        w = c.sb(ctx, "mix_win", [DH, 2, PROJ])
        cw = c.sb(ctx, "conv_w", [128, 3, 4])
        par = c.sb(ctx, "params", [128, NBC * SH, 2])
        q3 = c.sb(ctx, "lane_values", [128, 3, NBC * SH])
        tmp = c.sb(ctx, "param_tmp", [128, 4, NBC * SH])
        w_in, cw_in = c.sem("mix_w_in"), c.sem("conv_w_in")
        proj, ev = c.sem("mix_projected"), [c.sem("mix_v_copied"), c.sem("mix_gate_done")]
        pad0, own_s, conv = c.sem("v_pad_zeroed"), c.sem("mixp_v_own"), c.sem("convolved")
        pdone, pcopy, a1, a2 = c.sem("params_done"), c.sem("params_copied"), c.sem("params_act"), c.sem("params_max")
        qs, qt, silu = c.sem("lane_ready"), c.sem("lane_transposed"), c.sem("u_done")
        jobs = [(g, m, b, s) for b in range(BATCH) for s in range(3) for m in range(3) for g in (1, 0)]
        with nc.Block() as block:
            @block.sync
            def _(sp):
                sp.dma_start(w[:, :, :], c.ins["L0_attn_w_in"].rearrange("(o p) n -> p o n", p=DH)).then_inc(w_in, 16)
                sp.dma_start(cw[:, :, :], c.ins["L0_attn_conv_w"].rearrange("(k p) t -> p k t", p=128)
                             ).then_inc(cw_in, 16)

            @block.tensor
            def _(pe):
                pe.wait_ge(w_in, 16)
                for i in range(NBC):
                    for o in range(2):
                        ins = pe.matmul(c.bank[7][0:L, i * 2 * SH:(i + 1) * 2 * SH],
                                        c.xT[0:DH, o, i * L:(i + 1) * L], w[:, o, 2 * DIN:PROJ],
                                        start=(o == 0), stop=(o == 1))
                ins.then_inc(pdone, 1)
                for n, (g, m, b, s) in enumerate(jobs):
                    if n >= 6:
                        pe.wait_ge(ev[n % 2], (n - 6) // 2 + 1)
                    for o in range(2):
                        ins = pe.matmul(c.bank[n % 6][:, 0:S3], w[:, o, g * DIN + m * 128:g * DIN + (m + 1) * 128],
                                        c.xT[0:DH, o, b * T + s * S3:b * T + (s + 1) * S3],
                                        start=(o == 0), stop=(o == 1))
                    ins.then_inc(proj, 1)
                    if n == len(jobs) // 2:
                        pe.wait_ge(qs, 1)
                        for q in range(3):
                            for g2 in range(2):
                                at = (q * 2 + g2) * L
                                ins = pe.transpose(c.bank[6][0:LANES, at:at + L],
                                                   q3[0:L, q, g2 * LANES:(g2 + 1) * LANES],
                                                   c.const("ident", L)[:, 0:L])
                        ins.then_inc(qt, 1)

            @block.scalar
            def _(act):
                act.wait_ge(a2, 1)
                act.activation(tmp[0:L, 1, :], tmp[0:L, 0, :], ACT.Exp).then_inc(a1, 1)
                act.wait_ge(a1, 1)
                act.activation(tmp[0:L, 2, :], tmp[0:L, 1, :], ACT.Ln, bias=1.0).then_inc(a1, 1)
                act.activation(q3[0:L, 0, :], par[0:L, :, 1], ACT.Sigmoid).then_inc(a1, 1)
                for n, (g, m, b, s) in enumerate(jobs):
                    if g == 0:
                        act.wait_ge(proj, n + 1)
                        act.activation(sg[:, m, b * T + s * S3:b * T + (s + 1) * S3], c.bank[n % 6][:, 0:S3],
                                       ACT.Silu).then_inc(ev[1], 1)
                for k in range(3):
                    act.wait_ge(conv, k + 1)
                    act.activation(vT[:, k, :], vT[:, k, :], ACT.Silu).then_inc(silu, 1)

            @block.vector
            def _(dve):
                own = Own(dve, own_s)
                dve.memset(vpad[:, :, :, 0:3], 0.0).then_inc(pad0, 1)
                dve.wait_ge(pdone, 1)
                own.did(dve.tensor_copy(par[0:L, :, :].rearrange("p a b -> p (a b)"), c.bank[7][0:L, 0:2 * SH * NBC]))
                own.wait()
                a, nega, lg = par[0:L, :, 0], tmp[0:L, 0, :], tmp[0:L, 2, :]
                dve.scalar_tensor_tensor(nega, a, -1.0, a, ALU.mult, ALU.min).then_inc(a2, 1)
                own.did(dve.tensor_scalar(tmp[0:L, 3, :], a, 0.0, None, ALU.max))
                for n, (g, m, b, s) in enumerate(jobs):
                    if g == 1:
                        dve.wait_ge(proj, n + 1)
                        dve.tensor_copy(vpad[:, m, b, 3 + s * S3:3 + (s + 1) * S3],
                                        c.bank[n % 6][:, 0:S3]).then_inc(ev[0], 1)
                    if n == 5:
                        dve.wait_ge(a1, 3)
                        own.wait()
                        A, dt, S = tmp[0:L, 3, :], q3[0:L, 0, :], q3[0:L, 1, :]
                        own.did(dve.tensor_tensor(A, A, lg, ALU.add))
                        own.did(dve.tensor_tensor(tmp[0:L, 1, :], dt, dt, ALU.mult))
                        own.wait()
                        own.did(dve.tensor_tensor(tmp[0:L, 1, :], tmp[0:L, 1, :], A, ALU.mult))
                        own.wait()
                        own.did(dve.tensor_scalar(tmp[0:L, 1, :], tmp[0:L, 1, :], 1.0, None, ALU.add))
                        own.wait()
                        own.did(dve.reciprocal(S, tmp[0:L, 1, :]))
                        own.wait()
                        own.did(dve.tensor_tensor(tmp[0:L, 1, :], S, dt, ALU.mult))
                        own.wait()
                        dve.scalar_tensor_tensor(q3[0:L, 2, :], tmp[0:L, 1, :], -1.0, A, ALU.mult,
                                                 ALU.mult).then_inc(qs, 1)
                dve.wait_ge(qt, 1)
                dve.tensor_copy(coef[0:LANES, :, :, :].rearrange("p a b c -> p (a b c)"),
                                c.bank[6][0:LANES, 0:6 * L]).then_inc(pcopy, 1)
                dve.wait_ge(cw_in, 16)
                dve.wait_ge(pad0, 1)
                dve.wait_ge(ev[0], len(jobs) // 2)
                for k in range(3):
                    o = vT[:, k, :].rearrange("p (b t) -> p b t", b=BATCH)
                    own.did(dve.tensor_scalar(o, vpad[:, k, :, 0:T], cw[:, k, 0:1], None, ALU.mult))
                    for t in range(1, 4):
                        own.wait()
                        ins = dve.scalar_tensor_tensor(o, vpad[:, k, :, t:t + T], cw[:, k, t:t + 1], o,
                                                       ALU.mult, ALU.add)
                        if t < 3:
                            own.did(ins)
                        else:
                            ins.then_inc(conv, 1)


def mixer_responses(c, ctx, coef, gs, ab, zx, de):
    nc = c.nc
    W = L + 2
    g = c.sb(ctx, "G", [128, 2, L, W])
    zb = c.sb(ctx, "z_state", [128, 2, W])
    zt = c.sb(ctx, "z_tmp", [128, 2, W])
    x0 = c.sb(ctx, "x_start", [128, W])
    sd = c.sb(ctx, "S_dt", [128, 2, L])
    r = c.sb(ctx, "lane_masked", [128, 2, 4, NBC // 2])
    own_s, masked = c.sem("scan_steps"), c.sem("lane_masked_ready")

    def scan_count(t):
        return 8 + 6 * (t + 1)

    tp, ev, rest_ev = c.sem("G_transposed"), [c.sem("G_copied_v"), c.sem("G_copied_s")], c.sem("resp_copied")
    P = LANES
    jobs = [(q, t0) for t0 in range(0, L, 4) for q in range(2)]
    with nc.Block() as block:
        def copy_out(eng, copy, par):
            for n, (q, t0) in enumerate(jobs):
                if par is not None and n % 2 != par:
                    continue
                k = min(4, L - t0)
                eng.wait_ge(tp, n + 1)
                copy(gs[0:L, t0:t0 + k, q * P:(q + 1) * P],
                     c.bank[n % 6][0:L, 0:k * P].rearrange("p (a b) -> p a b", a=k)).then_inc(ev[0 if par is None else par], 1)

        @block.vector
        def _(dve):
            own = Own(dve, own_s)
            own.did(dve.memset(g[0:P].rearrange("p a b c -> p (a b c)"), 0.0))
            own.did(dve.memset(zb[0:P, :, :], 0.0))
            own.did(dve.memset(x0[0:P, :], 0.0))
            own.did(dve.tensor_tensor(sd[0:P, :, :], coef[0:P, 0, :, :], coef[0:P, 1, :, :], ALU.mult))
            own.wait()
            own.did(dve.memset(zb[0:P, :, L:L + 1], 1.0))
            own.did(dve.memset(x0[0:P, L + 1:L + 2], 1.0))
            for q in range(2):
                flat = g[0:P, q, :, :].rearrange("p t s -> p (t s)")
                own.did(dve.tensor_copy(flat[:, 0:(L - 1) * (W + 1) + 1:W + 1], sd[0:P, q, :]))
            own.wait()

            def prev(q, t):
                return g[0:P, q, t - 1, :] if t else x0[0:P, :]

            for t in range(L):
                for q in range(2):
                    own.wait(1)
                    own.did(dve.scalar_tensor_tensor(zt[0:P, q, :], prev(q, t), coef[0:P, 2, q, t:t + 1],
                                                     g[0:P, q, t, :], ALU.mult, ALU.add))
                for q in range(2):
                    own.wait(1)
                    own.did(dve.scalar_tensor_tensor(zb[0:P, q, :], zb[0:P, q, :], coef[0:P, 1, q, t:t + 1],
                                                     zt[0:P, q, :], ALU.mult, ALU.add))
                for q in range(2):
                    own.wait(1)
                    own.did(dve.scalar_tensor_tensor(g[0:P, q, t, :], zb[0:P, q, :], coef[0:P, 0, q, t:t + 1],
                                                     prev(q, t), ALU.mult, ALU.add))
                assert own.n == scan_count(t)
            own.wait()
            for q in range(2):
                vals = [zb[0:P, q, L:L + 1], g[0:P, q, L - 1, L + 1:L + 2],
                        g[0:P, q, L - 1, L:L + 1], zb[0:P, q, L + 1:L + 2]]
                for j, v in enumerate(vals):
                    dve.tensor_scalar(r[0:P, q, j, :], c.const("bc", P), v, None, ALU.mult).then_inc(masked, 1)
            copy_out(dve, dve.tensor_copy, 0)
            dve.wait_ge(tp, len(jobs) + 1)
            dve.tensor_copy(ab[0:L, :, :].rearrange("p a b -> p (a b)"), c.bank[6][0:L, 0:4 * P]).then_inc(rest_ev, 1)
            dve.wait_ge(tp, len(jobs) + 3)
            dve.tensor_copy(zx[0:L, :], c.bank[7][0:L, 0:2 * P]).then_inc(rest_ev, 1)
            dve.tensor_copy(de[:, :, :].rearrange("p a b -> p (a b)"),
                            c.bank[7][0:96, 256:256 + 2 * NBC]).then_inc(rest_ev, 1)

        @block.scalar
        def _(act):
            copy_out(act, act.copy, 1)

        @block.tensor
        def _(pe):
            idn = c.const("ident", P)[:, 0:P]
            for n, (q, t0) in enumerate(jobs):
                k = min(4, L - t0)
                if n >= 6:
                    pe.wait_ge(ev[n % 2], (n - 6) // 2 + 1)
                pe.wait_ge(own_s, scan_count(t0 + k - 1))
                for t in range(t0, t0 + k):
                    ins = pe.transpose(c.bank[n % 6][0:L, (t - t0) * P:(t - t0 + 1) * P], g[0:P, q, t, 0:L], idn)
                ins.then_inc(tp, 1)
            for z in range(2):
                for q in range(2):
                    at = (z * 2 + q) * P
                    ins = pe.transpose(c.bank[6][0:L, at:at + P], g[0:P, q, :, L + z], idn)
            ins.then_inc(tp, 1)
            pe.wait_ge(masked, 8)
            for q in range(2):
                ins = pe.transpose(c.bank[7][0:L, q * P:(q + 1) * P], zb[0:P, q, 0:L], idn)
            ins.then_inc(tp, 1)
            for j in range(2):
                for q in range(2):
                    at = 256 + j * NBC + q * (NBC // 2)
                    for z in range(2):
                        ins = pe.matmul(c.bank[7][0:96, at:at + NBC // 2], c.const(f"sel{z}", P), r[0:P, q, 2 * j + z, :],
                                        start=(z == 0), stop=(z == 1))
            ins.then_inc(tp, 1)


def mixer_bc(c, ctx, vT, gs, ab, zx, acT, bw):
    nc = c.nc
    NG = NBC * SH
    w = c.sb(ctx, "w_bc", [128, 3, 96])
    bcn = c.sb(ctx, "bc_normed", [128, 2, NG, ST])
    ac = c.sb(ctx, "C_start", [128, NG, 2, ST])
    ss = c.sb(ctx, "bc_sumsq", [128, 2 * NG])
    sr = c.sb(ctx, "bc_norm", [128, 2 * NG])
    w_in, done, sq, own_s = c.sem("w_bc_in"), c.sem("bc_done"), c.sem("bc_squared"), c.sem("bc_own")
    sm, rt, nd = c.sem("bc_sums"), c.sem("bc_roots"), c.sem("bc_normed_ready")
    tp, ev = c.sem("bc_transposed"), [c.sem("bc_copied_v"), c.sem("bc_copied_s")]
    per = [min(5, NBC - 5 * i) for i in range(8)]
    jobs = [(kind, i) for kind in range(3) for i in range(0, NBC, 8)]
    with nc.Block() as block:
        @block.sync
        def _(sp):
            sp.dma_start(w[:, :, :], c.ins["L0_attn_w_bc"].rearrange("(k p) n -> p k n", p=128)).then_inc(w_in, 16)

        @block.tensor
        def _(pe):
            pe.wait_ge(w_in, 16)
            for i in range(NBC):
                for k in range(3):
                    ins = pe.matmul(c.bank[i // 5][0:L, (i % 5) * 96:(i % 5 + 1) * 96],
                                    vT[:, k, i * L:(i + 1) * L], w[:, k, :], start=(k == 0), stop=(k == 2))
                if i % 5 == 4 or i == NBC - 1:
                    ins.then_inc(done, 1)
            pe.wait_ge(nd, 10)
            for n, (kind, i) in enumerate(jobs):
                k = min(8, NBC - i)
                if n >= 8:
                    pe.wait_ge(ev[n % 2], (n - 8) // 2 + 1)
                rows = 48 if kind < 2 else 96
                for j in range(i, i + k):
                    src = (bcn[0:L, kind, j * SH:(j + 1) * SH, :].rearrange("p a b -> p (a b)") if kind < 2 else
                           ac[0:L, j * SH:(j + 1) * SH, :, :].rearrange("p a b c -> p (a b c)"))
                    ins = pe.transpose(c.bank[n % 8][0:rows, (j - i) * L:(j - i + 1) * L], src,
                                       c.const("ident", L)[:, 0:L])
                ins.then_inc(tp, 1)

        def copy_out(eng, copy, par):
            for n, (kind, i) in enumerate(jobs):
                if n % 2 != par:
                    continue
                k = min(8, NBC - i)
                rows = 48 if kind < 2 else 96
                eng.wait_ge(tp, n + 1)
                dst = c.xT[0:48, kind, i * L:(i + k) * L] if kind < 2 else acT[:, i * L:(i + k) * L]
                copy(dst, c.bank[n % 8][0:rows, 0:k * L]).then_inc(ev[par], 1)

        @block.scalar
        def _(act):
            for i in range(8):
                act.wait_ge(done, i + 1)
                n = per[i] * 96
                act.activation(ac[0:L].rearrange("p a b c -> p (a b c)")[:, i * 480:i * 480 + n],
                               c.bank[i][0:L, 0:n], ACT.Square).then_inc(sq, 1)
            act.wait_ge(sm, 1)
            act.activation(sr[0:L, :], ss[0:L, :], ACT.Sqrt).then_inc(rt, 1)
            copy_out(act, act.copy, 1)

        @block.vector
        def _(dve):
            own = Own(dve, own_s)
            dve.wait_ge(sq, 8)
            own.did(dve.tensor_reduce(ss[0:L, :], ac[0:L].rearrange("p a b c -> p (a b) c"), X, ALU.add))
            own.wait()
            dve.tensor_scalar(ss[0:L, :], ss[0:L, :], 1e-12, None, ALU.add).then_inc(sm, 1)
            dve.wait_ge(rt, 1)
            own.did(dve.reciprocal(ss[0:L, :], sr[0:L, :]))
            own.wait()
            for i in range(8):
                k = per[i] * SH
                dve.tensor_tensor(bcn[0:L, :, i * 30:i * 30 + k, :].rearrange("p z g n -> p g z n"),
                                  c.bank[i][0:L, 0:k * 2 * ST].rearrange("p (g z n) -> p g z n", z=2, n=ST),
                                  ss[0:L, i * 60:i * 60 + 2 * k].rearrange("p (g z) -> p g z", z=2).unsqueeze(3)
                                  .broadcast_to((L, k, 2, ST)), ALU.mult).then_inc(nd, 1)
            dve.wait_ge(nd, 8)
            for z in range(2):
                dve.tensor_tensor(ac[0:L, :, z, :], bcn[0:L, 1, :, :],
                                  ab[0:L, z, :].unsqueeze(2).broadcast_to((L, NG, ST)), ALU.mult).then_inc(nd, 1)
                end = zx[0:L, :] if z == 0 else gs[0:L, L - 1, :]
                own.did(dve.tensor_tensor(bw[0:L, :, z, :], bcn[0:L, 0, :, :],
                                          end.unsqueeze(2).broadcast_to((L, NG, ST)), ALU.mult))
            copy_out(dve, dve.tensor_copy, 0)


def mixer_chain(c, ctx, sg, vT, gs, acT, bw, de):
    nc = c.nc
    cbd = c.sb(ctx, "C_by_head", [48, 2, SH, L])
    u = c.sb(ctx, "u_tokens", [128, 2, DIN])
    wt = c.sb(ctx, "mix_matrix", [128, 2, SH, L])
    tm = c.sb(ctx, "transition", [96, 2, 96])
    state = c.sb(ctx, "state", [96, BATCH, 2, DIN])
    yd = c.sb(ctx, "y_plus_Du", [128, 2, 3, L])
    dsk = c.sb(ctx, "D_skip", [128, 3])
    names = ["cbd_ready", "u_transposed", "u_copied", "cb_done", "wt_ready", "y_done", "y_used", "tm_ready",
             "state_done", "state_ready"]
    cbd_ready, u_t, u_ready, cb_done, wt_ready, y_done, y_used, tm_ready, s_done, s_ready = map(c.sem, names)
    d_in, own_s = c.sem("D_skip_in"), c.sem("chain_own")
    N = NBC
    steps = [(ch, b, b * NC1 + ch) for ch in range(NC1) for b in range(BATCH)]
    last = N - BATCH
    with nc.Block() as block:
        @block.sync
        def _(sp):
            for e in range(2):
                for k in range(3):
                    h = 2 * k + e
                    sp.dma_start(dsk[64 * e:64 * e + 64, k:k + 1], c.ins["L0_attn_D_skip"][h:h + 1].rearrange(
                        "(a n) -> a n", a=1).broadcast_to((64, 1))).then_inc(d_in, 16)

        @block.gpsimd
        def _(pool):
            for n, (ch, b, bc_) in enumerate(steps):
                if n >= 2:
                    pool.wait_ge(cb_done, n - 1)
                pool.tensor_tensor(cbd[:, n % 2, :, :],
                                   c.xT[0:48, 1, bc_ * L:(bc_ + 1) * L].unsqueeze(1).broadcast_to((48, SH, L)),
                                   c.const("h48", 48).unsqueeze(2).broadcast_to((48, SH, L)),
                                   ALU.mult).then_inc(cbd_ready, 1)

        @block.scalar
        def _(act):
            for n in range(N):
                act.wait_ge(u_t, n + 1)
                if n >= 2:
                    act.wait_ge(y_done, n - 1)
                    act.wait_ge(s_done, min(n - 1, last))
                act.copy(u[0:L, n % 2, :], c.bank[n % 2][0:L, 0:DIN]).then_inc(u_ready, 1)

        @block.tensor
        def _(pe):
            def prepare(n):
                ch, b, bc_ = steps[n]
                if n >= 2:
                    pe.wait_ge(u_ready, n - 1)
                for k in range(3):
                    ins = pe.transpose(c.bank[n % 2][0:L, k * 128:(k + 1) * 128], vT[:, k, bc_ * L:(bc_ + 1) * L],
                                       c.const("ident"))
                ins.then_inc(u_t, 1)
                pe.wait_ge(cbd_ready, n + 1)
                if n >= 2:
                    pe.wait_ge(wt_ready, n - 1)
                pe.matmul(c.bank[2 + n % 2][0:L, 0:SH * L], c.xT[0:48, 0, bc_ * L:(bc_ + 1) * L],
                          cbd[:, n % 2, :, :].rearrange("p a b -> p (a b)"), start=True, stop=True).then_inc(cb_done, 1)

            prepare(0)
            for n, (ch, b, bc_) in enumerate(steps):
                if n + 1 < N:
                    prepare(n + 1)
                ybank, sbank = c.bank[4 + n % 2], c.bank[6 + n % 2]
                if n >= 2:
                    pe.wait_ge(y_used, 3 * (n - 1))
                if ch:
                    pe.wait_ge(s_ready, n - BATCH + 1)
                pe.wait_ge(u_ready, n + 1)
                if n < last:
                    pe.wait_ge(tm_ready, n + 1)
                    if ch:
                        pe.matmul(sbank[0:96, 0:DIN], tm[:, n % 2, :], state[:, b, (ch - 1) % 2, :],
                                  start=True, stop=False)
                    pe.matmul(sbank[0:96, 0:DIN],
                              bw[0:L, bc_ * SH:(bc_ + 1) * SH, :, :].rearrange("p a b c -> p (a b c)"),
                              u[0:L, n % 2, :], start=(ch == 0), stop=True).then_inc(s_done, 1)
                pe.wait_ge(wt_ready, n + 1)
                for k in range(3):
                    if ch:
                        pe.matmul(ybank[:, k * L:(k + 1) * L], state[:, b, (ch - 1) % 2, k * 128:(k + 1) * 128],
                                  acT[:, bc_ * L:(bc_ + 1) * L], start=True, stop=False, skip_group_check=True)
                    for e in range(2):
                        h = 2 * k + e
                        ins = pe.matmul(ybank[64 * e:64 * e + 64, k * L:(k + 1) * L],
                                        u[0:L, n % 2, h * SP:(h + 1) * SP], wt[0:L, n % 2, h, :],
                                        start=(ch == 0), stop=True, skip_group_check=True)
                ins.then_inc(y_done, 1)

        @block.vector
        def _(dve):
            own = Own(dve, own_s)

            def prepare(n):
                ch, b, bc_ = steps[n]
                if n < last:
                    if n >= 2:
                        dve.wait_ge(s_done, n - 1)
                    own.did(dve.tensor_scalar(tm[:, n % 2, :], c.const("ident", 96)[:, 0:96],
                                              de[:, 0, bc_:bc_ + 1], None, ALU.mult))
                    own.wait()
                    dve.scalar_tensor_tensor(tm[:, n % 2, :], c.const("swap", 96), de[:, 1, bc_:bc_ + 1],
                                             tm[:, n % 2, :], ALU.mult, ALU.add).then_inc(tm_ready, 1)
                dve.wait_ge(cb_done, n + 1)
                if n >= 2:
                    dve.wait_ge(y_done, n - 1)
                dve.tensor_tensor(wt[0:L, n % 2, :, :],
                                  c.bank[2 + n % 2][0:L, 0:SH * L].rearrange("p (a b) -> p a b", a=SH),
                                  gs[0:L, :, bc_ * SH:(bc_ + 1) * SH].rearrange("p t h -> p h t"),
                                  ALU.mult).then_inc(wt_ready, 1)

            dve.wait_ge(d_in, 96)
            prepare(0)
            for n, (ch, b, bc_) in enumerate(steps):
                if n + 1 < N:
                    prepare(n + 1)
                if n < last:
                    dve.wait_ge(s_done, n + 1)
                    if ch >= 2:
                        dve.wait_ge(y_done, n - BATCH + 1)
                    dve.tensor_tensor(state[:, b, ch % 2, :], c.bank[6 + n % 2][0:96, 0:DIN], c.const("bd", 96),
                                      ALU.mult).then_inc(s_ready, 1)
                dve.wait_ge(y_done, n + 1)
                for k in range(3):
                    dve.scalar_tensor_tensor(yd[:, n % 2, k, :], vT[:, k, bc_ * L:(bc_ + 1) * L], dsk[:, k:k + 1],
                                             c.bank[4 + n % 2][:, k * L:(k + 1) * L], ALU.mult, ALU.add
                                             ).then_inc(y_used, 1)
                dve.wait_ge(y_used, 3 * (n + 1))
                o = sg[:, :, bc_ * L:(bc_ + 1) * L]
                own.did(dve.tensor_tensor(o, yd[:, n % 2, :, :], o, ALU.mult))


def mlps(c, name, variants, func):
    nc = c.nc
    with ExitStack() as ctx:
        w1 = c.sb(ctx, name + "_w1", [DH, 2, 2, FF])
        w2 = c.sb(ctx, name + "_w2", [128, 2, NF, D])
        b1 = c.sb(ctx, name + "_b1", [128, 2, NF])
        b2 = c.sb(ctx, name + "_b2", [1, 2, D])
        hid = c.sb(ctx, name + "_hidden", [128, 2, NF, CW])
        w_in = [c.sem(name + "_w_in0"), c.sem(name + "_w_in1")]
        up, act_done, down, added = (c.sem(name + x) for x in ("_up", "_act", "_down", "_added"))
        jobs = [(v, ch) for v, va in enumerate(variants) for ch in va["chunks"]]
        first, final, before, seen = {}, {}, {}, {}
        for n, (v, ch) in enumerate(jobs):
            first.setdefault(v, n)
            final[v] = n
            before[n] = seen.get(ch)
            seen[ch] = n
        with nc.Block() as block:
            @block.sync
            def _(sp):
                for v, va in enumerate(variants):
                    s = v % 2
                    if v >= 2:
                        sp.wait_ge(down, 3 * (final[v - 2] + 1))
                        sp.wait_ge(act_done, NF * (final[v - 2] + 1))
                    sp.dma_start(w1[:, s, :, :], va["w1"].rearrange("(o p) n -> p o n", p=DH)).then_inc(w_in[s], 16)
                    sp.dma_start(w2[:, s, :, :], va["w2"].rearrange("(f p) n -> p f n", p=128)).then_inc(w_in[s], 16)
                    sp.dma_start(b1[:, s, :], va["b1"].rearrange("(f p) -> p f", p=128),
                                 allow_slow_non_contiguous=True).then_inc(w_in[s], 16)
                    sp.dma_start(b2[:, s, :], va["b2"].rearrange("(a n) -> a n", a=1)).then_inc(w_in[s], 16)

            @block.tensor
            def _(pe):
                def up_proj(n):
                    v, ch = jobs[n]
                    s = v % 2
                    if n == first[v]:
                        pe.wait_ge(w_in[s], 64 * (v // 2 + 1))
                    for f in range(NF):
                        m = n * NF + f
                        if m >= 4:
                            pe.wait_ge(act_done, m - 3)
                        parts = variants[v]["parts"]
                        for k, (o, rows) in enumerate(parts):
                            ins = pe.matmul(c.bank[m % 4][:, 0:CW], w1[0:rows, s, o, f * 128:(f + 1) * 128],
                                            c.xT[0:rows, o, ch * CW:(ch + 1) * CW],
                                            start=(k == 0), stop=(k == len(parts) - 1))
                        ins.then_inc(up, 1)

                up_proj(0)
                for n, (v, ch) in enumerate(jobs):
                    if n + 1 < len(jobs):
                        up_proj(n + 1)
                    s, cols = v % 2, variants[v]["n"]
                    pe.wait_ge(act_done, NF * (n + 1))
                    for i in range(3):
                        m = 3 * n + i
                        if m >= 4:
                            pe.wait_ge(added, m - 3)
                        ps = c.bank[4 + m % 4][0:TT, 0:cols]
                        pe.matmul(ps, c.ones[0:1, 0:TT], b2[:, s, 0:cols], start=True, stop=False)
                        for f in range(NF):
                            ins = pe.matmul(ps, hid[:, n % 2, f, i * TT:(i + 1) * TT], w2[:, s, f, 0:cols],
                                            start=False, stop=(f == NF - 1))
                        ins.then_inc(down, 1)

            @block.scalar
            def _(act):
                for n, (v, ch) in enumerate(jobs):
                    if n >= 2:
                        act.wait_ge(down, 3 * (n - 1))
                    for f in range(NF):
                        m = n * NF + f
                        act.wait_ge(up, m + 1)
                        act.activation(hid[:, n % 2, f, :], c.bank[m % 4][:, 0:CW], func,
                                       bias=b1[:, v % 2, f:f + 1]).then_inc(act_done, 1)

            @block.vector
            def _(dve):
                for n, (v, ch) in enumerate(jobs):
                    cols, gain = variants[v]["n"], variants[v]["gain"]
                    for i in range(3):
                        m, t = 3 * n + i, 3 * ch + i
                        dve.wait_ge(down, m + 1)
                        if before[n] is not None:
                            dve.wait_ge(added, 3 * before[n] + i + 1)
                        ps, x = c.bank[4 + m % 4][0:TT, 0:cols], c.xN[0:TT, t, 0:cols]
                        if gain is None:
                            ins = dve.tensor_tensor(x, ps, x, ALU.add)
                        else:
                            ins = dve.scalar_tensor_tensor(x, ps, gain(t), x, ALU.mult, ALU.add)
                        ins.then_inc(added, 1)


def qkv(c, name, source, bias, q2, kT, v):
    nc = c.nc
    E2 = 64
    with ExitStack() as ctx:
        w = c.sb(ctx, name + "_w", [DH + 1, 2, 3 * D])
        wrow = c.sb(ctx, name + "_rows", [DH, 6, D]) if bias is not None else None
        parts = c.sb(ctx, name + "_parts", [128, 2, 2, HEADS, E2], F16)
        idh = c.sb(ctx, name + "_ident", [128, 128], F16)
        names = ("_w_in", "_b_in", "_set", "_w_turned", "_placed", "_proj", "_proj_v", "_high", "_low", "_again",
                 "_turned", "_k_out", "_q_out", "_v_out")
        (w_in, b_in, init, wt, placed, pqk, pv, high, low, again, turned, k_out, q_out, v_out) = (
            c.sem(name + x) for x in names)
        tiles = [(b, k) for b in range(BATCH) for k in range(len(KT))]
        N = len(tiles)

        def cols(n):
            b, k = tiles[n]
            return b * T + KT[k][0], KT[k][1]

        def turned_bank(n, z):
            return c.bank[4 + 2 * z + n % 2].bitcast(F16)

        with nc.Block() as block:
            @block.sync
            def _(sp):
                if bias is None:
                    sp.dma_start(w[0:DH, :, :], source.rearrange("(o p) n -> p o n", p=DH)).then_inc(w_in, 16)
                else:
                    sp.dma_start(wrow[:, :, :], source.rearrange("(a p) n -> p a n", p=DH)).then_inc(w_in, 16)
                    sp.dma_start(w[DH:DH + 1, 1, :], bias.rearrange("(a n) -> a n", a=1)).then_inc(b_in, 16)

            @block.gpsimd
            def _(pool):
                pool.memset(parts[:, :, 0, :, :], 0.0).then_inc(init, 1)
                pool.memset(parts[:, :, 1, :, :], 0.0).then_inc(init, 1)
                pool.tensor_copy(idh[:, :], c.const("ident")).then_inc(init, 1)
                pool.memset(v[:, :, :, :, HD:2 * HD], 1.0).then_inc(init, 1)
                pool.wait_ge(init, 4)
                pool.memset(parts[:, :, 1, :, 32:33], -1.0).then_inc(init, 1)
                for n in range(N):
                    m = cols(n)[1]
                    pool.wait_ge(high, n + 1)
                    for z, at in ((0, 33), (1, 16)):
                        pool.tensor_copy(parts[0:m, n % 2, z, :, at:at + HD], parts[0:m, n % 2, z, :, 0:HD]
                                         ).then_inc(again, 1)

            @block.tensor
            def _(pe):
                if bias is not None:
                    pe.wait_ge(w_in, 16)
                    for a in range(6):
                        for o in range(2):
                            ins = pe.transpose(c.bank[a][0:DH, o * DH:(o + 1) * DH],
                                               wrow[:, a, o * DH:(o + 1) * DH], c.const("ident", DH)[:, 0:DH])
                        ins.then_inc(wt, 1)
                    pe.wait_ge(placed, 6)
                    pe.wait_ge(b_in, 16)
                else:
                    pe.wait_ge(w_in, 16)
                    pe.wait_ge(placed, 1)

                def project(n):
                    at, m = cols(n)
                    if n >= 2:
                        pe.wait_ge(low, 2 * (n - 1))
                        pe.wait_ge(v_out, n - 1)
                    for o in range(2):
                        r = DH + o
                        ins = pe.matmul(c.bank[n % 2][0:m, 0:2 * D], c.xT[0:r, o, at:at + m], w[0:r, o, 0:2 * D],
                                        start=(o == 0), stop=(o == 1))
                    ins.then_inc(pqk, 1)
                    for o in range(2):
                        r = DH + o
                        ins = pe.matmul(c.bank[2 + n % 2][0:m, 0:D], c.xT[0:r, o, at:at + m], w[0:r, o, 2 * D:3 * D],
                                        start=(o == 0), stop=(o == 1))
                    ins.then_inc(pv, 1)

                project(0)
                pe.wait_ge(init, 5)
                for n in range(N):
                    if n + 1 < N:
                        project(n + 1)
                    m = cols(n)[1]
                    pe.wait_ge(low, 2 * n + 2)
                    pe.wait_ge(again, 2 * n + 2)
                    if n >= 2:
                        pe.wait_ge(k_out, n - 1)
                        pe.wait_ge(q_out, 2 * (n - 1))
                    for z in range(2):
                        for g in range(HEADS // 2):
                            ins = pe.transpose(turned_bank(n, z)[:, g * TT:g * TT + m],
                                               parts[0:m, n % 2, z, 2 * g:2 * g + 2, :].rearrange("p h e -> p (h e)"),
                                               idh[0:m, 0:m])
                        ins.then_inc(turned, 1)

            def turned_view(n, z, p0, p1):
                m = cols(n)[1]
                return turned_bank(n, z)[p0:p1, 0:6 * TT].rearrange("p (g t) -> p g t", g=6)[:, :, 0:m]

            @block.scalar
            def _(act):
                act.wait_ge(init, 5)
                for n in range(N + 1):
                    if n < N:
                        b, k = tiles[n]
                        at, m = cols(n)
                        act.wait_ge(pqk, n + 1)
                        if n >= 2:
                            act.wait_ge(turned, 2 * (n - 1))
                        act.copy(parts[0:m, n % 2, :, :, 0:HD],
                                 c.bank[n % 2][0:m, 0:2 * D].rearrange("p (z h e) -> p z h e", z=2, e=HD)
                                 ).then_inc(high, 1)
                        act.wait_ge(pv, n + 1)
                        act.copy(v[0:m, b, k, :, 0:HD], c.bank[2 + n % 2][0:m, 0:D].rearrange("p (h e) -> p h e", e=HD)
                                 ).then_inc(v_out, 1)
                    if n:
                        at, m = cols(n - 1)
                        act.wait_ge(turned, 2 * n - 1)
                        for e in range(2):
                            act.copy(q2[64 * e:64 * e + 64, :, e, at:at + m], turned_view(n - 1, 0, 64 * e, 64 * e + 64)
                                     ).then_inc(q_out, 1)

            @block.vector
            def _(dve):
                for b in range(BATCH):
                    for e in range(2):
                        dve.memset(q2[64 - 64 * e:128 - 64 * e, :, e, b * T:(b + 1) * T], 0.0)
                if bias is None:
                    dve.memset(w[DH:DH + 1, 1, :], 0.0).then_inc(placed, 1)
                else:
                    for a in range(6):
                        dve.wait_ge(wt, a + 1)
                        dve.tensor_copy(w[0:DH, :, a * DH:(a + 1) * DH],
                                        c.bank[a][0:DH, 0:D].rearrange("p (o n) -> p o n", o=2)).then_inc(placed, 1)
                dve.wait_ge(init, 5)
                for n in range(N + 1):
                    if n < N:
                        at, m = cols(n)
                        dve.wait_ge(high, n + 1)
                        ps = c.bank[n % 2][0:m, 0:2 * D].rearrange("p (z h e) -> p z h e", z=2, e=HD)
                        for z, to in ((0, 16), (1, 33)):
                            dve.tensor_tensor(parts[0:m, n % 2, z, :, to:to + HD], ps[:, z, :, :],
                                              parts[0:m, n % 2, z, :, 0:HD], ALU.subtract).then_inc(low, 1)
                    if n:
                        at, m = cols(n - 1)
                        dve.wait_ge(turned, 2 * n)
                        dve.tensor_copy(kT[:, :, at:at + m], turned_view(n - 1, 1, 0, 128)).then_inc(k_out, 1)


def attention(c, name, q2, kT, v, aT):
    nc = c.nc
    NK = len(KT)
    HALF = T // 2 + 1
    START = (0, T - HALF)
    scale = HD ** -0.5
    groups = [(b, j) for b in range(BATCH) for j in range(3)]
    G = len(groups)
    with ExitStack() as ctx:
        mx = c.sb(ctx, name + "_max", [128, 2, 2, 4, NK])
        mexp = c.sb(ctx, name + "_max_placed", [128, 2, 2, NK, 128], F16)
        p = c.sb(ctx, name + "_p", [128, 4, 2, HALF])
        idh = c.sb(ctx, name + "_ident", [128, 128], F16)
        den = c.sb(ctx, name + "_den", [128, 2, HALF])
        rec = c.sb(ctx, name + "_recip", [128, 2, HALF])
        names = ("_set", "_scored", "_maxed", "_placed", "_m_turned", "_m_copied", "_keyed", "_exp", "_summed",
                 "_spread", "_den_own", "_out")
        (init, scored, maxed, placed, mt, mc, keyed, expd, summed, spread, rown, outd) = (
            c.sem(name + x) for x in names)
        A_UNITS = [("s", hh, k, half) for hh in range(4) for k in range(NK) for half in range(2)] + [
            ("m", gi, 0, 0) for gi in range(2)]
        NA, NS = len(A_UNITS), 40
        B_UNITS = [(half, k, gi) for half in range(2) for k in range(NK) for gi in range(2)]
        NB = len(B_UNITS)

        def ring_bank(g, i):
            return c.bank[(g * NA + i) % 3]

        acc = c.bank[3]
        with nc.Block() as block:
            @block.gpsimd
            def _(pool):
                pool.tensor_copy(idh[:, :], c.const("ident")).then_inc(init, 1)
                pool.memset(mexp[:, :, :, :, :], 0.0).then_inc(init, 1)
                pool.memset(mx[:, :, :, :, :], 0.0).then_inc(init, 1)

            @block.tensor
            def _(pe):
                pe.wait_ge(init, 3)

                def ring_free(g, i):
                    n = g * NA + i - 3
                    if n < 0:
                        return
                    g0, i0 = divmod(n, NA)
                    if i0 < NS:
                        pe.wait_ge(maxed, g0 * NS + i0 + 1)
                    else:
                        pe.wait_ge(mc, 4 * g0 + 2 * (i0 - NS) + 2)

                def a_unit(g, i):
                    b, j = groups[g]
                    kind, x, k, half = A_UNITS[i]
                    ring_free(g, i)
                    if kind == "s":
                        q0, qn = KT[k]
                        k0 = START[half]
                        pe.matmul(ring_bank(g, i)[0:qn, 0:HALF],
                                  q2[:, 2 * j + x // 2, x % 2, b * T + q0:b * T + q0 + qn],
                                  kT[:, 2 * j + x // 2, b * T + k0:b * T + k0 + HALF],
                                  start=True, stop=True).then_inc(scored, 1)
                    else:
                        pe.wait_ge(placed, 2 * g + 2)
                        for k in range(NK):
                            q0, qn = KT[k]
                            ins = pe.transpose(ring_bank(g, i).bitcast(F16)[:, q0:q0 + qn],
                                               mexp[0:qn, g % 2, x, k, :], idh[0:qn, 0:qn])
                        ins.then_inc(mt, 1)

                def keys(g, i):
                    b, j = groups[g]
                    half, k, gi = B_UNITS[i]
                    n = g * NB + i
                    k0, kn = KT[k]
                    if i == 0:
                        pe.wait_ge(mc, 4 * g + 4)
                    if n >= 2:
                        pe.wait_ge(expd, n - 1)
                    for e in range(2):
                        ins = pe.matmul(c.pair[2 + n % 2][0:kn, 512 * e:512 * e + HALF],
                                        kT[:, 2 * j + gi, b * T + k0:b * T + k0 + kn],
                                        q2[:, 2 * j + gi, e, b * T + START[half]:b * T + START[half] + HALF],
                                        start=True, stop=True)
                    ins.then_inc(keyed, 1)

                def values(g, i):
                    b, j = groups[g]
                    half, k, _ = B_UNITS[i]
                    kn = KT[k][1]
                    n = g * NB + i
                    pe.wait_ge(expd, n + 2)
                    if k == 0 and n:
                        pe.wait_ge(outd, 2 * g + half)
                    for hh in range(4):
                        h = 4 * j + hh
                        ins = pe.matmul(acc[32 * hh:32 * hh + 32, 0:HALF], v[0:kn, b, k, h, :],
                                        p[0:kn, (n + hh // 2) % 4, hh % 2, :],
                                        start=(k == 0), stop=(k == NK - 1))
                    ins.then_inc(summed, 1)

                for i in range(NA):
                    a_unit(0, i)
                for g in range(G):
                    done = 0
                    for i in range(NB + 2):
                        if i < NB:
                            keys(g, i)
                        if i >= 3 and i % 2:
                            values(g, i - 3)
                        if g + 1 < G:
                            upto = min(NA, (i + 1) * NA // NB)
                            while done < upto:
                                a_unit(g + 1, done)
                                done += 1

            @block.vector
            def _(dve):
                dve.wait_ge(init, 3)

                def a_unit(g, i):
                    kind, x, k, half = A_UNITS[i]
                    if kind == "s":
                        qn = KT[k][1]
                        dve.wait_ge(scored, g * NS + i + 1)
                        dve.reduce_max(mx[0:qn, g % 2, half, x, k:k + 1], ring_bank(g, i)[0:qn, 0:HALF], X
                                       ).then_inc(maxed, 1)
                    elif x == 0:
                        dve.wait_ge(maxed, (g + 1) * NS)
                        if g >= 2:
                            dve.wait_ge(mt, 2 * (g - 1))
                        for e in range(2):
                            a, b_ = (mx[:, g % 2, hf, :, :].rearrange("p (i e) k -> p i e k", e=2)[:, :, e, :]
                                     for hf in range(2))
                            dve.tensor_tensor(mexp[:, g % 2, :, :, 64 * e + 32], a, b_, ALU.max).then_inc(placed, 1)
                    if kind == "m":
                        copy_max(dve, dve.tensor_copy, g, x)

                def copy_max(eng, copy, g, gi):
                    b, j = groups[g]
                    eng.wait_ge(mt, 2 * g + gi + 1)
                    for e in range(2):
                        r = 64 * e + 32
                        copy(q2[r:r + 1, 2 * j + gi, e, b * T:(b + 1) * T],
                             ring_bank(g, NS + gi).bitcast(F16)[r:r + 1, 0:T]).then_inc(mc, 1)

                def finish(g, half):
                    b, j = groups[g]
                    n = 2 * g + half
                    dve.wait_ge(summed, NK * (n + 1))
                    dve.stream_shuffle(den[:, n % 2, :], acc[:, 0:HALF], [16] * 16 + list(range(16, 32))
                                       ).then_inc(spread, 1)
                    dve.wait_ge(spread, n + 1)
                    dve.reciprocal(rec[:, n % 2, :], den[:, n % 2, :]).then_inc(rown, 1)
                    dve.wait_ge(rown, n + 1)
                    if half:
                        dve.wait_ge(outd, n)
                    at = b * T + START[half]
                    dve.tensor_tensor(aT[:, j, at:at + HALF], acc[:, 0:HALF], rec[:, n % 2, :], ALU.mult
                                      ).then_inc(outd, 1)

                for i in range(NA):
                    a_unit(0, i)
                for g in range(G):
                    done = 0
                    for i in range(NB + 2):
                        if i >= NB // 2 + 2 and i == NB // 2 + 2:
                            finish(g, 0)
                        if g + 1 < G:
                            upto = min(NA, (i + 1) * NA // NB)
                            while done < upto:
                                a_unit(g + 1, done)
                                done += 1
                    finish(g, 1)

            @block.scalar
            def _(act):
                for n in range(G * NB):
                    half, k, gi = B_UNITS[n % NB]
                    kn = KT[k][1]
                    act.wait_ge(keyed, n + 1)
                    if n >= 4:
                        act.wait_ge(summed, (n - 4) // 2 + 1)
                    act.activation(p[0:kn, n % 4, :, :],
                                   c.pair[2 + n % 2][0:kn, :].rearrange("p (e q) -> p e q", e=2)[:, :, 0:HALF],
                                   ACT.Exp, scale=scale).then_inc(expd, 1)


def ff0(c):
    i = c.ins
    mlps(c, "ff0", [dict(w1=i["L0_attn_ff_w1"], b1=i["L0_attn_ff_b1"], w2=i["L0_attn_ff_w2"], b2=i["L0_attn_ff_b2"],
                         parts=[(0, DH), (1, DH)], n=D, gain=None, chunks=range(NCH))],
         ACT.Gelu_apprx_tanh)


def attention_layer(c, name, w_qkv, b_qkv, project):
    with ExitStack() as ctx:
        aT = c.sb(ctx, name + "_aT", [128, 3, NT])
        with ExitStack() as inner:
            q2 = c.sb(inner, name + "_q2", [128, HEADS // 2, 2, NT], F16)
            kT = c.sb(inner, name + "_kT", [128, HEADS // 2, NT], F16)
            v = c.sb(inner, name + "_v", [128, BATCH, len(KT), HEADS, 2 * HD])
            qkv(c, name + "_qkv", w_qkv, b_qkv, q2, kT, v)
            attention(c, name, q2, kT, v, aT)
        project(ctx, aT)


def out_proj0(c, ctx, aT):
    nc = c.nc
    row = c.sb(ctx, "outp_rows", [DH, 2, D])
    spread = c.sb(ctx, "outp_spread", [DH, 2, 3, 128])
    w = c.sb(ctx, "outp_w", [128, 3, D])
    bias = c.sb(ctx, "outp_b", [128, D])
    w_in, zeroed, placed, tp, done = (c.sem("outp" + x) for x in ("_in", "_zeroed", "_spread", "_turned", "_placed"))
    with nc.Block() as block:
        @block.sync
        def _(sp):
            sp.dma_start(row[:, :, :], c.ins["L0_ffn_out_proj_w"].rearrange("(a p) n -> p a n", p=DH)
                         ).then_inc(w_in, 16)
            sp.dma_start(bias[:, :], c.ins["L0_ffn_out_proj_b"].rearrange("(a n) -> a n", a=1).broadcast_to((128, D))
                         ).then_inc(done, 16)
            sp.wait_ge(done, 16)

        @block.vector
        def _(dve):
            dve.memset(spread[:, :, :, :], 0.0).then_inc(zeroed, 1)
            dve.wait_ge(zeroed, 1)
            dve.wait_ge(w_in, 16)
            for a in range(2):
                dst = spread[:, a, :, :].rearrange("p g (h e) -> p (g h) e", e=2 * HD)[:, :, 0:HD]
                dve.tensor_copy(dst, row[:, a, :].rearrange("p (h e) -> p h e", e=HD)).then_inc(placed, 1)
            for g in range(3):
                dve.wait_ge(tp, g + 1)
                dve.tensor_copy(w[:, g, :], c.bank[g][:, 0:D])

        @block.tensor
        def _(pe):
            pe.wait_ge(placed, 2)
            for g in range(3):
                for a in range(2):
                    ins = pe.transpose(c.bank[g][:, a * DH:(a + 1) * DH], spread[:, a, g, :],
                                       c.const("ident", DH)[:, 0:DH])
                ins.then_inc(tp, 1)
    to_tokens(c, "outp", [], lambda i: [(aT[:, k, :], w[:, k, :]) for k in range(3)], lambda i: bias[0:TT, :])


def route(c, comb):
    nc = c.nc
    E = EXPERTS
    with ExitStack() as ctx:
        row = c.sb(ctx, "router_rows", [E, D])
        w = c.sb(ctx, "router_w", [DH, 2, E])
        rb = c.sb(ctx, "router_b", [1, E])
        lg = c.sb(ctx, "router_logits", [128, NTILE, E])
        pr = c.sb(ctx, "router_probs", [128, NTILE, E])
        top = c.sb(ctx, "top_one", [128, NTILE, E])
        tie = c.sb(ctx, "top_rank", [128, NTILE, E])
        m = c.sb(ctx, "router_max", [128, 4, NTILE])
        w_in, tp, placed, done = c.sem("router_in"), c.sem("router_turned"), c.sem("router_placed"), c.sem("logits")
        own_s, shifted, exped = c.sem("route_own"), c.sem("logits_shifted"), c.sem("router_exp")
        with nc.Block() as block:
            @block.sync
            def _(sp):
                sp.dma_start(row[:, :], c.ins["L0_ffn_router_w"]).then_inc(w_in, 16)
                sp.dma_start(rb[:, :], c.ins["L0_ffn_router_b"].rearrange("(a n) -> a n", a=1)).then_inc(w_in, 16)

            @block.tensor
            def _(pe):
                pe.wait_ge(w_in, 32)
                for o in range(2):
                    ins = pe.transpose(c.bank[1][0:DH, o * E:(o + 1) * E], row[:, o * DH:(o + 1) * DH],
                                       c.const("ident", E)[:, 0:E])
                ins.then_inc(tp, 1)
                pe.wait_ge(placed, 1)
                for i in range(NTILE):
                    ps = c.bank[0][0:TT, i * E:(i + 1) * E]
                    pe.matmul(ps, c.ones[0:1, 0:TT], rb[:, :], start=True, stop=False)
                    for o in range(2):
                        ins = pe.matmul(ps, c.xT[0:DH, o, i * TT:(i + 1) * TT], w[:, o, :], start=False, stop=(o == 1))
                ins.then_inc(done, 1)

            @block.scalar
            def _(act):
                act.wait_ge(shifted, 1)
                act.activation(pr[0:TT, :, :], lg[0:TT, :, :], ACT.Exp).then_inc(exped, 1)

            @block.vector
            def _(dve):
                own = Own(dve, own_s)

                def wide(ap):
                    return ap.unsqueeze(2).broadcast_to((TT, NTILE, E))

                def tt(out, a, b, op):
                    own.did(dve.tensor_tensor(out, a, b, op))
                    own.wait()

                def largest(out, a):
                    own.did(dve.tensor_reduce(out, a, X, ALU.max))
                    own.wait()

                P, L_, R, TOP = pr[0:TT], lg[0:TT], tie[0:TT], top[0:TT]
                m1, m2, mr, sm = (m[0:TT, k, :] for k in range(4))
                rank = c.const("rank", TT).unsqueeze(1).broadcast_to((TT, NTILE, E))
                dve.wait_ge(tp, 1)
                dve.tensor_copy(w[:, :, :].rearrange("p o e -> p (o e)"), c.bank[1][0:DH, 0:2 * E]).then_inc(placed, 1)
                dve.wait_ge(done, 1)
                own.did(dve.tensor_copy(L_.rearrange("p a b -> p (a b)"), c.bank[0][0:TT, 0:NTILE * E]))
                own.wait()
                largest(m1, L_)
                dve.tensor_tensor(L_, L_, wide(m1), ALU.subtract).then_inc(shifted, 1)
                dve.wait_ge(exped, 1)
                own.did(dve.tensor_reduce(sm, P, X, ALU.add))
                own.wait()
                own.did(dve.reciprocal(sm, sm))
                own.wait()
                tt(P, P, wide(sm), ALU.mult)

                def pick(values, best, one):
                    largest(best, values)
                    tt(R, values, wide(best), ALU.is_equal)
                    tt(R, R, rank, ALU.mult)
                    largest(mr, R)
                    tt(one, R, wide(mr), ALU.is_equal)

                pick(P, m1, TOP)
                own.did(dve.scalar_tensor_tensor(L_, TOP, -2.0, P, ALU.mult, ALU.add))
                own.wait()
                C = comb[0:TT]
                pick(L_, m2, C)
                tt(C, C, TOP, ALU.add)
                tt(C, C, P, ALU.mult)
                tt(sm, m1, m2, ALU.add)
                own.did(dve.reciprocal(sm, sm))
                own.wait()
                tt(C, C, wide(sm), ALU.mult)


def moe(c):
    i = c.ins
    with ExitStack() as ctx:
        comb = c.sb(ctx, "combine", [128, NTILE, EXPERTS])
        route(c, comb)
        mlps(c, "moe", [dict(w1=i["L0_ffn_w1"][e], b1=i["L0_ffn_b1"][e], w2=i["L0_ffn_w2"][e], b2=i["L0_ffn_b2"][e],
                             parts=[(0, DH), (1, DH)], n=D, gain=lambda t, e=e: comb[0:TT, t, e:e + 1],
                             chunks=range(NCH)) for e in range(EXPERTS)], ACT.Gelu)


def spiking(c):
    nc = c.nc
    NK, S3 = len(KT), T // 3
    with ExitStack() as ctx:
        wT = c.sb(ctx, "sp_wT", [DH + 1, 4, 2, D])
        qs = c.sb(ctx, "q_spikes", [DH, 2, NT], F16)
        ks = c.sb(ctx, "k_spikes", [128, BATCH, NK, D], F16)
        vs = c.sb(ctx, "v_spikes", [128, BATCH, NK, D], F16)
        kv = c.sb(ctx, "kv_counts", [DH, BATCH, 2, DH], F16)
        x3 = c.sb(ctx, "xa_spikes", [DH + 1, 2, NT])
        with ExitStack() as early:
            wr = c.sb(early, "sp_rows", [DH, 4, 2, D])
            pc = c.sb(early, "sp_cols", [DH, 4, 4, 2])
            prow = c.sb(early, "sp_prow", [DH + 1, 7, 4 * D])
            pr = prow[DH:DH + 1]
            w_in, var_r, sq_r, own_s = c.sem("sp_in"), c.sem("sp_var"), c.sem("sp_sqrt"), c.sem("sp_own")
            scaled, tp, placed = c.sem("sp_scaled"), c.sem("sp_turned"), c.sem("sp_placed")
            with nc.Block() as block:
                @block.sync
                def _(sp):
                    for w in range(4):
                        sp.dma_start(wr[:, w, :, :], c.ins["L1_attn_W"][w].rearrange("(a p) n -> p a n", p=DH)
                                     ).then_inc(w_in, 16)
                        for k, n in enumerate(("bn_gamma", "bn_var")):
                            sp.dma_start(pc[:, k, w, :], c.ins["L1_attn_" + n][w].rearrange("(a p) -> p a", p=DH),
                                         allow_slow_non_contiguous=True).then_inc(w_in, 16)
                    for k, n in enumerate(("b", "bn_gamma", "bn_beta", "bn_mean", "bn_var")):
                        sp.dma_start(pr[:, k, :], c.ins["L1_attn_" + n].rearrange("w n -> (w n)").rearrange(
                            "(a n) -> a n", a=1)).then_inc(w_in, 16)

                @block.scalar
                def _(act):
                    act.wait_ge(var_r, 2)
                    act.activation(pc[:, 2, :, :], pc[:, 1, :, :], ACT.Sqrt).then_inc(sq_r, 1)
                    act.activation(pr[:, 5, :], pr[:, 4, :], ACT.Sqrt).then_inc(sq_r, 1)

                @block.vector
                def _(dve):
                    own = Own(dve, own_s)
                    dve.wait_ge(w_in, 16 * 17)
                    dve.tensor_scalar(pc[:, 1, :, :], pc[:, 1, :, :], 1e-5, None, ALU.add).then_inc(var_r, 1)
                    dve.tensor_scalar(pr[:, 4, :], pr[:, 4, :], 1e-5, None, ALU.add).then_inc(var_r, 1)
                    dve.wait_ge(sq_r, 2)
                    own.did(dve.reciprocal(pc[:, 3, :, :], pc[:, 2, :, :]))
                    own.did(dve.reciprocal(pr[:, 6, :], pr[:, 5, :]))
                    own.wait()
                    own.did(dve.tensor_tensor(pc[:, 3, :, :], pc[:, 3, :, :], pc[:, 0, :, :], ALU.mult))
                    own.did(dve.tensor_tensor(pr[:, 6, :], pr[:, 6, :], pr[:, 1, :], ALU.mult))
                    own.did(dve.tensor_tensor(pr[:, 0, :], pr[:, 0, :], pr[:, 3, :], ALU.subtract))
                    own.wait()
                    own.did(dve.tensor_tensor(pr[:, 0, :], pr[:, 0, :], pr[:, 6, :], ALU.mult))
                    own.wait()
                    own.did(dve.tensor_tensor(wT[DH:DH + 1, :, 1, :], pr[:, 0, :].rearrange("p (w n) -> p w n", w=4),
                                              pr[:, 2, :].rearrange("p (w n) -> p w n", w=4), ALU.add))
                    for w in range(4):
                        for a in range(2):
                            dve.tensor_scalar(wr[:, w, a, :], wr[:, w, a, :], pc[:, 3, w, a:a + 1], None, ALU.mult
                                              ).then_inc(scaled, 1)
                    for n in range(8):
                        w, o = divmod(n, 2)
                        dve.wait_ge(tp, n + 1)
                        dve.tensor_copy(wT[0:DH, w, o, :], c.bank[n][0:DH, 0:D]).then_inc(placed, 1)

                @block.tensor
                def _(pe):
                    pe.wait_ge(scaled, 8)
                    for n in range(8):
                        w, o = divmod(n, 2)
                        for a in range(2):
                            ins = pe.transpose(c.bank[n][0:DH, a * DH:(a + 1) * DH], wr[:, w, a, o * DH:(o + 1) * DH],
                                               c.const("ident", DH)[:, 0:DH])
                        ins.then_inc(tp, 1)
        kjobs = [("kv", w, b, k) for w in (1, 2) for b in range(BATCH) for k in range(NK)]
        qjobs = [("q", m, ch, 0) for m in range(2) for ch in range(NCH)]
        cjobs = [("count", b, m, 0) for b in range(BATCH) for m in range(2)]
        xjobs = [("x", b, m, s) for b in range(BATCH) for m in range(2) for s in range(3)]
        jobs = kjobs + qjobs + cjobs + xjobs
        done, spiked, x3_ones = c.sem("sp_done"), c.sem("sp_spiked"), c.sem("sp_ones")
        with nc.Block() as block:
            @block.tensor
            def _(pe):
                for n, (kind, a, b, k) in enumerate(jobs):
                    if n >= 8:
                        pe.wait_ge(spiked, n - 7)
                    bank = c.bank[n % 8]
                    if kind == "kv":
                        k0, kn = KT[k]
                        ps = bank[0:kn, 0:D]
                        for o in range(2):
                            ins = pe.matmul(ps, c.xT[0:DH + o, o, b * T + k0:b * T + k0 + kn], wT[0:DH + o, a, o, :],
                                            start=(o == 0), stop=(o == 1))
                    elif kind == "q":
                        ps = bank[0:DH, 0:CW]
                        for o in range(2):
                            ins = pe.matmul(ps, wT[0:DH + o, 0, o, a * DH:(a + 1) * DH],
                                            c.xT[0:DH + o, o, b * CW:(b + 1) * CW], start=(o == 0), stop=(o == 1))
                    elif kind == "count":
                        if n == len(kjobs) + len(qjobs):
                            pe.wait_ge(spiked, n)
                        for j, (k0, kn) in enumerate(KT):
                            ins = pe.matmul(bank[0:DH, 0:DH], ks[0:kn, a, j, b * DH:(b + 1) * DH],
                                            vs[0:kn, a, j, b * DH:(b + 1) * DH], start=(j == 0), stop=(j == NK - 1))
                    else:
                        if n == len(jobs) - len(xjobs):
                            pe.wait_ge(spiked, n)
                        at = a * T + k * S3
                        ins = pe.matmul(bank[0:DH, 0:S3], kv[:, a, b, :], qs[:, b, at:at + S3], start=True, stop=True)
                    ins.then_inc(done, 1)

            @block.gpsimd
            def _(pool):
                pool.memset(x3[DH:DH + 1, :, :], 1.0).then_inc(x3_ones, 1)

            @block.vector
            def _(dve):
                for n, (kind, a, b, k) in enumerate(jobs):
                    dve.wait_ge(done, n + 1)
                    bank = c.bank[n % 8]
                    if kind == "kv":
                        kn = KT[k][1]
                        ins = dve.tensor_scalar((ks, vs)[a - 1][0:kn, b, k, :], bank[0:kn, 0:D], 2.0, None, ALU.is_ge)
                    elif kind == "q":
                        ins = dve.tensor_scalar(qs[:, a, b * CW:(b + 1) * CW], bank[0:DH, 0:CW], 2.0, None, ALU.is_ge)
                    elif kind == "count":
                        ins = dve.tensor_tensor(kv[:, a, b, :], bank[0:DH, 0:DH], c.const("kv", DH), ALU.mult)
                    else:
                        at = a * T + k * S3
                        ins = dve.tensor_scalar(x3[0:DH, b, at:at + S3], bank[0:DH, 0:S3], HD ** -0.125, 1.0,
                                                ALU.mult, ALU.is_ge)
                    ins.then_inc(spiked, 1)
        to_tokens(c, "sp_out", [], lambda i: [(x3[0:DH + o, o, :], wT[0:DH + o, 3, o, :]) for o in range(2)],
                  None, into=c.hN, spike=2.0)


WIDTHS = (D, D // 2, D // 3)


def small_proj(c, g, ctx, aT):
    nc = c.nc
    w = c.sb(ctx, "proj_w", [128, 2, 3, D])
    b = c.sb(ctx, "proj_b", [128, 2, D])
    w_in, own_s, zeroed = c.sem("proj_in"), c.sem("proj_own"), c.sem("proj_zeroed")
    with nc.Block() as block:
        @block.sync
        def _(sp):
            sp.wait_ge(zeroed, 1)
            for h in range(HEADS):
                r = 32 * (h % 4)
                sp.dma_start(w[r:r + HD, 0, h // 4, :], c.ins["L1_ffn_w_proj"][h * HD:(h + 1) * HD, :]
                             ).then_inc(w_in, 16)
            sp.dma_start(b[:, 0, :], c.ins["L1_ffn_b_proj"].rearrange("(a n) -> a n", a=1).broadcast_to((128, D))
                         ).then_inc(w_in, 16)

        @block.vector
        def _(dve):
            own = Own(dve, own_s)
            dve.memset(w[:, :, :, :], 0.0).then_inc(zeroed, 1)
            dve.wait_ge(w_in, 16 * (HEADS + 1))
            own.did(dve.tensor_scalar(w[:, 1, :, :], w[:, 0, :, :], g[:, 0:1], None, ALU.mult))
            own.did(dve.tensor_scalar(b[:, 1, :], b[:, 0, :], g[:, 0:1], None, ALU.mult))
            for i in (1, 2):
                n = WIDTHS[i]
                own.wait()
                for k in range((n + 63) // 64):
                    r = min(128, 2 * (n - 64 * k))
                    own.did(dve.scalar_tensor_tensor(w[0:r, 1, k, 0:n], w[0:r, 0, k, 0:n], g[0:r, i:i + 1],
                                                     w[0:r, 1, k, 0:n], ALU.mult, ALU.add))
                own.did(dve.scalar_tensor_tensor(b[:, 1, 0:n], b[:, 0, 0:n], g[:, i:i + 1],
                                                 b[:, 1, 0:n], ALU.mult, ALU.add))
    half = NTILE // 2
    to_tokens(c, "proj", [], lambda i: [(aT[:, k, :], w[:, i // half, k, :]) for k in range(3)],
              lambda i: b[0:TT, i // half, :])


def last_mlps(c, g):
    i = c.ins
    w = dict(w1=i["L1_ffn_w_fc1"], b1=i["L1_ffn_b_fc1"], w2=i["L1_ffn_w_fc2"], b2=i["L1_ffn_b_fc2"])
    parts = [[(0, DH), (1, DH)], [(0, WIDTHS[1])], [(0, WIDTHS[2])]]
    variants = [dict(w, parts=parts[0], n=D, gain=None, chunks=range(NCH // 2))]
    for k in range(3):
        variants.append(dict(w, parts=parts[k], n=WIDTHS[k], gain=lambda t, k=k: g[0:TT, k:k + 1],
                             chunks=range(NCH // 2, NCH)))
    mlps(c, "last", variants, ACT.Gelu)


def write_out(c, out):
    nc = c.nc
    summed, stored = c.sem("out_summed"), c.stored
    with nc.Block() as block:
        @block.vector
        def _(dve):
            for k in range(3):
                s = slice(6 * k, 6 * k + 6)
                dve.tensor_tensor(c.hN[0:TT, s, :], c.hN[0:TT, s, :], c.xN[0:TT, s, :], ALU.add).then_inc(summed, 1)

        @block.sync
        def _(sp):
            view = out.rearrange("b t d -> (b t) d").rearrange("(i p) d -> p i d", p=TT)
            for k in range(3):
                s = slice(6 * k, 6 * k + 6)
                sp.wait_ge(summed, k + 1)
                sp.dma_start(view[:, s, :], c.hN[0:TT, s, :]).then_inc(stored, 16)
            sp.wait_ge(stored, 48)


def last_ffn(c, ctx):
    nc = c.nc
    g = c.sb(ctx, "gumbel", [128, 3])
    g_in = c.sem("gumbel_in")
    with nc.Block() as block:
        @block.sync
        def _(sp):
            sp.dma_start(g[:, :], c.ins["L1_ffn_gumbel_weights"].rearrange("(a n) -> a n", a=1).broadcast_to((128, 3))
                         ).then_inc(g_in, 16)
            sp.wait_ge(g_in, 16)
    norm(c, "n1", True, "ln", ["L1_ffn_n1l_g", "L1_ffn_n1s_g"], ["L1_ffn_n1l_b", "L1_ffn_n1s_b"])
    attention_layer(c, "att1", c.ins["L1_ffn_w_qkv"], None, lambda ctx, aT: small_proj(c, g, ctx, aT))
    norm(c, "n2", False, "ln", ["L1_ffn_n2l_g", "L1_ffn_n2s_g"], ["L1_ffn_n2l_b", "L1_ffn_n2s_b"])
    last_mlps(c, g)


def tower(nc, ins, out):
    with ExitStack() as ctx:
        c = Core(nc, ins)
        load_shared(c, ctx)
        tok_features(c)
        layer_buffers(c, ctx)
        norm(c, "mixn", True, "rms", ["L0_attn_norm1_w"])
        mixer(c)
        c.layer_end()
        norm(c, "ff0n", False, "rms", ["L0_attn_norm2_w"])
        ff0(c)
        norm(c, "att0n", True, "ln", ["L0_ffn_ln1_g"], ["L0_ffn_ln1_b"], residual=True)
        attention_layer(c, "att0", ins["L0_ffn_in_proj_w"], ins["L0_ffn_in_proj_b"],
                        lambda ctx, aT: out_proj0(c, ctx, aT))
        c.layer_end()
        norm(c, "moen", False, "ln", ["L0_ffn_ln2_g"], ["L0_ffn_ln2_b"])
        moe(c)
        c.layer_end()
        norm(c, "spn", True, None, None, residual=True)
        spiking(c)
        c.layer_end()
        last_ffn(c, ctx)
        write_out(c, out)


_INS = ['x', 'cls_tok', 'L0_tok_freq_bands', 'L0_tok_W', 'L0_attn_norm1_w', 'L0_attn_w_in', 'L0_attn_conv_w',
        'L0_attn_w_bc', 'L0_attn_D_skip', 'L0_attn_w_out', 'L0_attn_norm2_w', 'L0_attn_ff_w1', 'L0_attn_ff_b1',
        'L0_attn_ff_w2', 'L0_attn_ff_b2', 'L0_ffn_ln1_g', 'L0_ffn_ln1_b', 'L0_ffn_in_proj_w', 'L0_ffn_in_proj_b',
        'L0_ffn_out_proj_w', 'L0_ffn_out_proj_b', 'L0_ffn_ln2_g', 'L0_ffn_ln2_b', 'L0_ffn_router_w',
        'L0_ffn_router_b', 'L0_ffn_w1', 'L0_ffn_b1', 'L0_ffn_w2', 'L0_ffn_b2', 'L1_attn_W', 'L1_attn_b',
        'L1_attn_bn_gamma', 'L1_attn_bn_beta', 'L1_attn_bn_mean', 'L1_attn_bn_var', 'L1_ffn_gumbel_weights',
        'L1_ffn_n1l_g', 'L1_ffn_n1l_b', 'L1_ffn_n1s_g', 'L1_ffn_n1s_b', 'L1_ffn_w_qkv', 'L1_ffn_w_proj',
        'L1_ffn_b_proj', 'L1_ffn_n2l_g', 'L1_ffn_n2l_b', 'L1_ffn_n2s_g', 'L1_ffn_n2s_b', 'L1_ffn_w_fc1',
        'L1_ffn_b_fc1', 'L1_ffn_w_fc2', 'L1_ffn_b_fc2']


def kernel(**inputs):
    import numpy as _np
    import concourse.bacc as _bacc
    from concourse import mybir as _mybir
    from concourse.bass_utils import run_bass_kernel_spmd as _run

    nc = _bacc.Bacc("TRN2", target_bir_lowering=False, num_devices=1)
    arrays, ins = {}, {}
    for name in _INS + ["consts"]:
        a = CONSTANTS if name == "consts" else _np.ascontiguousarray(inputs[name])
        arrays[f"in_{name}_dram"] = a
        ins[name] = nc.dram_tensor(f"in_{name}_dram", a.shape, _mybir.dt.from_np(a.dtype), kind="ExternalInput").ap()
    out = nc.dram_tensor("out_0_dram", (BATCH, T, D), F32, kind="ExternalOutput").ap()
    tower(nc, ins, out)
    r = _run(nc, [arrays], core_ids=[0])
    return r.results[0]["out_0_dram"]
```

```python
from contextlib import ExitStack

import numpy as np

import concourse.bass as bass
from concourse import mybir

ALU = mybir.AluOpType
ACT = mybir.ActivationFunctionType
F32 = mybir.dt.float32
F16 = mybir.dt.float16
I32 = mybir.dt.int32
X = mybir.AxisListType.X

BATCH, SEQ, D = 4, 512, 192
T = SEQ + 1
NT = BATCH * T
TT = 114
NTILE = NT // TT
CW = 3 * TT
NCH = NT // CW
DH = D // 2
NW = SEQ * 3 * D * BATCH // (BATCH * SEQ)
NB2 = 12
HEADS, HD = 12, 16
FF = 4 * D
NF = FF // 128
EXPERTS = 8
DIN, SH, ST, SP = 384, 6, 8, 64
L = 57
NC1 = T // L
NBC = NT // L
LANES = NBC * SH // 2
KT = [(k * TT, min(TT, T - k * TT)) for k in range((T + TT - 1) // TT)]
W_SCALE = 64.0
MAGIC = 12582912.0
TWO_PI = 6.283185
HALF_PI = 1.5707963

CONST = {}


def _constants():
    p = np.arange(128)
    parts = [("ident", np.eye(128))]
    row_h, row_z, row_n = p // 16, (p // 8) % 2, p % 8
    parts.append(("bd", row_h[:, None] % 2 == (p // SP)[None]))
    q = np.arange(96)
    swap = np.zeros((128, 96))
    swap[q, (q // 16) * 16 + (1 - (q // 8) % 2) * 8 + q % 8] = 1
    parts.append(("swap", swap))
    parts.append(("h48", (p // 8)[:, None] == np.arange(SH)[None]))
    for z in range(2):
        parts.append((f"sel{z}", ((p % SH)[:, None] == (q // 16)[None]) & (((q // 8) % 2) == z)[None]))
    parts.append(("bc", (p // SH)[:, None] == np.arange(NBC // 2)[None]))
    parts.append(("kv", (p // HD)[:, None] == (q // HD)[None]))
    parts.append(("rank", np.broadcast_to(EXPERTS - np.arange(EXPERTS), (128, EXPERTS))))
    at, cols = 0, []
    for name, a in parts:
        CONST[name] = (at, a.shape[1])
        at += a.shape[1]
        cols.append(np.asarray(a, np.float32))
    return np.ascontiguousarray(np.concatenate(cols, 1))


CONSTANTS = _constants()


class Own:

    def __init__(self, eng, sem):
        self.eng, self.sem, self.n = eng, sem, 0

    def did(self, ins):
        self.n += 1
        ins.then_inc(self.sem, 1)
        return ins

    def wait(self, but=0):
        if self.n > but:
            self.eng.wait_ge(self.sem, self.n - but)


class Core:

    def __init__(self, nc, ins):
        self.nc, self.ins, self.sems = nc, ins, []
        self.stored = nc.alloc_semaphore("out_stored")
        self.pair = [nc.alloc_psum_tensor(f"banks{2 * i}{2 * i + 1}", [128, 1024], F32) for i in range(4)]
        self.bank = [self.pair[i // 2][:, i % 2 * 512:(i % 2 + 1) * 512] for i in range(8)]

    def sem(self, name):
        self.sems.append(self.nc.alloc_semaphore(name))
        return self.sems[-1]

    def layer_end(self):
        self.nc.all_engine_barrier()
        self.nc.clear_and_free_semaphores(self.sems)
        self.nc.all_engine_barrier()
        self.sems = []

    def sb(self, ctx, name, shape, dt=F32):
        return ctx.enter_context(self.nc.sbuf_tensor(name, shape, dt))

    def const(self, name, rows=128):
        at, n = CONST[name]
        return self.consts[0:rows, at:at + n]


def bc(ap, shape):
    return ap.broadcast_to(shape)


def load_shared(c, out_ctx):
    nc = c.nc
    c.consts = c.sb(out_ctx, "consts", [128, CONSTANTS.shape[1]])
    c.ones = c.sb(out_ctx, "ones", [128, 512])
    c.hN = c.sb(out_ctx, "hN", [128, NTILE, D])
    loaded, ones_set = c.sem("consts_loaded"), c.sem("ones_set")
    with nc.Block() as block:
        @block.sync
        def _(sp):
            sp.dma_start(c.consts[:, :], c.ins["consts"]).then_inc(loaded, 16)
            sp.wait_ge(loaded, 16)

        @block.vector
        def _(dve):
            dve.memset(c.ones[:, :], 1.0).then_inc(ones_set, 1)
            dve.wait_ge(ones_set, 1)


def layer_buffers(c, ctx):
    c.xN = c.sb(ctx, "xN", [128, NTILE, D])
    c.xT = c.sb(ctx, "xT", [128, 2, NT])
    ones_row = c.sem("ones_row")
    with c.nc.Block() as block:
        @block.vector
        def _(dve):
            dve.memset(c.xT[DH:DH + 1, :, :], 1.0).then_inc(ones_row, 1)


def tok_features(c):
    nc = c.nc
    NCC = 5
    REST = NW % 128
    CC = [(k * 128, min(128, NW - k * 128)) for k in range(NCC)]
    HALF = NT // 2
    with ExitStack() as ctx:
        wT = c.sb(ctx, "tok_wT", [128, 2, NCC, NB2, D], F16)
        rT = c.sb(ctx, "raw_T", [128, NCC, NT])
        freq = c.sb(ctx, "freq", [128, 9])
        with ExitStack() as early:
            w = c.sb(early, "tok_w", [DH, 2, NW * NB2])
            raw = c.sb(early, "raw", [128, 4, 4, NW])
            w_in, f_in = [c.sem(f"tok_w_in{k}") for k in range(NCC)], c.sem("freq_in")
            raw_in = [c.sem(f"raw_in{b}") for b in range(BATCH)]
            tp, ev = c.sem("tok_transposed"), [c.sem("tok_copied_v"), c.sem("tok_copied_s")]
            zero_set = c.sem("cls_columns_zeroed")
            loads = [x for k in range(NCC) for x in [("w", k)] + ([("raw", k)] if k < BATCH else [])]
            jobs = []
            for kind, a in loads:
                if kind == "raw":
                    jobs += [("raw", a, k, n) for k, (c0, n) in enumerate(CC)]
                else:
                    jobs += [("w", a, f, CC[a][1]) for f in range(0, NB2, 2)]
            kind_of = [job[0] for job in jobs]

            def read_out(n):
                if kind_of[n] == "w":
                    return ev[0], 2 * kind_of[:n + 1].count("w")
                return ev[1], kind_of[:n + 1].count("raw")

            with nc.Block() as block:
                @block.sync
                def _(sp):
                    for kind, a in loads:
                        if kind == "raw":
                            sp.dma_start(raw[:, a, :, :], c.ins["x"][a].rearrange("c n d -> (c n d)").rearrange(
                                "(i p w) -> p i w", p=128, w=NW)).then_inc(raw_in[a], 16)
                        else:
                            cols = slice(CC[a][0] * NB2, (CC[a][0] + CC[a][1]) * NB2)
                            sp.dma_start(w[:, :, cols], c.ins["L0_tok_W"].rearrange("(o p) f -> p o f", p=DH)[:, :, cols]
                                         ).then_inc(w_in[a], 16)
                    bands = c.ins["L0_tok_freq_bands"].rearrange("(a n) -> a n", a=1)
                    sp.dma_start(freq[:, 0:6], bands.broadcast_to((128, 6))).then_inc(f_in, 16)
                    for e in range(2):
                        sp.dma_start(freq[e * REST:(e + 1) * REST, 6:9],
                                     c.ins["L0_tok_freq_bands"].rearrange("(n e) -> e n", e=2)[e:e + 1, :]
                                     .broadcast_to((REST, 3)), allow_slow_non_contiguous=True).then_inc(f_in, 16)
                    sp.wait_ge(f_in, 48)

                @block.tensor
                def _(pe):
                    idn = c.const("ident")
                    for n, (kind, a, k, m) in enumerate(jobs):
                        if n >= 8:
                            pe.wait_ge(*read_out(n - 8))
                        bank = c.bank[n % 8]
                        if kind == "raw":
                            if k == 0:
                                pe.wait_ge(raw_in[a], 16)
                            c0 = CC[k][0]
                            for i in range(4):
                                src = raw[:, a, i, c0:c0 + m]
                                ins = pe.transpose(bank[0:m, i * 128:(i + 1) * 128], src, idn)
                                if m < 128:
                                    ins = pe.matmul(bank[m:2 * m, i * 128:(i + 1) * 128], src, idn,
                                                    start=True, stop=True)
                        else:
                            if k == 0:
                                pe.wait_ge(w_in[a], 16)
                            c0 = CC[a][0]
                            for f in range(2):
                                for o in range(2):
                                    s = c0 * NB2 + k + f
                                    src = w[:, o, s:s + (m - 1) * NB2 + 1:NB2]
                                    idw = c.const("ident", DH)[:, 0:DH]
                                    if m == 128:
                                        ins = pe.transpose(bank[:, (f * 2 + o) * DH:(f * 2 + o + 1) * DH], src, idw)
                                    elif f == 0:
                                        ins = pe.transpose(bank[0:m, o * DH:(o + 1) * DH], src, idw)
                                    else:
                                        ins = pe.matmul(bank[m:2 * m, o * DH:(o + 1) * DH], src, idw,
                                                        start=True, stop=True)
                        ins.then_inc(tp, 1)

                @block.vector
                def _(dve):
                    for b in range(BATCH):
                        dve.memset(rT[:, :, b * T:b * T + 1], 0.0).then_inc(zero_set, 1)
                    count = 0
                    for n, (kind, a, f, m) in enumerate(jobs):
                        if kind == "raw":
                            continue
                        dve.wait_ge(tp, n + 1)
                        k = 2 if m == 128 else 1
                        src = c.bank[n % 8][:, 0:k * D]
                        high, low = (wT[:, z, a, f:f + k, :].rearrange("p f d -> p (f d)") for z in range(2))
                        dve.tensor_scalar(high, src, W_SCALE, None, ALU.mult).then_inc(ev[0], 1)
                        count += 1
                        dve.wait_ge(ev[0], count)
                        dve.scalar_tensor_tensor(low, src, W_SCALE, high, ALU.mult, ALU.subtract).then_inc(ev[0], 1)
                        count += 1

                @block.scalar
                def _(act):
                    for n, (kind, b, k, m) in enumerate(jobs):
                        if kind == "w":
                            continue
                        act.wait_ge(tp, n + 1)
                        act.copy(rT[:, k, b * T + 1:(b + 1) * T], c.bank[n % 8][:, :]).then_inc(ev[1], 1)

        fy = c.sb(ctx, "angle", [128, HALF])
        fm = c.sb(ctx, "angle_rounded", [128, HALF])
        fr = c.sb(ctx, "angle_rest", [128, 2, HALF])
        fa = c.sb(ctx, "angle_abs", [128, 2, HALF])
        feat = c.sb(ctx, "features", [128, 2, 2, HALF])
        fh = c.sb(ctx, "feature_halves", [128, 2, 2, 2, HALF], F16)
        halfpi = c.sb(ctx, "half_pi", [128, 1])
        vown = c.sem("tok_v_own")
        rest, used = c.sem("angle_ready"), c.sem("angle_used")
        fhigh, flow, fused = c.sem("features_high"), [c.sem("sines_low"), c.sem("cosines_low")], c.sem("features_used")
        accd, out_v, cls_in = c.sem("tok_accumulated"), c.sem("tok_h_written"), c.sem("cls_in")
        steps = [(hf, k, f, wf) for hf in range(2)
                 for k, f, wf in [(k, f, f) for k in range(NCC - 1) for f in range(6)]
                 + [(NCC - 1, 6 + p, 2 * p) for p in range(3)]]
        per = len(steps) // 2
        with nc.Block() as block:
            def low_part(eng, n, q):
                eng.wait_ge(fhigh, n + 1)
                s = n % 2
                eng.tensor_tensor(fh[:, s, q, 1, :], feat[:, s, q, :], fh[:, s, q, 0, :], ALU.subtract
                                  ).then_inc(flow[q], 1)

            @block.vector
            def _(dve):
                own = Own(dve, vown)
                own.did(dve.memset(halfpi[:, :], HALF_PI))

                def write_h(hf):
                    dve.wait_ge(accd, hf + 1)
                    for t in range(9):
                        dve.tensor_scalar(c.hN[0:TT, hf * 9 + t, :], c.bank[t // 2][0:TT, (t % 2) * D:(t % 2 + 1) * D],
                                          1.0 / W_SCALE, None, ALU.mult).then_inc(out_v, 1)

                for n, (hf, k, f, wf) in enumerate(steps):
                    m, s = 128, n % 2
                    src = rT[0:m, k, hf * HALF:(hf + 1) * HALF]
                    own.did(dve.tensor_scalar(fy[0:m, :], src, freq[0:m, f:f + 1], None, ALU.mult))
                    own.wait()
                    own.did(dve.tensor_scalar(fm[0:m, :], fy[0:m, :], MAGIC, MAGIC, ALU.add, ALU.subtract))
                    own.wait()
                    if n >= 2:
                        dve.wait_ge(used, 2 * (n - 1))
                    own.did(dve.tensor_tensor(fr[0:m, s, :], fy[0:m, :], fm[0:m, :], ALU.subtract))
                    own.wait()
                    dve.tensor_scalar(fa[:, s, :].bitcast(I32), fr[:, s, :].bitcast(I32), 0x7fffffff, None,
                                      ALU.bitwise_and).then_inc(rest, 1)
                    if n:
                        low_part(dve, n - 1, 1)
                    if n == per:
                        write_h(0)
                low_part(dve, len(steps) - 1, 1)
                write_h(1)

            @block.scalar
            def _(act):
                def high_parts(n):
                    s = n % 2
                    act.wait_ge(used, 2 * n + 2)
                    if n >= 2:
                        act.wait_ge(fused, n - 1)
                    act.copy(fh[:, s, :, 0, :], feat[:, s, :, :]).then_inc(fhigh, 1)

                for n in range(len(steps)):
                    s = n % 2
                    act.wait_ge(rest, n + 1)
                    if n >= 2:
                        for q in range(2):
                            act.wait_ge(flow[q], n - 1)
                    act.activation(feat[:, s, 0, :], fr[:, s, :], ACT.Sin, scale=TWO_PI).then_inc(used, 1)
                    act.activation(feat[:, s, 1, :], fa[:, s, :], ACT.Sin, bias=halfpi[:, :],
                                   scale=-TWO_PI).then_inc(used, 1)
                    high_parts(n)

            @block.gpsimd
            def _(pool):
                for n in range(len(steps)):
                    low_part(pool, n, 0)

            @block.tensor
            def _(pe):
                for n, (hf, k, f, wf) in enumerate(steps):
                    s = n % 2
                    pe.wait_ge(fhigh, n + 1)
                    if n == per:
                        pe.wait_ge(out_v, 9)
                    for z, y in ((0, 0), (0, 1), (1, 0)):
                        for q in range(2):
                            if z:
                                pe.wait_ge(flow[q], n + 1)
                            for t in range(9):
                                ins = pe.matmul(c.bank[t // 2][0:TT, (t % 2) * D:(t % 2 + 1) * D],
                                                fh[:, s, q, z, t * TT:(t + 1) * TT], wT[:, y, k, 6 * q + wf, :],
                                                start=(n % per == 0 and q == z == y == 0 and t % 2 == 0),
                                                stop=(n % per == per - 1 and q == z == 1), skip_group_check=True)
                    ins.then_inc(fused, 1)
                    if n % per == per - 1:
                        pe.matmul(c.bank[7][0:1, 0:1], c.ones[0:1, 0:1], c.ones[0:1, 0:1],
                                  start=True, stop=True).then_inc(accd, 1)

            @block.sync
            def _(sp):
                sp.wait_ge(out_v, 18)
                for b in range(BATCH):
                    t, r = divmod(b * T, TT)
                    sp.dma_start(c.hN[r:r + 1, t, :], c.ins["cls_tok"][0]).then_inc(cls_in, 16)
                sp.wait_ge(cls_in, 16 * BATCH)


def stats(dve, own, c, src, st, mv):
    for i in range(NTILE):
        own.did(dve.bn_stats(st[0:TT, i, :], src[0:TT, i, :]))
    own.wait()
    for i in range(NTILE):
        own.did(dve.bn_aggr(mv[0:TT, i, :], st[0:TT, i, :]))
    own.wait()


class Split:

    def __init__(self, c, ctx, name):
        self.x = c.sb(ctx, name + "_x", [128, 2, NT])
        self.h = c.sb(ctx, name + "_halves", [128, 4, NT], F16)


ALL_TERMS = [(0, 0, 128), (1, 1, 128), (2, 0, 128), (0, 2, 128), (1, 3, 64)]


def first_terms(rows):
    return [(0, 0, rows), (2, 0, rows), (0, 2, rows)]


def norm(c, name, outer, kind, gains, biases=None, residual=False, split=None):
    nc = c.nc
    with ExitStack() as ctx:
        st = c.sb(ctx, name + "_st", [128, NTILE, 6])
        mv = c.sb(ctx, name + "_mv", [128, NTILE, 2])
        ve = c.sb(ctx, name + "_ve", [128, NTILE])
        sd = c.sb(ctx, name + "_sd", [128, NTILE])
        rs = c.sb(ctx, name + "_rs", [128, NTILE])
        yN = c.sb(ctx, name + "_yN", [128, NTILE, D])
        gb = c.sb(ctx, name + "_gb", [128, 4, 2])
        own_s, gb_in = c.sem(name + "_v_own"), c.sem(name + "_gains_in")
        var_ready, sd_ready, y_ready = c.sem(name + "_var"), c.sem(name + "_sqrt"), c.sem(name + "_normed")
        tp, ev = c.sem(name + "_transposed"), [c.sem(name + "_cp_v"), c.sem(name + "_cp_s")]
        n_dma = len(gains or []) + len(biases or [])
        halves = len(gains) if gains else 1
        src = yN if kind else c.xN
        passes = int(outer) + (kind is not None)
        both = bool(outer and kind)
        sc = c.sb(ctx, name + "_sc", [128, 2, NTILE])
        shift_ready, x_ready = c.sem(name + "_shift"), c.sem(name + "_x_ready")
        if split:
            spans = [[(0, 0, 128)], [(0, 128, 64), (64, 128, 64)]]
        else:
            spans = [[(0, 0, DH)], [(0, DH, DH)]]
        n_dma *= sum(map(len, spans))
        rows = 128 if split else DH
        high, low = c.sem(name + "_high"), [c.sem(name + "_low_v"), c.sem(name + "_low_p")]
        out = split.x if split else c.xT
        with nc.Block() as block:
            @block.sync
            def _(sp):
                for i, g in enumerate((gains or []) + (biases or [])):
                    at = i if i < halves else 2 + i - halves
                    for o in range(2):
                        for p0, c0, k in spans[o]:
                            sp.dma_start(gb[p0:p0 + k, at, o:o + 1], c.ins[g][c0:c0 + k].rearrange("(p a) -> p a", a=1),
                                         allow_slow_non_contiguous=True).then_inc(gb_in, 16)
                if n_dma:
                    sp.wait_ge(gb_in, 16 * n_dma)

            def copy_out(eng, par):
                if n_dma:
                    eng.wait_ge(gb_in, 16 * n_dma)
                for n in range(2 * NCH):
                    if n % 2 != par:
                        continue
                    ch, o = divmod(n, 2)
                    if split and par == 0 and ch:
                        low_part(eng, ch - 1, 0)
                    half = 1 if halves == 2 and ch >= NCH // 2 else 0
                    eng.wait_ge(tp, n + 1)
                    dst, ps = out[0:rows, o, ch * CW:(ch + 1) * CW], c.bank[n % 8][0:rows, 0:CW]
                    g, b = gb[0:rows, half, o:o + 1], gb[0:rows, 2 + half, o:o + 1]
                    if par == 0:
                        if not gains:
                            ins = eng.tensor_copy(dst, ps)
                        elif biases:
                            ins = eng.tensor_scalar(dst, ps, g, b, ALU.mult, ALU.add)
                        else:
                            ins = eng.tensor_scalar(dst, ps, g, None, ALU.mult)
                    else:
                        if not gains:
                            ins = eng.activation(dst, ps, ACT.Copy)
                        elif biases:
                            ins = eng.activation(dst, ps, ACT.Identity, bias=b, scale=g)
                        else:
                            ins = eng.activation(dst, ps, ACT.Copy, scale=g)
                    ins.then_inc(ev[par], 1)
                    if split and par == 1:
                        eng.wait_ge(ev[0], ch + 1)
                        eng.wait_ge(ev[1], ch + 1)
                        cols = slice(ch * CW, (ch + 1) * CW)
                        eng.copy(split.h[:, 0:2, cols], split.x[:, :, cols]).then_inc(high, 1)

            def low_part(eng, ch, o):
                eng.wait_ge(high, ch + 1)
                cols, r = slice(ch * CW, (ch + 1) * CW), (128, 64)[o]
                eng.tensor_tensor(split.h[0:r, 2 + o, cols], split.x[0:r, o, cols], split.h[0:r, o, cols],
                                  ALU.subtract).then_inc(low[o], 1)

            @block.gpsimd
            def _(pool):
                if split:
                    for ch in range(NCH):
                        low_part(pool, ch, 1)

            @block.vector
            def _(dve):
                own = Own(dve, own_s)
                done = 0

                def rstd(e):
                    nonlocal done
                    dve.tensor_scalar(ve[0:TT, :], var, e, None, ALU.add).then_inc(var_ready, 1)
                    done += 1
                    dve.wait_ge(sd_ready, done)
                    own.did(dve.reciprocal(rs[0:TT, :], sd[0:TT, :]))
                    own.wait()

                if residual:
                    own.did(dve.tensor_tensor(c.hN[0:TT, :, :], c.hN[0:TT, :, :], c.xN[0:TT, :, :], ALU.add))
                    own.wait()
                if outer:
                    stats(dve, own, c, c.hN, st, mv)
                    mean, var = mv[0:TT, :, 0], mv[0:TT, :, 1]
                    rstd(1e-5)
                if outer and kind is None:
                    for i in range(NTILE):
                        dve.tensor_scalar(c.xN[0:TT, i, :], c.hN[0:TT, i, :], mv[0:TT, i, 0:1],
                                          rs[0:TT, i:i + 1], ALU.subtract, ALU.mult).then_inc(y_ready, 1)
                elif outer:
                    own.did(dve.tensor_copy(sc[0:TT, 0, :], rs[0:TT, :]))
                    dve.scalar_tensor_tensor(sc[0:TT, 1, :], mean, -1.0, rs[0:TT, :], ALU.mult, ALU.mult
                                             ).then_inc(shift_ready, 1)
                    own.did(dve.tensor_tensor(var, var, rs[0:TT, :], ALU.mult))
                    own.wait()
                    own.did(dve.tensor_tensor(var, var, rs[0:TT, :], ALU.mult))
                    own.wait()
                    dve.wait_ge(shift_ready, 1)
                    rstd(1e-6 if kind == "rms" else 1e-5)
                    own.did(dve.tensor_tensor(rs[0:TT, :], rs[0:TT, :], sc[0:TT, 0, :], ALU.mult))
                    own.wait()
                    for i in range(NTILE):
                        dve.tensor_scalar(yN[0:TT, i, :], c.hN[0:TT, i, :], mv[0:TT, i, 0:1],
                                          rs[0:TT, i:i + 1], ALU.subtract, ALU.mult).then_inc(y_ready, 1)
                else:
                    stats(dve, own, c, c.xN, st, mv)
                    var = mv[0:TT, :, 1]
                    if kind == "rms":
                        own.did(dve.tensor_tensor(ve[0:TT, :], mv[0:TT, :, 0], mv[0:TT, :, 0], ALU.mult))
                        own.wait()
                        own.did(dve.tensor_tensor(mv[0:TT, :, 1], ve[0:TT, :], mv[0:TT, :, 1], ALU.add))
                        own.wait()
                    rstd(1e-6 if kind == "rms" else 1e-5)
                    for i in range(NTILE):
                        if kind == "rms":
                            ins = dve.tensor_scalar(yN[0:TT, i, :], c.xN[0:TT, i, :], rs[0:TT, i:i + 1], None,
                                                    ALU.mult)
                        else:
                            ins = dve.tensor_scalar(yN[0:TT, i, :], c.xN[0:TT, i, :], mv[0:TT, i, 0:1],
                                                    rs[0:TT, i:i + 1], ALU.subtract, ALU.mult)
                        ins.then_inc(y_ready, 1)
                copy_out(dve, 0)
                if split:
                    low_part(dve, NCH - 1, 0)

            @block.scalar
            def _(act):
                for i in range(passes):
                    act.wait_ge(var_ready, i + 1)
                    act.activation(sd[0:TT, :], ve[0:TT, :], ACT.Sqrt).then_inc(sd_ready, 1)
                if both:
                    act.wait_ge(shift_ready, 1)
                    for i in range(NTILE):
                        act.activation(c.xN[0:TT, i, :], c.hN[0:TT, i, :], ACT.Identity, bias=sc[0:TT, 1, i:i + 1],
                                       scale=sc[0:TT, 0, i:i + 1]).then_inc(x_ready, 1)
                copy_out(act, 1)

            @block.tensor
            def _(pe):
                for n in range(2 * NCH):
                    ch, o = divmod(n, 2)
                    if n >= 8:
                        pe.wait_ge(ev[n % 2], (n - 8) // 2 + 1)
                    pe.wait_ge(y_ready, 3 * ch + 3)
                    for i in range(3):
                        for p0, c0, k in spans[o]:
                            ps = c.bank[n % 8][p0:p0 + k, i * TT:(i + 1) * TT]
                            y, idn = src[0:TT, 3 * ch + i, c0:c0 + k], c.const("ident", TT)[:, 0:TT]
                            ins = pe.matmul(ps, y, idn, start=True, stop=True) if p0 else pe.transpose(ps, y, idn)
                    ins.then_inc(tp, 1)


def mixer(c):
    with ExitStack() as ctx:
        sg = c.sb(ctx, "gate_silu", [128, 3, NT])
        vT = c.sb(ctx, "u_T", [128, 3, NT])
        coef = c.sb(ctx, "coef", [128, 3, 2, L])
        mixer_project(c, sg, vT, coef)
        gs = c.sb(ctx, "G_s", [128, L, 2 * LANES])
        ab = c.sb(ctx, "start_resp", [128, 2, 2 * LANES])
        zx = c.sb(ctx, "end_resp", [128, 2 * LANES])
        de = c.sb(ctx, "end_trans", [96, 2, NBC])
        raw = c.sb(ctx, "bc_raw", [L, NBC * 96])
        with ExitStack() as inner:
            mixer_responses(c, inner, coef, gs, ab, zx, de, vT, raw)
        acT = c.sb(ctx, "C_start_T", [96, NT])
        place = [c.xT[:, o, :].bitcast(F16) for o in range(2)]
        half = Halves()
        half.b = place[0][0:112, 0:NT]
        half.ch = place[0][0:112, NT:2 * NT]
        half.cl = place[1][0:48, 0:NT]
        half.spare = place[1][0:48, NT:2 * NT]
        half.wh = c.sb(ctx, "B_end_high", [128, NBC * 96], F16)
        half.wl = c.sb(ctx, "B_end_low", [L, NBC * 96], F16)
        with ExitStack() as inner:
            mixer_bc(c, inner, raw, gs, ab, zx, acT, half)
        with ExitStack() as inner:
            mixer_chain(c, inner, sg, vT, gs, acT, half, de)
        with ExitStack() as inner:
            w = c.sb(inner, "mix_wout", [128, 3, D])
            to_tokens(c, "mixout", [(w[:, :, :], c.ins["L0_attn_w_out"].rearrange("(k p) n -> p k n", p=128))],
                      lambda i: [(sg[:, k, :], w[:, k, :]) for k in range(3)], None)


def to_tokens(c, name, loads, terms, row, into=None, spike=None):
    nc = c.nc
    into = c.xN if into is None else into
    w_in, done, added = c.sem(name + "_w_in"), c.sem(name + "_done"), c.sem(name + "_added")
    biased = c.sem(name + "_biased")
    with nc.Block() as block:
        @block.sync
        def _(sp):
            for dst, src in loads:
                sp.dma_start(dst, src).then_inc(w_in, 16)

        @block.gpsimd
        def _(pool):
            if row is not None:
                for i in range(NTILE):
                    pool.tensor_tensor(into[0:TT, i, :], into[0:TT, i, :], row(i), ALU.add).then_inc(biased, 1)

        @block.tensor
        def _(pe):
            if loads:
                pe.wait_ge(w_in, 16 * len(loads))
            for i in range(NTILE):
                if i >= 8:
                    pe.wait_ge(added, i - 7)
                ps = c.bank[i % 8][0:TT, 0:D]
                for k, (a, w) in enumerate(terms(i)):
                    ins = pe.matmul(ps, a[:, i * TT:(i + 1) * TT], w, start=(k == 0), stop=(k == len(terms(i)) - 1))
                ins.then_inc(done, 1)

        @block.vector
        def _(dve):
            for i in range(NTILE):
                dve.wait_ge(done, i + 1)
                if row is not None:
                    dve.wait_ge(biased, i + 1)
                ps, x = c.bank[i % 8][0:TT, 0:D], into[0:TT, i, :]
                if spike is None:
                    ins = dve.tensor_tensor(x, ps, x, ALU.add)
                else:
                    ins = dve.scalar_tensor_tensor(x, ps, spike, x, ALU.is_ge, ALU.add)
                ins.then_inc(added, 1)


def mixer_project(c, sg, vT, coef):
    nc = c.nc
    PROJ = 2 * DIN + 2 * SH
    S3 = T // 3
    with ExitStack() as ctx:
        vpad = c.sb(ctx, "v_padded", [128, 3, BATCH, T + 3])
        w = c.sb(ctx, "mix_win", [DH, 2, PROJ])
        cw = c.sb(ctx, "conv_w", [128, 3, 4])
        par = c.sb(ctx, "params", [128, NBC * SH, 2])
        q3 = c.sb(ctx, "lane_values", [128, 3, NBC * SH])
        tmp = c.sb(ctx, "param_tmp", [128, 4, NBC * SH])
        w_in, cw_in = c.sem("mix_w_in"), c.sem("conv_w_in")
        proj, ev = c.sem("mix_projected"), [c.sem("mix_v_copied"), c.sem("mix_gate_done")]
        pad0, own_s, conv = c.sem("v_pad_zeroed"), c.sem("mixp_v_own"), c.sem("convolved")
        pdone, pcopy, a1, a2 = c.sem("params_done"), c.sem("params_copied"), c.sem("params_act"), c.sem("params_max")
        qs, qt, silu = c.sem("lane_ready"), c.sem("lane_transposed"), c.sem("u_done")
        jobs = [(g, m, b, s) for m in range(3) for b in range(BATCH) for s in range(3) for g in (1, 0)]
        with nc.Block() as block:
            @block.sync
            def _(sp):
                sp.dma_start(w[:, :, :], c.ins["L0_attn_w_in"].rearrange("(o p) n -> p o n", p=DH)).then_inc(w_in, 16)
                sp.dma_start(cw[:, :, :], c.ins["L0_attn_conv_w"].rearrange("(k p) t -> p k t", p=128)
                             ).then_inc(cw_in, 16)

            @block.tensor
            def _(pe):
                pe.wait_ge(w_in, 16)
                for i in range(NBC):
                    for o in range(2):
                        ins = pe.matmul(c.bank[7][0:L, i * 2 * SH:(i + 1) * 2 * SH],
                                        c.xT[0:DH, o, i * L:(i + 1) * L], w[:, o, 2 * DIN:PROJ],
                                        start=(o == 0), stop=(o == 1))
                ins.then_inc(pdone, 1)
                for n, (g, m, b, s) in enumerate(jobs):
                    if n >= 6:
                        pe.wait_ge(ev[n % 2], (n - 6) // 2 + 1)
                    for o in range(2):
                        ins = pe.matmul(c.bank[n % 6][:, 0:S3], w[:, o, g * DIN + m * 128:g * DIN + (m + 1) * 128],
                                        c.xT[0:DH, o, b * T + s * S3:b * T + (s + 1) * S3],
                                        start=(o == 0), stop=(o == 1))
                    ins.then_inc(proj, 1)
                    if n == len(jobs) // 2:
                        pe.wait_ge(qs, 1)
                        for q in range(3):
                            for g2 in range(2):
                                at = (q * 2 + g2) * L
                                ins = pe.transpose(c.bank[6][0:LANES, at:at + L],
                                                   q3[0:L, q, g2 * LANES:(g2 + 1) * LANES],
                                                   c.const("ident", L)[:, 0:L])
                        ins.then_inc(qt, 1)

            @block.scalar
            def _(act):
                act.wait_ge(a2, 1)
                act.activation(tmp[0:L, 1, :], tmp[0:L, 0, :], ACT.Exp).then_inc(a1, 1)
                act.wait_ge(a1, 1)
                act.activation(tmp[0:L, 2, :], tmp[0:L, 1, :], ACT.Ln, bias=1.0).then_inc(a1, 1)
                act.activation(q3[0:L, 0, :], par[0:L, :, 1], ACT.Sigmoid).then_inc(a1, 1)

                def silu_u(i):
                    m, b = divmod(i, BATCH)
                    act.wait_ge(conv, i + 1)
                    u = vT[:, m, b * T:(b + 1) * T]
                    act.activation(u, u, ACT.Silu).then_inc(silu, 1)

                for n, (g, m, b, s) in enumerate(jobs):
                    if g == 0:
                        act.wait_ge(proj, n + 1)
                        act.activation(sg[:, m, b * T + s * S3:b * T + (s + 1) * S3], c.bank[n % 6][:, 0:S3],
                                       ACT.Silu).then_inc(ev[1], 1)
                    if (g, s) == (0, 2) and n > 5:
                        silu_u(n // 6 - 1)
                silu_u(len(jobs) // 6 - 1)

            @block.vector
            def _(dve):
                own = Own(dve, own_s)
                dve.memset(vpad[:, :, :, 0:3], 0.0).then_inc(pad0, 1)
                dve.wait_ge(pdone, 1)
                own.did(dve.tensor_copy(par[0:L, :, :].rearrange("p a b -> p (a b)"), c.bank[7][0:L, 0:2 * SH * NBC]))
                own.wait()
                a, nega, lg = par[0:L, :, 0], tmp[0:L, 0, :], tmp[0:L, 2, :]
                dve.scalar_tensor_tensor(nega, a, -1.0, a, ALU.mult, ALU.min).then_inc(a2, 1)
                own.did(dve.tensor_scalar(tmp[0:L, 3, :], a, 0.0, None, ALU.max))
                def convolve(m, b):
                    o = vT[:, m, b * T:(b + 1) * T]
                    dve.wait_ge(ev[0], 3 * (m * BATCH + b + 1))
                    own.did(dve.tensor_scalar(o, vpad[:, m, b, 0:T], cw[:, m, 0:1], None, ALU.mult))
                    for t in range(1, 4):
                        own.wait()
                        ins = dve.scalar_tensor_tensor(o, vpad[:, m, b, t:t + T], cw[:, m, t:t + 1], o,
                                                       ALU.mult, ALU.add)
                        if t < 3:
                            own.did(ins)
                        else:
                            ins.then_inc(conv, 1)

                for n, (g, m, b, s) in enumerate(jobs):
                    if g == 1:
                        dve.wait_ge(proj, n + 1)
                        dve.tensor_copy(vpad[:, m, b, 3 + s * S3:3 + (s + 1) * S3],
                                        c.bank[n % 6][:, 0:S3]).then_inc(ev[0], 1)
                        if s == 2:
                            if n < 6:
                                dve.wait_ge(cw_in, 16)
                                dve.wait_ge(pad0, 1)
                            convolve(m, b)
                    if n == 5:
                        dve.wait_ge(a1, 3)
                        own.wait()
                        A, dt, S = tmp[0:L, 3, :], q3[0:L, 0, :], q3[0:L, 1, :]
                        own.did(dve.tensor_tensor(A, A, lg, ALU.add))
                        own.did(dve.tensor_tensor(tmp[0:L, 1, :], dt, dt, ALU.mult))
                        own.wait()
                        own.did(dve.tensor_tensor(tmp[0:L, 1, :], tmp[0:L, 1, :], A, ALU.mult))
                        own.wait()
                        own.did(dve.tensor_scalar(tmp[0:L, 1, :], tmp[0:L, 1, :], 1.0, None, ALU.add))
                        own.wait()
                        own.did(dve.reciprocal(S, tmp[0:L, 1, :]))
                        own.wait()
                        own.did(dve.tensor_tensor(tmp[0:L, 1, :], S, dt, ALU.mult))
                        own.wait()
                        dve.scalar_tensor_tensor(q3[0:L, 2, :], tmp[0:L, 1, :], -1.0, A, ALU.mult,
                                                 ALU.mult).then_inc(qs, 1)
                dve.wait_ge(qt, 1)
                dve.tensor_copy(coef[0:LANES, :, :, :].rearrange("p a b c -> p (a b c)"),
                                c.bank[6][0:LANES, 0:6 * L]).then_inc(pcopy, 1)


def mixer_responses(c, ctx, coef, gs, ab, zx, de, vT, raw):
    nc = c.nc
    W = L + 2
    g = c.sb(ctx, "G", [128, 2, L, W])
    zb = c.sb(ctx, "z_state", [128, 2, W])
    zt = c.sb(ctx, "z_tmp", [128, 2, W])
    x0 = c.sb(ctx, "x_start", [128, W])
    sd = c.sb(ctx, "S_dt", [128, 2, L])
    r = c.sb(ctx, "lane_masked", [128, 2, 4, NBC // 2])
    own_s, masked = c.sem("scan_steps"), c.sem("lane_masked_ready")

    def scan_count(t):
        return 8 + 6 * (t + 1)

    tp, ev, rest_ev = c.sem("G_transposed"), c.sem("G_copied"), c.sem("resp_copied")
    P = LANES
    jobs = [(q, t0) for t0 in range(0, L, 4) for q in range(2)]
    w = c.sb(ctx, "w_bc", [128, 3, 96])
    w_in, done, moved = c.sem("w_bc_in"), c.sem("bc_done"), c.sem("bc_moved")
    per = [min(5, NBC - 5 * i) for i in range(8)]

    def bc_range(i):
        return slice(i * 480, i * 480 + per[i] * 96)

    def bc_after(n):
        return n // 3 if n % 3 == 2 and n // 3 < 8 else None

    with nc.Block() as block:
        @block.sync
        def _(sp):
            sp.dma_start(w[:, :, :], c.ins["L0_attn_w_bc"].rearrange("(k p) n -> p k n", p=128)).then_inc(w_in, 16)

        @block.vector
        def _(dve):
            own = Own(dve, own_s)
            own.did(dve.memset(g[0:P].rearrange("p a b c -> p (a b c)"), 0.0))
            own.did(dve.memset(zb[0:P, :, :], 0.0))
            own.did(dve.memset(x0[0:P, :], 0.0))
            own.did(dve.tensor_tensor(sd[0:P, :, :], coef[0:P, 0, :, :], coef[0:P, 1, :, :], ALU.mult))
            own.wait()
            own.did(dve.memset(zb[0:P, :, 0:1], 1.0))
            own.did(dve.memset(x0[0:P, 1:2], 1.0))
            for q in range(2):
                flat = g[0:P, q, :, :].rearrange("p t s -> p (t s)")
                own.did(dve.tensor_copy(flat[:, 2:(L - 1) * (W + 1) + 3:W + 1], sd[0:P, q, :]))
            own.wait()

            def prev(q, t):
                return g[0:P, q, t - 1, 0:t + 3] if t else x0[0:P, 0:3]

            for t in range(L):
                n = t + 3
                for q in range(2):
                    own.wait(1)
                    own.did(dve.scalar_tensor_tensor(zt[0:P, q, 0:n], prev(q, t), coef[0:P, 2, q, t:t + 1],
                                                     g[0:P, q, t, 0:n], ALU.mult, ALU.add))
                for q in range(2):
                    own.wait(1)
                    own.did(dve.scalar_tensor_tensor(zb[0:P, q, 0:n], zb[0:P, q, 0:n], coef[0:P, 1, q, t:t + 1],
                                                     zt[0:P, q, 0:n], ALU.mult, ALU.add))
                for q in range(2):
                    own.wait(1)
                    own.did(dve.scalar_tensor_tensor(g[0:P, q, t, 0:n], zb[0:P, q, 0:n], coef[0:P, 0, q, t:t + 1],
                                                     prev(q, t), ALU.mult, ALU.add))
                assert own.n == scan_count(t)
            own.wait()
            for q in range(2):
                vals = [zb[0:P, q, 0:1], g[0:P, q, L - 1, 1:2], g[0:P, q, L - 1, 0:1], zb[0:P, q, 1:2]]
                for j, v in enumerate(vals):
                    dve.tensor_scalar(r[0:P, q, j, :], c.const("bc", P), v, None, ALU.mult).then_inc(masked, 1)
            dve.wait_ge(tp, len(jobs) + 1)
            dve.tensor_copy(ab[0:L, :, :].rearrange("p a b -> p (a b)"), c.bank[6][0:L, 0:4 * P]).then_inc(rest_ev, 1)
            dve.wait_ge(tp, len(jobs) + 3)
            dve.tensor_copy(zx[0:L, :], c.bank[7][0:L, 0:2 * P]).then_inc(rest_ev, 1)
            dve.tensor_copy(de[:, :, :].rearrange("p a b -> p (a b)"),
                            c.bank[7][0:96, 256:256 + 2 * NBC]).then_inc(rest_ev, 1)

        @block.scalar
        def _(act):
            for n, (q, t0) in enumerate(jobs):
                k = min(4, L - t0)
                act.wait_ge(tp, n + 1)
                act.copy(gs[0:L, t0:t0 + k, q * P:(q + 1) * P],
                         c.bank[n % 6][0:L, 0:k * P].rearrange("p (a b) -> p a b", a=k)).then_inc(ev, 1)
                i = bc_after(n)
                if i is not None:
                    act.wait_ge(done, i + 1)
                    act.copy(raw[0:L, bc_range(i)], c.bank[6 + i % 2][0:L, 0:per[i] * 96]).then_inc(moved, 1)

        @block.tensor
        def _(pe):
            idn = c.const("ident", P)[:, 0:P]
            for n, (q, t0) in enumerate(jobs):
                k = min(4, L - t0)
                if n >= 6:
                    pe.wait_ge(ev, n - 5)
                pe.wait_ge(own_s, scan_count(t0 + k - 1))
                for t in range(t0, t0 + k):
                    ins = pe.transpose(c.bank[n % 6][0:L, (t - t0) * P:(t - t0 + 1) * P], g[0:P, q, t, 2:W], idn)
                ins.then_inc(tp, 1)
                i = bc_after(n)
                if i is not None:
                    if i == 0:
                        pe.wait_ge(w_in, 16)
                    if i >= 2:
                        pe.wait_ge(moved, i - 1)
                    for j in range(per[i]):
                        at = (5 * i + j) * L
                        for m in range(3):
                            ins = pe.matmul(c.bank[6 + i % 2][0:L, j * 96:(j + 1) * 96], vT[:, m, at:at + L],
                                            w[:, m, :], start=(m == 0), stop=(m == 2))
                    ins.then_inc(done, 1)
            pe.wait_ge(moved, 8)
            pe.wait_ge(ev, len(jobs))
            for z in range(2):
                for q in range(2):
                    at = (z * 2 + q) * P
                    ins = pe.transpose(c.bank[6][0:L, at:at + P], g[0:P, q, :, z], idn)
            ins.then_inc(tp, 1)
            pe.wait_ge(masked, 8)
            for q in range(2):
                ins = pe.transpose(c.bank[7][0:L, q * P:(q + 1) * P], zb[0:P, q, 2:W], idn)
            ins.then_inc(tp, 1)
            for j in range(2):
                for q in range(2):
                    at = 256 + j * NBC + q * (NBC // 2)
                    for z in range(2):
                        ins = pe.matmul(c.bank[7][0:96, at:at + NBC // 2], c.const(f"sel{z}", P), r[0:P, q, 2 * j + z, :],
                                        start=(z == 0), stop=(z == 1))
            ins.then_inc(tp, 1)


class Halves:
    pass


def mixer_bc(c, ctx, raw, gs, ab, zx, acT, half):
    nc = c.nc
    NG = NBC * SH
    bwf = raw[0:L, 0:NG * 2 * ST]
    bw = bwf.rearrange("p (a b c) -> p a b c", b=2, c=ST)
    ac = bw
    squares = c.sem("bc_squares")
    bcn = c.sb(ctx, "bc_normed", [128, 2, NG, ST])
    ss = c.sb(ctx, "bc_sumsq", [128, 2 * NG])
    sr = c.sb(ctx, "bc_norm", [128, 2 * NG])
    own_s = c.sem("bc_own")
    sm, rt, nd = c.sem("bc_sums"), c.sem("bc_roots"), c.sem("bc_normed_ready")
    names = ("zeroed", "transposed", "high", "low", "start_copied", "end_ready", "end_high", "end_low")
    zeroed, tp, high, low, acd, bwd, bwh, bwl = (c.sem("bc_" + q) for q in names)
    per = [min(5, NBC - 5 * i) for i in range(8)]
    jobs = [(kind, i) for kind in (2, 0, 1) for i in range(0, NBC, 8)]
    with nc.Block() as block:
        @block.tensor
        def _(pe):
            for n, (kind, i) in enumerate(jobs):
                k = min(8, NBC - i)
                if i == 0:
                    pe.wait_ge(nd, 10)
                if n >= 8:
                    if n - 8 < 5:
                        pe.wait_ge(acd, n - 7)
                    else:
                        pe.wait_ge(low, n - 12)
                rows = 48 if kind < 2 else 96
                for j in range(i, i + k):
                    src = (bcn[0:L, kind, j * SH:(j + 1) * SH, :].rearrange("p a b -> p (a b)") if kind < 2 else
                           ac[0:L, j * SH:(j + 1) * SH, :, :].rearrange("p a b c -> p (a b c)"))
                    ins = pe.transpose(c.bank[n % 8][0:rows, (j - i) * L:(j - i + 1) * L], src,
                                       c.const("ident", L)[:, 0:L])
                ins.then_inc(tp, 1)

        def job(n):
            kind, i = jobs[n]
            k = min(8, NBC - i)
            return kind, slice(i * L, (i + k) * L), c.bank[n % 8][:, 0:k * L]

        @block.gpsimd
        def _(pool):
            pool.memset(half.b[32:64, :], 0.0).then_inc(zeroed, 1)
            pool.memset(half.ch[32:64, :], 0.0).then_inc(zeroed, 1)
            pool.memset(half.wh[32:64, :], 0.0).then_inc(zeroed, 1)
            pool.wait_ge(bwh, 2)
            pool.tensor_tensor(half.wl[:, :], bwf, half.wh[0:L, :], ALU.subtract).then_inc(bwl, 1)

        @block.scalar
        def _(act):
            act.activation(bcn[0:L].rearrange("p a b c -> p (a b c)"), raw[:, :], ACT.Square).then_inc(squares, 1)
            act.wait_ge(sm, 1)
            act.activation(sr[0:L, :], ss[0:L, :], ACT.Sqrt).then_inc(rt, 1)
            act.wait_ge(zeroed, 3)
            for n in range(len(jobs)):
                kind, cols, ps = job(n)
                if n == len(jobs) - 1:
                    act.wait_ge(bwd, 2)
                    act.copy(half.wh[0:L, :], bwf).then_inc(bwh, 1)
                    act.copy(half.wh[64:64 + L, :], bwf).then_inc(bwh, 1)
                act.wait_ge(tp, n + 1)
                if kind == 0:
                    act.copy(half.b[0:48, cols], ps[0:48]).then_inc(high, 1)
                elif kind == 1:
                    act.copy(half.ch[0:48, cols], ps[0:48]).then_inc(high, 1)
                    act.copy(half.ch[64:112, cols], ps[0:48]).then_inc(high, 1)
                else:
                    act.copy(acT[:, cols], ps[0:96]).then_inc(acd, 1)

        @block.vector
        def _(dve):
            own = Own(dve, own_s)
            dve.wait_ge(squares, 1)
            own.did(dve.tensor_reduce(ss[0:L, :], bcn[0:L].rearrange("p a b c -> p (a b) c"), X, ALU.add))
            own.wait()
            dve.tensor_scalar(ss[0:L, :], ss[0:L, :], 1e-12, None, ALU.add).then_inc(sm, 1)
            dve.wait_ge(rt, 1)
            own.did(dve.reciprocal(ss[0:L, :], sr[0:L, :]))
            own.wait()
            for i in range(8):
                k = per[i] * SH
                dve.tensor_tensor(bcn[0:L, :, i * 30:i * 30 + k, :].rearrange("p z g n -> p g z n"),
                                  raw[0:L, i * 480:i * 480 + k * 2 * ST].rearrange("p (g z n) -> p g z n", z=2, n=ST),
                                  ss[0:L, i * 60:i * 60 + 2 * k].rearrange("p (g z) -> p g z", z=2).unsqueeze(3)
                                  .broadcast_to((L, k, 2, ST)), ALU.mult).then_inc(nd, 1)
            dve.wait_ge(nd, 8)
            for z in range(2):
                dve.tensor_tensor(ac[:, :, z, :], bcn[0:L, 1, :, :],
                                  ab[0:L, z, :].unsqueeze(2).broadcast_to((L, NG, ST)), ALU.mult).then_inc(nd, 1)

            def low_part(n):
                kind, cols, ps = job(n)
                dve.wait_ge(high, n - 4 if kind == 0 else 5 + 2 * (n - 9))
                if kind == 0:
                    dst, hi = half.b[64:112, cols], half.b[0:48, cols]
                else:
                    dst, hi = half.cl[:, cols], half.ch[0:48, cols]
                dve.tensor_tensor(dst, ps[0:48], hi, ALU.subtract).then_inc(low, 1)

            for n in range(5, 10):
                low_part(n)
            dve.wait_ge(nd, 10)
            dve.wait_ge(tp, 5)
            for z in range(2):
                end = zx[0:L, :] if z == 0 else gs[0:L, L - 1, :]
                dve.tensor_tensor(bw[:, :, z, :], bcn[0:L, 0, :, :],
                                  end.unsqueeze(2).broadcast_to((L, NG, ST)), ALU.mult).then_inc(bwd, 1)
            for n in range(10, len(jobs)):
                low_part(n)


def mixer_chain(c, ctx, sg, vT, gs, acT, half, de):
    nc = c.nc
    LOW = 64
    cbh = c.sb(ctx, "C_by_head_high", [112, 2, SH, L], F16)
    cbl = half.spare[:, 0:2 * SH * L].rearrange("p (s h t) -> p s h t", s=2, h=SH)
    mask = c.sb(ctx, "head_mask", [112, SH], F16)
    u = c.sb(ctx, "u_halves", [128, 2, DIN], F16)
    wt = c.sb(ctx, "mix_matrix", [L, 2, SH, L])
    wh = c.sb(ctx, "mix_matrix_high", [128, 2, SH, L], F16)
    wl = c.sb(ctx, "mix_matrix_low", [L, 2, SH, L], F16)
    tm = c.sb(ctx, "transition", [96, 2, 96])
    tq = c.sb(ctx, "transition_part", [96, 2, 96])
    state = c.sb(ctx, "state", [96, BATCH, 2, 2 * SP])
    yd = c.sb(ctx, "y_plus_Du", [128, 2, 3, L])
    dsk = c.sb(ctx, "D_skip", [128, 3])
    names = ["chain_set", "cbd_ready", "u_transposed", "u_high", "u_low", "cb_done", "wt_ready", "wt_high", "wt_low",
             "y_done", "y_used", "tm_parts", "tm_ready", "state_done", "state_ready"]
    (init, cbd_ready, u_t, u_high, u_low, cb_done, wt_ready, wt_high, wt_low, y_done, y_used, tm_parts, tm_ready,
     s_done, s_ready) = map(c.sem, names)
    d_in, own_s, ac_ready, a3_set = (c.sem(q) for q in ("D_skip_in", "chain_own", "C_start_placed", "a3_zeroed"))
    a3 = c.sb(ctx, "C_start_apart", [96, 2, 3, L])
    N = NBC
    steps = [(ch, b, b * NC1 + ch) for ch in range(NC1) for b in range(BATCH)]
    last = N - BATCH
    with nc.Block() as block:
        @block.sync
        def _(sp):
            for e in range(2):
                for k in range(3):
                    h = 2 * k + e
                    sp.dma_start(dsk[64 * e:64 * e + 64, k:k + 1], c.ins["L0_attn_D_skip"][h:h + 1].rearrange(
                        "(a n) -> a n", a=1).broadcast_to((64, 1))).then_inc(d_in, 16)

        @block.gpsimd
        def _(pool):
            pool.memset(u[32:64, :, :], 0.0).then_inc(init, 1)
            pool.memset(wh[32:64, :, :, :], 0.0).then_inc(init, 1)
            pool.memset(mask[32:64, :], 0.0).then_inc(init, 1)
            pool.wait_ge(init, 3)
            pool.tensor_copy(mask[0:48, :], c.const("h48", 48)).then_inc(init, 1)
            pool.wait_ge(init, 4)
            pool.tensor_copy(mask[64:112, :], c.const("h48", 48)).then_inc(init, 1)
            pool.wait_ge(init, 5)
            for n, (ch, b, bc_) in enumerate(steps):
                cols = slice(bc_ * L, (bc_ + 1) * L)
                if n >= 2:
                    pool.wait_ge(cb_done, n - 1)
                pool.tensor_tensor(cbh[:, n % 2, :, :], half.ch[:, cols].unsqueeze(1).broadcast_to((112, SH, L)),
                                   mask[:, :].unsqueeze(2).broadcast_to((112, SH, L)), ALU.mult).then_inc(cbd_ready, 1)
                if n:
                    pool.wait_ge(cbd_ready, 2 * n)
                pool.wait_ge(cbd_ready, 2 * n + 1)
                pool.tensor_tensor(cbl[:, n % 2, :, :], half.cl[:, cols].unsqueeze(1).broadcast_to((48, SH, L)),
                                   mask[0:48, :].unsqueeze(2).broadcast_to((48, SH, L)), ALU.mult
                                   ).then_inc(cbd_ready, 1)
                pool.wait_ge(cbd_ready, 2 * n + 2)
                if n < last:
                    if n >= 2:
                        pool.wait_ge(s_done, n - 1)
                    for z, m in ((0, c.const("ident", 96)[:, 0:96]), (1, c.const("swap", 96))):
                        pool.tensor_tensor(tq[:, z, :], m, de[:, z, bc_:bc_ + 1].broadcast_to((96, 96)),
                                           ALU.mult).then_inc(tm_parts, 1)
                    pool.wait_ge(tm_parts, 2 * n + 2)
                    pool.tensor_tensor(tm[:, n % 2, :], tq[:, 0, :], tq[:, 1, :], ALU.add
                                       ).then_inc(tm_ready, 1)
                    pool.wait_ge(tm_ready, n + 1)

        @block.scalar
        def _(act):
            act.wait_ge(init, 2)
            act.wait_ge(a3_set, 1)
            for n in range(N):
                act.wait_ge(u_t, n + 1)
                if n >= 2:
                    act.wait_ge(y_done, n - 1)
                    act.wait_ge(s_done, min(n - 1, last))
                act.copy(u[0:L, n % 2, :], c.bank[n % 2][0:L, 0:DIN]).then_inc(u_high, 1)
                bc_ = steps[n][2]
                for k in range(3):
                    r = slice(32 * k, 32 * k + 32)
                    act.copy(a3[r, n % 2, k, :], acT[r, bc_ * L:(bc_ + 1) * L]).then_inc(ac_ready, 1)
                act.wait_ge(wt_ready, n + 1)
                for r in (0, LOW):
                    act.copy(wh[r:r + L, n % 2, :, :], wt[:, n % 2, :, :]).then_inc(wt_high, 1)

        @block.tensor
        def _(pe):
            def prepare(n):
                ch, b, bc_ = steps[n]
                cols = slice(bc_ * L, (bc_ + 1) * L)
                if n >= 2:
                    pe.wait_ge(u_low, n - 1)
                for k in range(3):
                    ins = pe.transpose(c.bank[n % 2][0:L, k * 128:(k + 1) * 128], vT[:, k, cols], c.const("ident"))
                ins.then_inc(u_t, 1)
                pe.wait_ge(cbd_ready, 2 * n + 2)
                if n >= 2:
                    pe.wait_ge(wt_ready, n - 1)
                ps = c.bank[2 + n % 2][0:L, 0:SH * L]
                pe.matmul(ps, half.b[:, cols], cbh[:, n % 2, :, :].rearrange("p a b -> p (a b)"),
                          start=True, stop=False)
                pe.matmul(ps, half.b[0:48, cols], cbl[:, n % 2, :, :].rearrange("p a b -> p (a b)"),
                          start=False, stop=True).then_inc(cb_done, 1)

            prepare(0)
            for n, (ch, b, bc_) in enumerate(steps):
                if n + 1 < N:
                    prepare(n + 1)
                ybank, sbank = c.bank[4 + n % 2], c.bank[6 + n % 2]
                if n >= 2:
                    pe.wait_ge(y_used, 3 * (n - 1))
                if ch:
                    pe.wait_ge(s_ready, n - BATCH + 1)
                pe.wait_ge(u_low, n + 1)
                if n < last:
                    if ch:
                        pe.wait_ge(tm_ready, n + 1)
                    for j in range(3):
                        r, uc = slice(32 * j, 32 * j + 32), slice(j * 128, (j + 1) * 128)
                        ps, wc = sbank[r, 0:2 * SP], slice(bc_ * 96 + 32 * j, bc_ * 96 + 32 * j + 32)
                        if ch:
                            pe.matmul(ps, tm[r, n % 2, r], state[r, b, (ch - 1) % 2, :], start=True, stop=False,
                                      skip_group_check=True)
                        pe.matmul(ps, half.wh[0:LOW + L, wc], u[0:LOW + L, n % 2, uc],
                                  start=(ch == 0), stop=False, skip_group_check=True)
                        ins = pe.matmul(ps, half.wl[:, wc], u[0:L, n % 2, uc],
                                        start=False, stop=True, skip_group_check=True)
                    ins.then_inc(s_done, 1)
                pe.wait_ge(wt_high, 2 * (n + 1))
                pe.wait_ge(wt_low, n + 1)
                if ch:
                    pe.wait_ge(ac_ready, 3 * (n + 1))
                    pe.matmul(ybank[:, 0:3 * L], state[:, b, (ch - 1) % 2, :],
                              a3[:, n % 2, :, :].rearrange("p k t -> p (k t)"),
                              start=True, stop=False, skip_group_check=True)
                for k in range(3):
                    for e in range(2):
                        h = 2 * k + e
                        ps = ybank[64 * e:64 * e + 64, k * L:(k + 1) * L]
                        us = u[:, n % 2, h * SP:(h + 1) * SP]
                        pe.matmul(ps, us[0:LOW + L], wh[0:LOW + L, n % 2, h, :],
                                  start=(ch == 0), stop=False, skip_group_check=True)
                        ins = pe.matmul(ps, us[0:L], wl[:, n % 2, h, :], start=False, stop=True,
                                        skip_group_check=True)
                ins.then_inc(y_done, 1)

        @block.vector
        def _(dve):
            own = Own(dve, own_s)

            def prepare(n):
                ch, b, bc_ = steps[n]
                dve.wait_ge(u_high, n + 1)
                if n >= 2:
                    dve.wait_ge(y_done, n - 1)
                dve.tensor_tensor(u[LOW:LOW + L, n % 2, :], c.bank[n % 2][0:L, 0:DIN], u[0:L, n % 2, :], ALU.subtract
                                  ).then_inc(u_low, 1)
                dve.wait_ge(cb_done, n + 1)
                if n >= 2:
                    dve.wait_ge(wt_high, 2 * (n - 1))
                dve.tensor_tensor(wt[:, n % 2, :, :],
                                  c.bank[2 + n % 2][0:L, 0:SH * L].rearrange("p (a b) -> p a b", a=SH),
                                  gs[0:L, :, bc_ * SH:(bc_ + 1) * SH].rearrange("p t h -> p h t"),
                                  ALU.mult).then_inc(wt_ready, 1)

            def low_part(n):
                dve.wait_ge(wt_high, 2 * (n + 1))
                dve.tensor_tensor(wl[:, n % 2, :, :], wt[:, n % 2, :, :], wh[0:L, n % 2, :, :], ALU.subtract
                                  ).then_inc(wt_low, 1)

            dve.memset(a3[:, :, :, :], 0.0).then_inc(a3_set, 1)
            dve.wait_ge(d_in, 96)
            prepare(0)
            low_part(0)
            for n, (ch, b, bc_) in enumerate(steps):
                if n + 1 < N:
                    prepare(n + 1)
                if n < last:
                    dve.wait_ge(s_done, n + 1)
                    if ch >= 2:
                        dve.wait_ge(y_done, n - BATCH + 1)
                    dve.tensor_tensor(state[:, b, ch % 2, :], c.bank[6 + n % 2][0:96, 0:2 * SP], c.const("bd", 96),
                                      ALU.mult).then_inc(s_ready, 1)
                if n + 1 < N:
                    low_part(n + 1)
                dve.wait_ge(y_done, n + 1)
                for k in range(3):
                    dve.scalar_tensor_tensor(yd[:, n % 2, k, :], vT[:, k, bc_ * L:(bc_ + 1) * L], dsk[:, k:k + 1],
                                             c.bank[4 + n % 2][:, k * L:(k + 1) * L], ALU.mult, ALU.add
                                             ).then_inc(y_used, 1)
                dve.wait_ge(y_used, 3 * (n + 1))
                o = sg[:, :, bc_ * L:(bc_ + 1) * L]
                own.did(dve.tensor_tensor(o, yd[:, n % 2, :, :], o, ALU.mult))


def mlps(c, name, x, variants, func):
    nc = c.nc
    with ExitStack() as ctx:
        w1f = c.sb(ctx, name + "_w1_in", [128, 2, FF])
        w2f = c.sb(ctx, name + "_w2_in", [128, NF, D])
        w1 = c.sb(ctx, name + "_w1", [128, 2, 3, FF], F16)
        w2 = c.sb(ctx, name + "_w2", [128, 2, NF, 2, D], F16)
        b1 = c.sb(ctx, name + "_b1", [128, 2, NF])
        b2 = c.sb(ctx, name + "_b2", [128, 2, D])
        hid = c.sb(ctx, name + "_hidden", [128, 2, NF, CW])
        hh = c.sb(ctx, name + "_hidden_halves", [128, 2, 2, NF, CW], F16)
        part = c.sb(ctx, name + "_sum", [128, 2, D])
        w1_in, w2_in = c.sem(name + "_w1_loaded"), c.sem(name + "_w2_loaded")
        b_in = [c.sem(name + "_b_in0"), c.sem(name + "_b_in1")]
        w_high, w_scaled, w_split = c.sem(name + "_w_high"), c.sem(name + "_w_scaled"), c.sem(name + "_w_split")
        up, act_done, high, low, down, own_s, added = (
            c.sem(name + q) for q in ("_up", "_act", "_high", "_low", "_down", "_part_own", "_added"))
        sets = [va for k, va in enumerate(variants) if k == 0 or va["w1"] is not variants[k - 1]["w1"]]
        jobs = [(va, next(u for u, su in enumerate(sets) if su["w1"] is va["w1"]), ch)
                for va in variants for ch in va["chunks"]]
        first, final = {}, {}
        for n, (va, u, ch) in enumerate(jobs):
            first.setdefault(u, n)
            final[u] = n
        F2 = NF // 2
        with nc.Block() as block:
            @block.sync
            def _(sp):
                for v, va in enumerate(sets):
                    s = v % 2
                    if v:
                        sp.wait_ge(w_split, 3 * v)
                    w = va["w1"]
                    sp.dma_start(w1f[:, 0, :], w[0:128, :]).then_inc(w1_in, 16)
                    for p in (0, 64):
                        sp.dma_start(w1f[p:p + 64, 1, :], w[128:D, :]).then_inc(w1_in, 16)
                    sp.dma_start(w2f[:, :, :], va["w2"].rearrange("(f p) n -> p f n", p=128)).then_inc(w2_in, 16)
                    if v >= 2:
                        sp.wait_ge(act_done, NF * (final[v - 2] + 1))
                        sp.wait_ge(added, 3 * (final[v - 2] + 1))
                    sp.dma_start(b1[:, s, :], va["b1"].rearrange("(f p) -> p f", p=128),
                                 allow_slow_non_contiguous=True).then_inc(b_in[s], 16)
                    sp.dma_start(b2[:, s, :], va["b2"].rearrange("(a n) -> a n", a=1).broadcast_to((128, D))
                                 ).then_inc(b_in[s], 16)

            def split_weights(v, hi_eng, scale, lo_eng):
                s = v % 2
                highs = [(w1[:, s, 0:2, :], w1f[:, :, :], w1_in, 48), (w2[:, s, :, 0, :], w2f[:, :, :], w2_in, 16)]
                lows = [(w1[:, s, 2, :], w1f[:, 0, :], w1[:, s, 0, :], 1),
                        (w1[64:128, s, 1, :], w1f[64:128, 1, :], w1[64:128, s, 1, :], 1),
                        (w2[:, s, :, 1, :], w2f[:, :, :], w2[:, s, :, 0, :], 2)]
                if hi_eng is not None:
                    if v >= 2:
                        hi_eng.wait_ge(down, 3 * (final[v - 2] + 1))
                    for dst, src, loaded, per in highs:
                        hi_eng.wait_ge(loaded, per * (v + 1))
                        scale(dst, src).then_inc(w_high, 1)
                if lo_eng is not None:
                    if hi_eng is not None:
                        for src, need in ((w1f, 1), (w2f, 2)):
                            lo_eng.wait_ge(w_high, 2 * v + need)
                            lo_eng.tensor_scalar(src[:, :, :], src[:, :, :], W_SCALE, None, ALU.mult
                                                 ).then_inc(w_scaled, 1)
                    for k, (dst, a, b, need) in enumerate(lows):
                        lo_eng.wait_ge(w_high, 2 * v + need)
                        if hi_eng is not None:
                            lo_eng.wait_ge(w_scaled, 2 * (v - 1) + need)
                        if k:
                            lo_eng.wait_ge(w_split, 3 * v + k)
                        if hi_eng is not None:
                            ins = lo_eng.tensor_tensor(dst, a, b, ALU.subtract)
                        else:
                            ins = lo_eng.scalar_tensor_tensor(dst, a, W_SCALE, b, ALU.mult, ALU.subtract)
                        ins.then_inc(w_split, 1)

            @block.gpsimd
            def _(pool):
                for v in range(1, len(sets)):
                    split_weights(v, pool, lambda dst, src: pool.tensor_scalar(dst, src, W_SCALE, None, ALU.mult), pool)

            @block.tensor
            def _(pe):
                def up_proj(n):
                    va, v, ch = jobs[n]
                    s, terms = v % 2, va["terms"]
                    if n == first[v]:
                        pe.wait_ge(w_split, 3 * (v + 1))
                    for f in range(NF):
                        m = n * NF + f
                        if m >= 4:
                            pe.wait_ge(act_done, m - 3)
                        for k, (ws, xs, rows) in enumerate(terms):
                            ins = pe.matmul(c.bank[m % 4][:, 0:CW], w1[0:rows, s, ws, f * 128:(f + 1) * 128],
                                            x.h[0:rows, xs, ch * CW:(ch + 1) * CW],
                                            start=(k == 0), stop=(k == len(terms) - 1))
                        ins.then_inc(up, 1)

                up_proj(0)
                for n, (va, v, ch) in enumerate(jobs):
                    if n + 1 < len(jobs):
                        up_proj(n + 1)
                    s, cols = v % 2, va["n"]
                    pe.wait_ge(low, F2 * (n + 1))
                    for i in range(3):
                        m = 3 * n + i
                        if m >= 4:
                            pe.wait_ge(added, m - 3)
                        ps = c.bank[4 + m % 4][0:TT, 0:2 * cols].rearrange("p (z n) -> p z n", z=2)
                        t = slice(i * TT, (i + 1) * TT)
                        for f in range(NF):
                            def high_products():
                                return pe.matmul(ps, hh[:, n % 2, 0, f, t], w2[:, s, f, :, 0:cols],
                                                 start=(f == 0), stop=(f == NF - 1), skip_group_check=True)
                            if f == 0:
                                high_products()
                            pe.matmul(ps[:, 0, :], hh[:, n % 2, 1, f, t], w2[:, s, f, 0, 0:cols],
                                      start=False, stop=False, skip_group_check=True)
                            if f:
                                ins = high_products()
                        ins.then_inc(down, 1)

            @block.scalar
            def _(act):
                split_weights(0, act, lambda dst, src: act.activation(dst, src, ACT.Copy, scale=W_SCALE), None)
                for n, (va, v, ch) in enumerate(jobs):
                    if n == first[v]:
                        act.wait_ge(b_in[v % 2], 32 * (v // 2 + 1))
                    if n >= 2:
                        act.wait_ge(low, F2 * (n - 1))
                        act.wait_ge(down, 3 * (n - 1))
                    for f in range(NF):
                        m = n * NF + f
                        act.wait_ge(up, m + 1)
                        act.activation(hid[:, n % 2, f, :], c.bank[m % 4][:, 0:CW], func,
                                       bias=b1[:, v % 2, f:f + 1], scale=1.0 / W_SCALE).then_inc(act_done, 1)
                        if f % 2:
                            act.wait_ge(act_done, m + 1)
                            act.copy(hh[:, n % 2, 0, f - 1:f + 1, :], hid[:, n % 2, f - 1:f + 1, :]).then_inc(high, 1)

            @block.vector
            def _(dve):
                own = Own(dve, own_s)
                split_weights(0, None, None, dve)

                def low_parts(n):
                    for f in range(0, NF, 2):
                        dve.wait_ge(high, F2 * n + f // 2 + 1)
                        if n >= 2 and f == 0:
                            dve.wait_ge(down, 3 * (n - 1))
                        dve.tensor_tensor(hh[:, n % 2, 1, f:f + 2, :], hid[:, n % 2, f:f + 2, :],
                                          hh[:, n % 2, 0, f:f + 2, :], ALU.subtract).then_inc(low, 1)

                low_parts(0)
                for n, (va, v, ch) in enumerate(jobs):
                    if n + 1 < len(jobs):
                        low_parts(n + 1)
                    cols, gain = va["n"], va["gain"]
                    if n == first[v]:
                        dve.wait_ge(b_in[v % 2], 32 * (v // 2 + 1))
                    for i in range(3):
                        m, t = 3 * n + i, 3 * ch + i
                        dve.wait_ge(down, m + 1)
                        ps, y, q = c.bank[4 + m % 4][0:TT], c.xN[0:TT, t, 0:cols], part[0:TT, m % 2, 0:cols]
                        own.did(dve.scalar_tensor_tensor(q, ps[:, 0:cols], 1.0 / W_SCALE, b2[0:TT, v % 2, 0:cols],
                                                         ALU.mult, ALU.add))
                        own.wait()
                        own.did(dve.scalar_tensor_tensor(q, ps[:, cols:2 * cols], 1.0 / W_SCALE, q,
                                                         ALU.mult, ALU.add))
                        own.wait()
                        if m >= 3:
                            dve.wait_ge(added, m - 2)
                        if gain is None:
                            ins = dve.tensor_tensor(y, q, y, ALU.add)
                        else:
                            ins = dve.scalar_tensor_tensor(y, q, gain(t), y, ALU.mult, ALU.add)
                        ins.then_inc(added, 1)


def qkv(c, name, source, bias, q2, kT, v):
    nc = c.nc
    E2 = 64
    with ExitStack() as ctx:
        w = c.sb(ctx, name + "_w", [DH + 1, 2, 3 * D])
        wrow = c.sb(ctx, name + "_rows", [DH, 6, D]) if bias is not None else None
        parts = c.sb(ctx, name + "_parts", [128, 2, 2, HEADS, E2], F16)
        idh = c.sb(ctx, name + "_ident", [128, 128], F16)
        names = ("_w_in", "_b_in", "_set", "_w_turned", "_placed", "_proj", "_proj_v", "_high", "_low", "_again",
                 "_turned", "_k_out", "_q_out", "_v_out")
        (w_in, b_in, init, wt, placed, pqk, pv, high, low, again, turned, k_out, q_out, v_out) = (
            c.sem(name + x) for x in names)
        tiles = [(b, k) for b in range(BATCH) for k in range(len(KT))]
        N = len(tiles)

        def cols(n):
            b, k = tiles[n]
            return b * T + KT[k][0], KT[k][1]

        def turned_bank(n, z):
            return c.bank[4 + 2 * z + n % 2].bitcast(F16)

        with nc.Block() as block:
            @block.sync
            def _(sp):
                if bias is None:
                    sp.dma_start(w[0:DH, :, :], source.rearrange("(o p) n -> p o n", p=DH)).then_inc(w_in, 16)
                else:
                    sp.dma_start(wrow[:, :, :], source.rearrange("(a p) n -> p a n", p=DH)).then_inc(w_in, 16)
                    sp.dma_start(w[DH:DH + 1, 1, :], bias.rearrange("(a n) -> a n", a=1)).then_inc(b_in, 16)

            @block.gpsimd
            def _(pool):
                pool.memset(parts[:, :, 0, :, :], 0.0).then_inc(init, 1)
                pool.memset(parts[:, :, 1, :, :], 0.0).then_inc(init, 1)
                pool.tensor_copy(idh[:, :], c.const("ident")).then_inc(init, 1)
                pool.memset(v[:, :, :, :, HD:2 * HD], 1.0).then_inc(init, 1)
                pool.wait_ge(init, 4)
                pool.memset(parts[:, :, 1, :, 32:33], -1.0).then_inc(init, 1)
                for n in range(N):
                    m = cols(n)[1]
                    pool.wait_ge(high, n + 1)
                    for z, at in ((0, 33), (1, 16)):
                        pool.tensor_copy(parts[0:m, n % 2, z, :, at:at + HD], parts[0:m, n % 2, z, :, 0:HD]
                                         ).then_inc(again, 1)

            @block.tensor
            def _(pe):
                if bias is not None:
                    pe.wait_ge(w_in, 16)
                    for a in range(6):
                        for o in range(2):
                            ins = pe.transpose(c.bank[a][0:DH, o * DH:(o + 1) * DH],
                                               wrow[:, a, o * DH:(o + 1) * DH], c.const("ident", DH)[:, 0:DH])
                        ins.then_inc(wt, 1)
                    pe.wait_ge(placed, 6)
                    pe.wait_ge(b_in, 16)
                else:
                    pe.wait_ge(w_in, 16)
                    pe.wait_ge(placed, 1)

                def project(n):
                    at, m = cols(n)
                    if n >= 2:
                        pe.wait_ge(low, 2 * (n - 1))
                        pe.wait_ge(v_out, n - 1)
                    for o in range(2):
                        r = DH + o
                        ins = pe.matmul(c.bank[n % 2][0:m, 0:2 * D], c.xT[0:r, o, at:at + m], w[0:r, o, 0:2 * D],
                                        start=(o == 0), stop=(o == 1))
                    ins.then_inc(pqk, 1)
                    for o in range(2):
                        r = DH + o
                        ins = pe.matmul(c.bank[2 + n % 2][0:m, 0:D], c.xT[0:r, o, at:at + m], w[0:r, o, 2 * D:3 * D],
                                        start=(o == 0), stop=(o == 1))
                    ins.then_inc(pv, 1)

                project(0)
                pe.wait_ge(init, 5)
                for n in range(N):
                    if n + 1 < N:
                        project(n + 1)
                    m = cols(n)[1]
                    pe.wait_ge(low, 2 * n + 2)
                    pe.wait_ge(again, 2 * n + 2)
                    if n >= 2:
                        pe.wait_ge(k_out, n - 1)
                        pe.wait_ge(q_out, 2 * (n - 1))
                    for z in range(2):
                        for g in range(HEADS // 2):
                            ins = pe.transpose(turned_bank(n, z)[:, g * TT:g * TT + m],
                                               parts[0:m, n % 2, z, 2 * g:2 * g + 2, :].rearrange("p h e -> p (h e)"),
                                               idh[0:m, 0:m])
                        ins.then_inc(turned, 1)

            def turned_view(n, z, p0, p1):
                m = cols(n)[1]
                return turned_bank(n, z)[p0:p1, 0:6 * TT].rearrange("p (g t) -> p g t", g=6)[:, :, 0:m]

            @block.scalar
            def _(act):
                act.wait_ge(init, 5)
                for n in range(N + 1):
                    if n < N:
                        b, k = tiles[n]
                        at, m = cols(n)
                        act.wait_ge(pqk, n + 1)
                        if n >= 2:
                            act.wait_ge(turned, 2 * (n - 1))
                        act.copy(parts[0:m, n % 2, :, :, 0:HD],
                                 c.bank[n % 2][0:m, 0:2 * D].rearrange("p (z h e) -> p z h e", z=2, e=HD)
                                 ).then_inc(high, 1)
                        act.wait_ge(pv, n + 1)
                        act.copy(v[0:m, b, k, :, 0:HD], c.bank[2 + n % 2][0:m, 0:D].rearrange("p (h e) -> p h e", e=HD)
                                 ).then_inc(v_out, 1)
                    if n:
                        at, m = cols(n - 1)
                        act.wait_ge(turned, 2 * n - 1)
                        for e in range(2):
                            act.copy(q2[64 * e:64 * e + 64, :, e, at:at + m], turned_view(n - 1, 0, 64 * e, 64 * e + 64)
                                     ).then_inc(q_out, 1)

            @block.vector
            def _(dve):
                if bias is None:
                    dve.memset(w[DH:DH + 1, 1, :], 0.0).then_inc(placed, 1)
                else:
                    for a in range(6):
                        dve.wait_ge(wt, a + 1)
                        dve.tensor_copy(w[0:DH, :, a * DH:(a + 1) * DH],
                                        c.bank[a][0:DH, 0:D].rearrange("p (o n) -> p o n", o=2)).then_inc(placed, 1)
                dve.wait_ge(init, 5)
                for n in range(N + 1):
                    if n < N:
                        at, m = cols(n)
                        dve.wait_ge(high, n + 1)
                        ps = c.bank[n % 2][0:m, 0:2 * D].rearrange("p (z h e) -> p z h e", z=2, e=HD)
                        for z, to in ((0, 16), (1, 33)):
                            dve.tensor_tensor(parts[0:m, n % 2, z, :, to:to + HD], ps[:, z, :, :],
                                              parts[0:m, n % 2, z, :, 0:HD], ALU.subtract).then_inc(low, 1)
                    if n:
                        at, m = cols(n - 1)
                        dve.wait_ge(turned, 2 * n)
                        dve.tensor_copy(kT[:, :, at:at + m], turned_view(n - 1, 1, 0, 128)).then_inc(k_out, 1)
                    if n < HEADS:
                        g, e = divmod(n, 2)
                        dve.memset(q2[64 - 64 * e:128 - 64 * e, g, e, :].bitcast(F32), 0.0)


def attention(c, name, q2, kT, v, aT):
    nc = c.nc
    NK = len(KT)
    HALF = T // 2 + 1
    START = (0, T - HALF)
    scale = HD ** -0.5
    groups = [(b, j) for b in range(BATCH) for j in range(3)]
    G = len(groups)
    with ExitStack() as ctx:
        mx = c.sb(ctx, name + "_max", [128, 2, 2, 4, NK])
        mexp = c.sb(ctx, name + "_max_placed", [128, 2, 2, NK, 128], F16)
        p = c.sb(ctx, name + "_p", [128, 4, 2, HALF])
        idh = c.sb(ctx, name + "_ident", [128, 128], F16)
        names = ("_set", "_scored", "_maxed", "_placed", "_m_turned", "_m_copied_s", "_m_copied_v", "_keyed", "_exp", "_summed",
                 "_sums_copied")
        (init, scored, maxed, placed, mt, mc_s, mc_v, keyed, expd, summed, copied) = (
            c.sem(name + x) for x in names)
        NS, LAG = 40, 6
        S_UNITS = [(hh, k, half) for hh in range(4) for k in range(NK) for half in range(2)]
        ring = []
        for g in range(G + 1):
            scores_ = [("s", g, i) for i in range(NS)] if g < G else []
            turns = [("m", g - 1, gi) for gi in range(2)] if g else []
            ring += scores_[:LAG] + turns + scores_[LAG:]
        place = {unit: at for at, unit in enumerate(ring)}
        B_UNITS = [(half, k, gi) for half in range(2) for k in range(NK) for gi in range(2)]
        NB = len(B_UNITS)
        START_RING = place[("m", 0, 1)] + 1
        EARLY = 9

        def ring_upto(n):
            at = START_RING + (n + 1) * (NS + 2) // NB + min(EARLY, (n + 1) * EARLY // NB)
            return min(len(ring), at)

        def turn_of(unit):
            return next(n for n in range(G * NB) if ring_upto(n) > place[unit])

        mc = (mc_s, mc_v)
        acc = c.bank[3]

        def copy_max(eng, copy, g, gi):
            b, j = groups[g]
            eng.wait_ge(mt, 2 * g + gi + 1)
            bank = c.bank[place[("m", g, gi)] % 3].bitcast(F16)
            for e in range(2):
                r = 64 * e + 32
                copy(q2[r:r + 1, 2 * j + gi, e, b * T:(b + 1) * T], bank[r:r + 1, 0:T]).then_inc(mc[gi], 1)

        with nc.Block() as block:
            @block.gpsimd
            def _(pool):
                pool.tensor_copy(idh[:, :], c.const("ident")).then_inc(init, 1)
                pool.memset(mexp[:, :, :, :, :], 0.0).then_inc(init, 1)
                pool.memset(mx[:, :, :, :, :], 0.0).then_inc(init, 1)

            @block.tensor
            def _(pe):
                pe.wait_ge(init, 3)

                def ring_unit(at):
                    kind, g, i = ring[at]
                    b, j = groups[g]
                    bank = c.bank[at % 3]
                    if at >= 3:
                        kind0, g0, i0 = ring[at - 3]
                        if kind0 == "s":
                            pe.wait_ge(maxed, g0 * NS + i0 + 1)
                        else:
                            pe.wait_ge(mc[i0], 2 * g0 + 2)
                    if kind == "s":
                        hh, k, half = S_UNITS[i]
                        q0, qn = KT[k]
                        k0 = START[half]
                        pe.matmul(bank[0:qn, 0:HALF],
                                  q2[:, 2 * j + hh // 2, hh % 2, b * T + q0:b * T + q0 + qn],
                                  kT[:, 2 * j + hh // 2, b * T + k0:b * T + k0 + HALF],
                                  start=True, stop=True).then_inc(scored, 1)
                    else:
                        pe.wait_ge(placed, 2 * g + 2)
                        for k in range(NK):
                            q0, qn = KT[k]
                            ins = pe.transpose(bank.bitcast(F16)[:, q0:q0 + qn],
                                               mexp[0:qn, g % 2, i, k, :], idh[0:qn, 0:qn])
                        ins.then_inc(mt, 1)

                def keys(n, e):
                    g, i = divmod(n, NB)
                    b, j = groups[g]
                    half, k, gi = B_UNITS[i]
                    k0, kn = KT[k]
                    if e == 0:
                        if i == 0:
                            pe.wait_ge(mc_s, 2 * g + 2)
                            pe.wait_ge(mc_v, 2 * g + 2)
                        if n >= 2:
                            pe.wait_ge(expd, n - 1)
                    pe.matmul(c.pair[2 + n % 2][0:kn, 512 * e:512 * e + HALF],
                              kT[:, 2 * j + gi, b * T + k0:b * T + k0 + kn],
                              q2[:, 2 * j + gi, e, b * T + START[half]:b * T + START[half] + HALF],
                              start=True, stop=True).then_inc(keyed, 1)

                def values(n):
                    g, i = divmod(n, NB)
                    b, j = groups[g]
                    half, k, _ = B_UNITS[i]
                    kn = KT[k][1]
                    pe.wait_ge(expd, n + 2)
                    if k == 0 and n:
                        pe.wait_ge(copied, 2 * g + half)
                    for hh in range(4):
                        h = 4 * j + hh
                        ins = pe.matmul(acc[32 * hh:32 * hh + 32, 0:HALF], v[0:kn, b, k, h, :],
                                        p[0:kn, (n + hh // 2) % 4, hh % 2, :],
                                        start=(k == 0), stop=(k == NK - 1))
                    ins.then_inc(summed, 1)

                at = 0
                while at < START_RING:
                    ring_unit(at)
                    at += 1
                for n in range(G * NB + 3):
                    if n < G * NB:
                        keys(n, 0)
                        if at < ring_upto(n):
                            ring_unit(at)
                            at += 1
                        keys(n, 1)
                    if n >= 3 and n % 2:
                        values(n - 3)
                    while at < ring_upto(n):
                        ring_unit(at)
                        at += 1

            @block.vector
            def _(dve):
                dve.wait_ge(init, 3)

                for at, (kind, g, i) in enumerate(ring):
                    if kind == "s":
                        hh, k, half = S_UNITS[i]
                        qn = KT[k][1]
                        dve.wait_ge(scored, g * NS + i + 1)
                        dve.reduce_max(mx[0:qn, g % 2, half, hh, k:k + 1], c.bank[at % 3][0:qn, 0:HALF], X
                                       ).then_inc(maxed, 1)
                        if i == NS - 1:
                            dve.wait_ge(maxed, (g + 1) * NS)
                            if g >= 2:
                                dve.wait_ge(mt, 2 * (g - 1))
                            for e in range(2):
                                a, b_ = (mx[:, g % 2, hf, :, :].rearrange("p (i e) k -> p i e k", e=2)[:, :, e, :]
                                         for hf in range(2))
                                dve.tensor_tensor(mexp[:, g % 2, :, :, 64 * e + 32], a, b_, ALU.max
                                                  ).then_inc(placed, 1)
                    elif i == 1:
                        copy_max(dve, dve.tensor_copy, g, 1)

            @block.scalar
            def _(act):
                def copy_sums(n):
                    b, j = groups[n // 2]
                    act.wait_ge(summed, NK * (n + 1))
                    if n % 2:
                        act.wait_ge(copied, n)
                    at = b * T + START[n % 2]
                    act.copy(aT[:, j, at:at + HALF], acc[:, 0:HALF]).then_inc(copied, 1)

                copy_max(act, act.copy, 0, 0)
                turned_in = {turn_of(("m", g, 0)): g for g in range(1, G)}
                for n in range(G * NB):
                    g, i = divmod(n, NB)
                    half, k, gi = B_UNITS[i]
                    kn = KT[k][1]
                    act.wait_ge(keyed, 2 * n + 2)
                    if n >= 4:
                        act.wait_ge(summed, (n - 4) // 2 + 1)
                    act.activation(p[0:kn, n % 4, :, :],
                                   c.pair[2 + n % 2][0:kn, :].rearrange("p (e q) -> p e q", e=2)[:, :, 0:HALF],
                                   ACT.Exp, scale=scale).then_inc(expd, 1)
                    if n in turned_in:
                        copy_max(act, act.copy, turned_in[n], 0)
                    if i == 1 and g:
                        copy_sums(2 * g - 1)
                    if i == 11:
                        copy_sums(2 * g)
                copy_sums(2 * G - 1)


def ff0(c, x):
    i = c.ins
    mlps(c, "ff0", x, [dict(w1=i["L0_attn_ff_w1"], b1=i["L0_attn_ff_b1"], w2=i["L0_attn_ff_w2"], b2=i["L0_attn_ff_b2"],
                            terms=ALL_TERMS, n=D, gain=None, chunks=range(NCH))],
         ACT.Gelu_apprx_tanh)


def attention_layer(c, name, w_qkv, b_qkv, project):
    with ExitStack() as ctx:
        aT = c.sb(ctx, name + "_aT", [128, 3, NT])
        with ExitStack() as inner:
            q2 = c.sb(inner, name + "_q2", [128, HEADS // 2, 2, NT], F16)
            kT = c.sb(inner, name + "_kT", [128, HEADS // 2, NT], F16)
            v = c.sb(inner, name + "_v", [128, BATCH, len(KT), HEADS, 2 * HD])
            qkv(c, name + "_qkv", w_qkv, b_qkv, q2, kT, v)
            attention(c, name, q2, kT, v, aT)
        project(ctx, aT)


def heads_out(c, name, aT, weights):
    nc = c.nc
    with ExitStack() as ctx:
        r = c.sb(ctx, name + "_recip", [128, 2, HEADS])
        o = c.sb(ctx, name + "_heads", [128, 2, D])
        oT = c.sb(ctx, name + "_heads_T", [DH + 1, 2, 2, TT])
        names = ("_ones", "_tokens", "_recips", "_divided", "_turned", "_channels", "_done", "_added")
        ones, tokens, recips, divided, turned, channels, done, added = (c.sem(name + q) for q in names)
        with nc.Block() as block:
            @block.gpsimd
            def _(pool):
                pool.memset(oT[DH:DH + 1, :, :, :], 1.0).then_inc(ones, 1)

            @block.tensor
            def _(pe):
                for n in range(NTILE + 2):
                    if n < NTILE:
                        if n >= 3:
                            pe.wait_ge(divided, n - 2)
                        for j in range(3):
                            ins = pe.transpose(c.bank[n % 3][0:TT, j * 128:(j + 1) * 128],
                                               aT[:, j, n * TT:(n + 1) * TT], c.const("ident"))
                        ins.then_inc(tokens, 1)
                    i = n - 1
                    if 0 <= i < NTILE:
                        pe.wait_ge(divided, i + 1)
                        if i >= 2:
                            pe.wait_ge(channels, i - 1)
                        for k in range(2):
                            ins = pe.transpose(c.bank[3 + i % 2][0:DH, k * TT:(k + 1) * TT],
                                               o[0:TT, i % 2, k * DH:(k + 1) * DH], c.const("ident", TT)[:, 0:TT])
                        ins.then_inc(turned, 1)
                    i = n - 2
                    if 0 <= i:
                        pe.wait_ge(channels, i + 1)
                        if i == 0:
                            pe.wait_ge(ones, 1)
                        if i >= 3:
                            pe.wait_ge(added, i - 2)
                        w = weights(i)
                        for k in range(2):
                            ins = pe.matmul(c.bank[5 + i % 3][0:TT, 0:D], oT[0:DH + k, i % 2, k, :], w[0:DH + k, k, :],
                                            start=(k == 0), stop=(k == 1))
                        ins.then_inc(done, 1)

            @block.scalar
            def _(act):
                for i in range(NTILE):
                    act.wait_ge(turned, i + 1)
                    if i >= 2:
                        act.wait_ge(done, i - 1)
                    act.copy(oT[0:DH, i % 2, :, :], c.bank[3 + i % 2][0:DH, 0:2 * TT].rearrange("p (k t) -> p k t", k=2)
                             ).then_inc(channels, 1)

            @block.vector
            def _(dve):
                def add(i):
                    dve.wait_ge(done, i + 1)
                    dve.tensor_tensor(c.xN[0:TT, i, :], c.bank[5 + i % 3][0:TT, 0:D], c.xN[0:TT, i, :], ALU.add
                                      ).then_inc(added, 1)

                for i in range(NTILE):
                    dve.wait_ge(tokens, i + 1)
                    ps = c.bank[i % 3][0:TT, 0:3 * 128].rearrange("p (h e) -> p h e", e=2 * HD)
                    dve.reciprocal(r[0:TT, i % 2, :].unsqueeze(2), ps[:, :, HD:HD + 1]).then_inc(recips, 1)
                    dve.wait_ge(recips, i + 1)
                    if i >= 2:
                        dve.wait_ge(turned, i - 1)
                    dve.tensor_tensor(o[0:TT, i % 2, :].rearrange("p (h e) -> p h e", e=HD), ps[:, :, 0:HD],
                                      r[0:TT, i % 2, :].unsqueeze(2).broadcast_to((TT, HEADS, HD)), ALU.mult
                                      ).then_inc(divided, 1)
                    if i >= 2:
                        add(i - 2)
                add(NTILE - 2)
                add(NTILE - 1)


def out_proj0(c, ctx, aT):
    nc = c.nc
    row = c.sb(ctx, "outp_rows", [DH, 2, D])
    w = c.sb(ctx, "outp_w", [DH + 1, 2, D])
    w_in, b_in, tp, placed = (c.sem("outp_w" + x) for x in ("_in", "_bias_in", "_turned", "_placed"))
    with nc.Block() as block:
        @block.sync
        def _(sp):
            sp.dma_start(row[:, :, :], c.ins["L0_ffn_out_proj_w"].rearrange("(a p) n -> p a n", p=DH)
                         ).then_inc(w_in, 16)
            sp.dma_start(w[DH:DH + 1, 1, :], c.ins["L0_ffn_out_proj_b"].rearrange("(a n) -> a n", a=1)
                         ).then_inc(b_in, 16)
            sp.wait_ge(b_in, 16)

        @block.vector
        def _(dve):
            for o in range(2):
                dve.wait_ge(tp, o + 1)
                dve.tensor_copy(w[0:DH, o, :], c.bank[o][0:DH, 0:D]).then_inc(placed, 1)

        @block.tensor
        def _(pe):
            pe.wait_ge(w_in, 16)
            for o in range(2):
                for a in range(2):
                    ins = pe.transpose(c.bank[o][0:DH, a * DH:(a + 1) * DH], row[:, a, o * DH:(o + 1) * DH],
                                       c.const("ident", DH)[:, 0:DH])
                ins.then_inc(tp, 1)
    heads_out(c, "outp", aT, lambda i: w)


def route(c, x, comb):
    nc = c.nc
    E = EXPERTS
    with ExitStack() as ctx:
        row = c.sb(ctx, "router_rows", [E, D])
        w = c.sb(ctx, "router_w", [128, 2, E])
        rb = c.sb(ctx, "router_b", [E, 1])
        lT = c.sb(ctx, "router_logits_T", [E, NT])
        lg = c.sb(ctx, "router_logits", [128, NTILE, E])
        pr = c.sb(ctx, "router_probs", [128, NTILE, E])
        top = c.sb(ctx, "top_one", [128, NTILE, E])
        tie = c.sb(ctx, "top_rank", [128, NTILE, E])
        m = c.sb(ctx, "router_max", [128, 4, NTILE])
        w_in, tp, placed, done = c.sem("router_in"), c.sem("router_turned"), c.sem("router_placed"), c.sem("logits")
        own_s, shifted, exped = c.sem("route_own"), c.sem("logits_shifted"), c.sem("router_exp")
        chunk, biased = c.sem("logits_chunk"), c.sem("logits_biased")
        with nc.Block() as block:
            @block.sync
            def _(sp):
                sp.dma_start(row[:, :], c.ins["L0_ffn_router_w"]).then_inc(w_in, 16)
                sp.dma_start(rb[:, :], c.ins["L0_ffn_router_b"].rearrange("(n a) -> n a", a=1)).then_inc(w_in, 16)

            @block.tensor
            def _(pe):
                pe.wait_ge(w_in, 32)
                for o, k in ((0, 128), (1, 64)):
                    ins = pe.transpose(c.bank[1][0:k, o * E:(o + 1) * E], row[:, o * 128:o * 128 + k],
                                       c.const("ident", E)[:, 0:E])
                ins.then_inc(tp, 1)
                pe.wait_ge(placed, 2)
                for ch in range(NCH):
                    for o, k in ((0, 128), (1, 64)):
                        ins = pe.matmul(c.bank[2 + ch][0:E, 0:CW], w[0:k, o, :], x.x[0:k, o, ch * CW:(ch + 1) * CW],
                                        start=(o == 0), stop=(o == 1))
                    ins.then_inc(chunk, 1)
                for i in range(NTILE):
                    pe.wait_ge(biased, i // 3 + 1)
                    ins = pe.transpose(c.bank[0][0:TT, i * E:(i + 1) * E], lT[:, i * TT:(i + 1) * TT],
                                       c.const("ident", E)[:, 0:E])
                ins.then_inc(done, 1)

            @block.scalar
            def _(act):
                act.wait_ge(w_in, 32)
                for ch in range(NCH):
                    act.wait_ge(chunk, ch + 1)
                    act.activation(lT[:, ch * CW:(ch + 1) * CW], c.bank[2 + ch][0:E, 0:CW], ACT.Identity,
                                   bias=rb[:, :]).then_inc(biased, 1)
                act.wait_ge(shifted, 1)
                act.activation(pr[0:TT, :, :], lg[0:TT, :, :], ACT.Exp).then_inc(exped, 1)

            @block.vector
            def _(dve):
                own = Own(dve, own_s)

                def wide(ap):
                    return ap.unsqueeze(2).broadcast_to((TT, NTILE, E))

                def tt(out, a, b, op):
                    own.did(dve.tensor_tensor(out, a, b, op))
                    own.wait()

                def largest(out, a):
                    own.did(dve.tensor_reduce(out, a, X, ALU.max))
                    own.wait()

                P, L_, R, TOP = pr[0:TT], lg[0:TT], tie[0:TT], top[0:TT]
                m1, m2, mr, sm = (m[0:TT, k, :] for k in range(4))
                rank = c.const("rank", TT).unsqueeze(1).broadcast_to((TT, NTILE, E))
                dve.wait_ge(tp, 1)
                for o, k in ((0, 128), (1, 64)):
                    dve.tensor_copy(w[0:k, o, :], c.bank[1][0:k, o * E:(o + 1) * E]).then_inc(placed, 1)
                dve.wait_ge(done, 1)
                own.did(dve.tensor_copy(L_.rearrange("p a b -> p (a b)"), c.bank[0][0:TT, 0:NTILE * E]))
                own.wait()
                largest(m1, L_)
                dve.tensor_tensor(L_, L_, wide(m1), ALU.subtract).then_inc(shifted, 1)
                dve.wait_ge(exped, 1)
                own.did(dve.tensor_reduce(sm, P, X, ALU.add))
                own.wait()
                own.did(dve.reciprocal(sm, sm))
                own.wait()
                tt(P, P, wide(sm), ALU.mult)

                def pick(values, best, one):
                    largest(best, values)
                    tt(R, values, wide(best), ALU.is_equal)
                    tt(R, R, rank, ALU.mult)
                    largest(mr, R)
                    tt(one, R, wide(mr), ALU.is_equal)

                pick(P, m1, TOP)
                own.did(dve.scalar_tensor_tensor(L_, TOP, -2.0, P, ALU.mult, ALU.add))
                own.wait()
                C = comb[0:TT]
                pick(L_, m2, C)
                tt(C, C, TOP, ALU.add)
                tt(C, C, P, ALU.mult)
                tt(sm, m1, m2, ALU.add)
                own.did(dve.reciprocal(sm, sm))
                own.wait()
                tt(C, C, wide(sm), ALU.mult)


def moe(c, x):
    i = c.ins
    with ExitStack() as ctx:
        comb = c.sb(ctx, "combine", [128, NTILE, EXPERTS])
        route(c, x, comb)
        mlps(c, "moe", x, [dict(w1=i["L0_ffn_w1"][e], b1=i["L0_ffn_b1"][e], w2=i["L0_ffn_w2"][e], b2=i["L0_ffn_b2"][e],
                                terms=ALL_TERMS, n=D, gain=lambda t, e=e: comb[0:TT, t, e:e + 1],
                                chunks=range(NCH)) for e in range(EXPERTS)], ACT.Gelu)


def spiking(c):
    nc = c.nc
    NK, S3 = len(KT), T // 3
    with ExitStack() as ctx:
        wT = c.sb(ctx, "sp_wT", [DH + 1, 4, 2, D])
        qs = c.sb(ctx, "q_spikes", [DH, 2, NT], F16)
        ks = c.sb(ctx, "k_spikes", [128, BATCH, NK, D], F16)
        vs = c.sb(ctx, "v_spikes", [128, BATCH, NK, D], F16)
        kv = c.sb(ctx, "kv_counts", [DH, BATCH, 2, DH], F16)
        x3 = c.sb(ctx, "xa_spikes", [DH + 1, 2, NT])
        with ExitStack() as early:
            wr = c.sb(early, "sp_rows", [DH, 4, 2, D])
            pc = c.sb(early, "sp_cols", [DH, 4, 4, 2])
            prow = c.sb(early, "sp_prow", [DH + 1, 7, 4 * D])
            pr = prow[DH:DH + 1]
            w_in, var_r, sq_r, own_s = c.sem("sp_in"), c.sem("sp_var"), c.sem("sp_sqrt"), c.sem("sp_own")
            scaled, tp, placed = c.sem("sp_scaled"), c.sem("sp_turned"), c.sem("sp_placed")
            with nc.Block() as block:
                @block.sync
                def _(sp):
                    for w in range(4):
                        sp.dma_start(wr[:, w, :, :], c.ins["L1_attn_W"][w].rearrange("(a p) n -> p a n", p=DH)
                                     ).then_inc(w_in, 16)
                    for k, n in enumerate(("bn_gamma", "bn_var")):
                        sp.dma_start(pc[:, k, :, :].rearrange("p w a -> p (w a)"),
                                     c.ins["L1_attn_" + n].rearrange("w (a p) -> p (w a)", p=DH),
                                     allow_slow_non_contiguous=True).then_inc(w_in, 16)

                @block.scalar
                def _(act):
                    for k, n in enumerate(("b", "bn_gamma", "bn_beta", "bn_mean", "bn_var")):
                        act.dma_start(pr[:, k, :], c.ins["L1_attn_" + n].rearrange("w n -> (w n)").rearrange(
                            "(a n) -> a n", a=1)).then_inc(w_in, 16)
                    act.wait_ge(var_r, 2)
                    act.activation(pc[:, 2, :, :], pc[:, 1, :, :], ACT.Sqrt).then_inc(sq_r, 1)
                    act.activation(pr[:, 5, :], pr[:, 4, :], ACT.Sqrt).then_inc(sq_r, 1)

                @block.vector
                def _(dve):
                    own = Own(dve, own_s)
                    dve.wait_ge(w_in, 16 * 11)
                    dve.tensor_scalar(pc[:, 1, :, :], pc[:, 1, :, :], 1e-5, None, ALU.add).then_inc(var_r, 1)
                    dve.tensor_scalar(pr[:, 4, :], pr[:, 4, :], 1e-5, None, ALU.add).then_inc(var_r, 1)
                    dve.wait_ge(sq_r, 2)
                    own.did(dve.reciprocal(pc[:, 3, :, :], pc[:, 2, :, :]))
                    own.did(dve.reciprocal(pr[:, 6, :], pr[:, 5, :]))
                    own.wait()
                    own.did(dve.tensor_tensor(pc[:, 3, :, :], pc[:, 3, :, :], pc[:, 0, :, :], ALU.mult))
                    own.did(dve.tensor_tensor(pr[:, 6, :], pr[:, 6, :], pr[:, 1, :], ALU.mult))
                    own.did(dve.tensor_tensor(pr[:, 0, :], pr[:, 0, :], pr[:, 3, :], ALU.subtract))
                    own.wait()
                    own.did(dve.tensor_tensor(pr[:, 0, :], pr[:, 0, :], pr[:, 6, :], ALU.mult))
                    own.wait()
                    own.did(dve.tensor_tensor(wT[DH:DH + 1, :, 1, :], pr[:, 0, :].rearrange("p (w n) -> p w n", w=4),
                                              pr[:, 2, :].rearrange("p (w n) -> p w n", w=4), ALU.add))
                    for w in range(4):
                        for a in range(2):
                            dve.tensor_scalar(wr[:, w, a, :], wr[:, w, a, :], pc[:, 3, w, a:a + 1], None, ALU.mult
                                              ).then_inc(scaled, 1)
                    for n in range(8):
                        w, o = divmod(n, 2)
                        dve.wait_ge(tp, n + 1)
                        dve.tensor_copy(wT[0:DH, w, o, :], c.bank[n][0:DH, 0:D]).then_inc(placed, 1)

                @block.tensor
                def _(pe):
                    pe.wait_ge(scaled, 8)
                    for n in range(8):
                        w, o = divmod(n, 2)
                        for a in range(2):
                            ins = pe.transpose(c.bank[n][0:DH, a * DH:(a + 1) * DH], wr[:, w, a, o * DH:(o + 1) * DH],
                                               c.const("ident", DH)[:, 0:DH])
                        ins.then_inc(tp, 1)
        kjobs = [("kv", w, b, k) for w in (1, 2) for b in range(BATCH) for k in range(NK)]
        qjobs = [("q", m, ch, 0) for m in range(2) for ch in range(NCH)]
        cjobs = [("count", b, m, 0) for b in range(BATCH) for m in range(2)]
        xjobs = [("x", b, m, s) for b in range(BATCH) for m in range(2) for s in range(3)]
        jobs = kjobs + qjobs + cjobs + xjobs
        done, spiked, x3_ones = c.sem("sp_done"), c.sem("sp_spiked"), c.sem("sp_ones")
        with nc.Block() as block:
            @block.tensor
            def _(pe):
                for n, (kind, a, b, k) in enumerate(jobs):
                    if n >= 8:
                        pe.wait_ge(spiked, n - 7)
                    bank = c.bank[n % 8]
                    if kind == "kv":
                        k0, kn = KT[k]
                        ps = bank[0:kn, 0:D]
                        for o in range(2):
                            ins = pe.matmul(ps, c.xT[0:DH + o, o, b * T + k0:b * T + k0 + kn], wT[0:DH + o, a, o, :],
                                            start=(o == 0), stop=(o == 1))
                    elif kind == "q":
                        ps = bank[0:DH, 0:CW]
                        for o in range(2):
                            ins = pe.matmul(ps, wT[0:DH + o, 0, o, a * DH:(a + 1) * DH],
                                            c.xT[0:DH + o, o, b * CW:(b + 1) * CW], start=(o == 0), stop=(o == 1))
                    elif kind == "count":
                        if n == len(kjobs) + len(qjobs):
                            pe.wait_ge(spiked, n)
                        for j, (k0, kn) in enumerate(KT):
                            ins = pe.matmul(bank[0:DH, 0:DH], ks[0:kn, a, j, b * DH:(b + 1) * DH],
                                            vs[0:kn, a, j, b * DH:(b + 1) * DH], start=(j == 0), stop=(j == NK - 1))
                    else:
                        if n == len(jobs) - len(xjobs):
                            pe.wait_ge(spiked, n)
                        at = a * T + k * S3
                        ins = pe.matmul(bank[0:DH, 0:S3], kv[:, a, b, :], qs[:, b, at:at + S3], start=True, stop=True)
                    ins.then_inc(done, 1)

            @block.gpsimd
            def _(pool):
                pool.memset(x3[DH:DH + 1, :, :], 1.0).then_inc(x3_ones, 1)

            @block.vector
            def _(dve):
                for n, (kind, a, b, k) in enumerate(jobs):
                    dve.wait_ge(done, n + 1)
                    bank = c.bank[n % 8]
                    if kind == "kv":
                        kn = KT[k][1]
                        ins = dve.tensor_scalar((ks, vs)[a - 1][0:kn, b, k, :], bank[0:kn, 0:D], 2.0, None, ALU.is_ge)
                    elif kind == "q":
                        ins = dve.tensor_scalar(qs[:, a, b * CW:(b + 1) * CW], bank[0:DH, 0:CW], 2.0, None, ALU.is_ge)
                    elif kind == "count":
                        ins = dve.tensor_tensor(kv[:, a, b, :], bank[0:DH, 0:DH], c.const("kv", DH), ALU.mult)
                    else:
                        at = a * T + k * S3
                        ins = dve.tensor_scalar(x3[0:DH, b, at:at + S3], bank[0:DH, 0:S3], HD ** -0.125, 1.0,
                                                ALU.mult, ALU.is_ge)
                    ins.then_inc(spiked, 1)
        to_tokens(c, "sp_out", [], lambda i: [(x3[0:DH + o, o, :], wT[0:DH + o, 3, o, :]) for o in range(2)],
                  None, into=c.hN, spike=2.0)


WIDTHS = (D, D // 2, D // 3)


def small_proj(c, g, ctx, aT):
    nc = c.nc
    w = c.sb(ctx, "proj_w", [DH + 1, 2, 2, D])
    w_in, own_s = c.sem("proj_in"), c.sem("proj_own")
    with nc.Block() as block:
        @block.sync
        def _(sp):
            sp.dma_start(w[0:DH, 0, :, :], c.ins["L1_ffn_w_proj"].rearrange("(k p) n -> p k n", p=DH)
                         ).then_inc(w_in, 16)
            sp.dma_start(w[DH:DH + 1, 0, 1, :], c.ins["L1_ffn_b_proj"].rearrange("(a n) -> a n", a=1)
                         ).then_inc(w_in, 16)

        @block.vector
        def _(dve):
            own = Own(dve, own_s)
            dve.wait_ge(w_in, 32)
            for k in range(2):
                own.did(dve.tensor_scalar(w[0:DH + k, 1, k, :], w[0:DH + k, 0, k, :], g[0:DH + k, 0:1], None, ALU.mult))
            for i in (1, 2):
                n = WIDTHS[i]
                own.wait()
                for r0, r1, k in ((0, n, 0), (DH, DH + 1, 1)):
                    own.did(dve.scalar_tensor_tensor(w[r0:r1, 1, k, 0:n], w[r0:r1, 0, k, 0:n], g[r0:r1, i:i + 1],
                                                     w[r0:r1, 1, k, 0:n], ALU.mult, ALU.add))
            own.wait()
    half = NTILE // 2
    heads_out(c, "proj", aT, lambda i: w[:, i // half, :, :])


def last_mlps(c, g, x):
    i = c.ins
    w = dict(w1=i["L1_ffn_w_fc1"], b1=i["L1_ffn_b_fc1"], w2=i["L1_ffn_w_fc2"], b2=i["L1_ffn_b_fc2"])
    terms = [ALL_TERMS, first_terms(WIDTHS[1]), first_terms(WIDTHS[2])]
    variants = [dict(w, terms=terms[0], n=D, gain=None, chunks=range(NCH // 2))]
    for k in range(3):
        variants.append(dict(w, terms=terms[k], n=WIDTHS[k], gain=lambda t, k=k: g[0:TT, k:k + 1],
                             chunks=range(NCH // 2, NCH)))
    mlps(c, "last", x, variants, ACT.Gelu)


def write_out(c, out):
    nc = c.nc
    summed, stored = c.sem("out_summed"), c.stored
    with nc.Block() as block:
        @block.vector
        def _(dve):
            for k in range(3):
                s = slice(6 * k, 6 * k + 6)
                dve.tensor_tensor(c.hN[0:TT, s, :], c.hN[0:TT, s, :], c.xN[0:TT, s, :], ALU.add).then_inc(summed, 1)

        @block.sync
        def _(sp):
            view = out.rearrange("b t d -> (b t) d").rearrange("(i p) d -> p i d", p=TT)
            for k in range(3):
                s = slice(6 * k, 6 * k + 6)
                sp.wait_ge(summed, k + 1)
                sp.dma_start(view[:, s, :], c.hN[0:TT, s, :]).then_inc(stored, 16)
            sp.wait_ge(stored, 48)


def last_ffn(c, ctx):
    nc = c.nc
    g = c.sb(ctx, "gumbel", [128, 3])
    g_in = c.sem("gumbel_in")
    with nc.Block() as block:
        @block.sync
        def _(sp):
            sp.dma_start(g[:, :], c.ins["L1_ffn_gumbel_weights"].rearrange("(a n) -> a n", a=1).broadcast_to((128, 3))
                         ).then_inc(g_in, 16)
            sp.wait_ge(g_in, 16)
    norm(c, "n1", True, "ln", ["L1_ffn_n1l_g", "L1_ffn_n1s_g"], ["L1_ffn_n1l_b", "L1_ffn_n1s_b"])
    attention_layer(c, "att1", c.ins["L1_ffn_w_qkv"], None, lambda ctx, aT: small_proj(c, g, ctx, aT))
    x = Split(c, ctx, "last")
    norm(c, "n2", False, "ln", ["L1_ffn_n2l_g", "L1_ffn_n2s_g"], ["L1_ffn_n2l_b", "L1_ffn_n2s_b"], split=x)
    last_mlps(c, g, x)


def tower(nc, ins, out):
    with ExitStack() as ctx:
        c = Core(nc, ins)
        load_shared(c, ctx)
        tok_features(c)
        layer_buffers(c, ctx)
        norm(c, "mixn", True, "rms", ["L0_attn_norm1_w"])
        mixer(c)
        c.layer_end()
        with ExitStack() as inner:
            x = Split(c, inner, "ff0")
            norm(c, "ff0n", False, "rms", ["L0_attn_norm2_w"], split=x)
            ff0(c, x)
        norm(c, "att0n", True, "ln", ["L0_ffn_ln1_g"], ["L0_ffn_ln1_b"], residual=True)
        attention_layer(c, "att0", ins["L0_ffn_in_proj_w"], ins["L0_ffn_in_proj_b"],
                        lambda ctx, aT: out_proj0(c, ctx, aT))
        c.layer_end()
        with ExitStack() as inner:
            x = Split(c, inner, "moe")
            norm(c, "moen", False, "ln", ["L0_ffn_ln2_g"], ["L0_ffn_ln2_b"], split=x)
            moe(c, x)
        c.layer_end()
        norm(c, "spn", True, None, None, residual=True)
        spiking(c)
        c.layer_end()
        last_ffn(c, ctx)
        write_out(c, out)


_INS = ['x', 'cls_tok', 'L0_tok_freq_bands', 'L0_tok_W', 'L0_attn_norm1_w', 'L0_attn_w_in', 'L0_attn_conv_w',
        'L0_attn_w_bc', 'L0_attn_D_skip', 'L0_attn_w_out', 'L0_attn_norm2_w', 'L0_attn_ff_w1', 'L0_attn_ff_b1',
        'L0_attn_ff_w2', 'L0_attn_ff_b2', 'L0_ffn_ln1_g', 'L0_ffn_ln1_b', 'L0_ffn_in_proj_w', 'L0_ffn_in_proj_b',
        'L0_ffn_out_proj_w', 'L0_ffn_out_proj_b', 'L0_ffn_ln2_g', 'L0_ffn_ln2_b', 'L0_ffn_router_w',
        'L0_ffn_router_b', 'L0_ffn_w1', 'L0_ffn_b1', 'L0_ffn_w2', 'L0_ffn_b2', 'L1_attn_W', 'L1_attn_b',
        'L1_attn_bn_gamma', 'L1_attn_bn_beta', 'L1_attn_bn_mean', 'L1_attn_bn_var', 'L1_ffn_gumbel_weights',
        'L1_ffn_n1l_g', 'L1_ffn_n1l_b', 'L1_ffn_n1s_g', 'L1_ffn_n1s_b', 'L1_ffn_w_qkv', 'L1_ffn_w_proj',
        'L1_ffn_b_proj', 'L1_ffn_n2l_g', 'L1_ffn_n2l_b', 'L1_ffn_n2s_g', 'L1_ffn_n2s_b', 'L1_ffn_w_fc1',
        'L1_ffn_b_fc1', 'L1_ffn_w_fc2', 'L1_ffn_b_fc2']


def kernel(**inputs):
    import numpy as _np
    import concourse.bacc as _bacc
    from concourse import mybir as _mybir
    from concourse.bass_utils import run_bass_kernel_spmd as _run

    nc = _bacc.Bacc("TRN2", target_bir_lowering=False, num_devices=1)
    arrays, ins = {}, {}
    for name in _INS + ["consts"]:
        a = CONSTANTS if name == "consts" else _np.ascontiguousarray(inputs[name])
        arrays[f"in_{name}_dram"] = a
        ins[name] = nc.dram_tensor(f"in_{name}_dram", a.shape, _mybir.dt.from_np(a.dtype), kind="ExternalInput").ap()
    out = nc.dram_tensor("out_0_dram", (BATCH, T, D), F32, kind="ExternalOutput").ap()
    tower(nc, ins, out)
    r = _run(nc, [arrays], core_ids=[0])
    return r.results[0]["out_0_dram"]
```
